# Optimizing a Trainium2 kernel written in Bass

```python
import numpy as np
import jax
import jax.numpy as jnp

def _softmax(x, axis=-1):
    return jax.nn.softmax(x, axis=axis)

def _gelu(x):
    return jax.nn.gelu(x, approximate=True)

def _silu(x):
    return jax.nn.silu(x)

def _sigmoid(x):
    return jax.nn.sigmoid(x)

def _layernorm(x, axis=-1, eps=1e-05):
    m = jnp.mean(x, axis=axis, keepdims=True)
    v = jnp.var(x, axis=axis, keepdims=True)
    return (x - m) / jnp.sqrt(v + eps)

def _scatter_add(tgt, idx, src, axis=0):
    return tgt.at[idx].add(src)

def _segment_sum(src, seg, n):
    return jax.ops.segment_sum(src, seg, n)
kernel_name = 'mk_adj_resnorm_d4_adj_r2_b4c71a'

def setup_inputs(seed: int=0):
    np.random.seed(seed)
    _w = jnp.asarray

    def _rec_inputs():
        import jax
        import jax.numpy as jnp
        _gk = jax.random.key(seed)
        x = -0.0002928 + 1 * jax.random.normal(jax.random.fold_in(_gk, 1), (4096, 256), jnp.float32)
        _a = jax.random.bernoulli(jax.random.fold_in(_gk, 2), 0.000488281, (4096, 4096))
        _a = jnp.logical_or(_a, jnp.swapaxes(_a, -1, -2))
        _a = jnp.logical_or(_a, jnp.eye(4096, dtype=bool))
        adj = _a.astype(jnp.int32)
        return (x, adj)
    x, adj = _rec_inputs()

    def _L0_gnn_setup():
        import jax, jax.numpy as jnp
        import numpy as np
        N, D_IN, D_OUT = (4096, 256, 256)
        key = jax.random.key(seed)
        ks = jax.random.split(key, 8)
        scale_in = 1.0 / np.sqrt(D_IN)
        scale_cat = 1.0 / np.sqrt(2 * D_OUT)
        return {'x': jax.random.normal(ks[0], (N, D_IN), dtype=jnp.float32), 'adj': jax.random.randint(ks[1], (N, N), 0, 2, dtype=jnp.int32), 'W_self': jax.random.uniform(ks[2], (D_IN, D_OUT), jnp.float32, -scale_in, scale_in), 'b_self': jax.random.uniform(ks[3], (D_OUT,), jnp.float32, -scale_in, scale_in), 'W_nb': jax.random.uniform(ks[4], (D_IN, D_OUT), jnp.float32, -scale_in, scale_in), 'b_nb': jax.random.uniform(ks[5], (D_OUT,), jnp.float32, -scale_in, scale_in), 'W_comb': jax.random.uniform(ks[6], (2 * D_OUT, D_OUT), jnp.float32, -scale_cat, scale_cat), 'b_comb': jax.random.uniform(ks[7], (D_OUT,), jnp.float32, -scale_cat, scale_cat)}
    _L0_gnn_all = _L0_gnn_setup()
    _L0_gnn_in = {k: v for k, v in _L0_gnn_all.items() if k in ('W_self', 'b_self', 'W_nb', 'b_nb', 'W_comb', 'b_comb')}
    del _L0_gnn_all

    def _L1_gnn_setup():
        import jax, jax.numpy as jnp
        import numpy as np
        N = 2048
        IN_FEAT = 256
        EMBED = 256
        HEADS = 8
        HEAD_DIM = EMBED // HEADS
        SCALING = HEAD_DIM ** (-0.5)
        key = jax.random.key(seed)
        ks = jax.random.split(key, 7)
        x = jax.random.normal(ks[0], (N, IN_FEAT), dtype=jnp.float32)
        adj = jax.random.randint(ks[1], (N, N), 0, 2, dtype=jnp.int32)
        s = 0.04
        WQ = jax.random.normal(ks[2], (EMBED, IN_FEAT), dtype=jnp.float32) * s
        WK = jax.random.normal(ks[3], (EMBED, IN_FEAT), dtype=jnp.float32) * s
        WV = jax.random.normal(ks[4], (EMBED, IN_FEAT), dtype=jnp.float32) * s
        we = jax.random.normal(ks[5], (1, HEAD_DIM), dtype=jnp.float32) * 0.1
        be = jnp.zeros((1,), dtype=jnp.float32)
        return {'x': x, 'adj': adj, 'WQ': WQ, 'WK': WK, 'WV': WV, 'we': we, 'be': be}
    _L1_gnn_all = _L1_gnn_setup()
    _L1_gnn_in = {k: v for k, v in _L1_gnn_all.items() if k in ('WQ', 'WK', 'WV', 'we', 'be')}
    del _L1_gnn_all

    def _L2_gnn_setup():
        import jax, jax.numpy as jnp
        import numpy as np
        N = 4096
        D = 256
        key = jax.random.key(seed)
        ks = jax.random.split(key, 7)
        X = jax.random.normal(ks[0], (N, D), dtype=jnp.float32)
        adj = jax.random.randint(ks[1], (N, N), 0, 2, dtype=jnp.int32)
        adj = adj.at[jnp.arange(N), jnp.arange(N)].set(1)
        s = 1.0 / np.sqrt(D)
        Wq = jax.random.normal(ks[2], (D, D), dtype=jnp.float32) * s
        Wk = jax.random.normal(ks[3], (D, D), dtype=jnp.float32) * s
        Wv = jax.random.normal(ks[4], (D, D), dtype=jnp.float32) * s
        Wo = jax.random.normal(ks[5], (D, D), dtype=jnp.float32) * s
        bo = jnp.zeros((D,), dtype=jnp.float32)
        return {'X': X, 'adj': adj, 'Wq': Wq, 'Wk': Wk, 'Wv': Wv, 'Wo': Wo, 'bo': bo}
    _L2_gnn_all = _L2_gnn_setup()
    _L2_gnn_in = {k: v for k, v in _L2_gnn_all.items() if k in ('Wq', 'Wk', 'Wv', 'Wo', 'bo')}
    del _L2_gnn_all

    def _L3_gnn_setup():
        import jax, jax.numpy as jnp
        import numpy as np
        N = 4096
        D_IN = 256
        D_OUT = 256
        key = jax.random.key(seed)
        k1, k2, k3, k4 = jax.random.split(key, 4)
        node_feats = jax.random.normal(k1, (N, D_IN), dtype=jnp.float32)
        adj_matrix = jax.random.randint(k2, (N, N), 0, 2, dtype=jnp.int32)
        w_self = jax.random.normal(k3, (D_OUT, D_IN), dtype=jnp.float32) * D_IN ** (-0.5)
        w_neigh = jax.random.normal(k4, (D_OUT, D_IN), dtype=jnp.float32) * D_IN ** (-0.5)
        return {'node_feats': node_feats, 'adj_matrix': adj_matrix, 'w_self': w_self, 'w_neigh': w_neigh}
    _L3_gnn_all = _L3_gnn_setup()
    _L3_gnn_in = {k: v for k, v in _L3_gnn_all.items() if k in ('w_self', 'w_neigh')}
    del _L3_gnn_all
    return {'x': x, 'adj': adj, 'L0_gnn_W_self': _L0_gnn_in['W_self'], 'L0_gnn_b_self': _L0_gnn_in['b_self'], 'L0_gnn_W_nb': _L0_gnn_in['W_nb'], 'L0_gnn_b_nb': _L0_gnn_in['b_nb'], 'L0_gnn_W_comb': _L0_gnn_in['W_comb'], 'L0_gnn_b_comb': _L0_gnn_in['b_comb'], 'L1_gnn_WQ': _L1_gnn_in['WQ'], 'L1_gnn_WK': _L1_gnn_in['WK'], 'L1_gnn_WV': _L1_gnn_in['WV'], 'L1_gnn_we': _L1_gnn_in['we'], 'L1_gnn_be': _L1_gnn_in['be'], 'L2_gnn_Wq': _L2_gnn_in['Wq'], 'L2_gnn_Wk': _L2_gnn_in['Wk'], 'L2_gnn_Wv': _L2_gnn_in['Wv'], 'L2_gnn_Wo': _L2_gnn_in['Wo'], 'L2_gnn_bo': _L2_gnn_in['bo'], 'L3_gnn_w_self': _L3_gnn_in['w_self'], 'L3_gnn_w_neigh': _L3_gnn_in['w_neigh']}

def reference(x, adj, L0_gnn_W_self, L0_gnn_b_self, L0_gnn_W_nb, L0_gnn_b_nb, L0_gnn_W_comb, L0_gnn_b_comb, L1_gnn_WQ, L1_gnn_WK, L1_gnn_WV, L1_gnn_we, L1_gnn_be, L2_gnn_Wq, L2_gnn_Wk, L2_gnn_Wv, L2_gnn_Wo, L2_gnn_bo, L3_gnn_w_self, L3_gnn_w_neigh):
    import jax
    import jax.numpy as jnp

    def _L0_gnn_ref(x, adj, W_self, b_self, W_nb, b_nb, W_comb, b_comb):
        import jax, jax.numpy as jnp
        import numpy as np
        N, D_IN, D_OUT = (4096, 256, 256)
        mask = (adj > 0).astype(x.dtype)
        deg = jnp.sum(mask, axis=1, keepdims=True)
        agg = mask @ x / jnp.maximum(deg, 1.0)
        self_f = x @ W_self + b_self
        nb_f = agg @ W_nb + b_nb
        combined = jnp.concatenate([self_f, nb_f], axis=-1)
        out = combined @ W_comb + b_comb
        return jax.nn.relu(out)

    def _L1_gnn_ref(x, adj, WQ, WK, WV, we, be):
        import jax, jax.numpy as jnp
        import numpy as np
        N = 2048
        IN_FEAT = 256
        EMBED = 256
        HEADS = 8
        HEAD_DIM = EMBED // HEADS
        SCALING = HEAD_DIM ** (-0.5)
        n = x.shape[0]
        Q = (x @ WQ.T).reshape(n, HEADS, HEAD_DIM).transpose(1, 0, 2)
        K = (x @ WK.T).reshape(n, HEADS, HEAD_DIM).transpose(1, 0, 2)
        V = (x @ WV.T).reshape(n, HEADS, HEAD_DIM).transpose(1, 0, 2)
        energy = Q @ we.T + be
        attn = jnp.einsum('hqd,hkd->hqk', Q, K) * SCALING + energy
        attn = attn + jnp.where(adj > 0, 0.0, -jnp.inf)
        attn = jax.nn.softmax(attn, axis=-1)
        hard = (attn == jnp.max(attn, axis=-1, keepdims=True)).astype(jnp.float32) / HEADS
        out = jnp.einsum('hqk,hkd->hqd', hard, V)
        return out.transpose(1, 0, 2).reshape(n, EMBED)

    def _L2_gnn_ref(X, adj, Wq, Wk, Wv, Wo, bo):
        import jax, jax.numpy as jnp
        import numpy as np
        N = 4096
        D = 256
        Q = X @ Wq.T
        K = X @ Wk.T
        V = X @ Wv.T
        scale = 1.0 / jnp.sqrt(jnp.asarray(D, X.dtype))
        scores = jnp.einsum('nd,md->nm', Q, K) * scale
        scores = jnp.where(adj == 0, -jnp.inf, scores)
        attn = jax.nn.softmax(scores, axis=-1)
        out = attn @ V
        out = out @ Wo.T + bo
        return out

    def _L3_gnn_ref(node_feats, adj_matrix, w_self, w_neigh):
        import jax, jax.numpy as jnp
        import numpy as np
        N = 4096
        D_IN = 256
        D_OUT = 256
        adj_f = adj_matrix.astype(node_feats.dtype)
        s = adj_f @ node_feats[:, 0]
        has_neigh = jnp.sum(adj_matrix, axis=1) > 0
        s = jnp.where(has_neigh, s, jnp.zeros_like(s))
        neigh_term = s[:, None] * jnp.sum(w_neigh, axis=1)[None, :]
        return jax.nn.relu(node_feats @ w_self.T + neigh_term)
    x = _layernorm(x + _L0_gnn_ref(x, adj, L0_gnn_W_self, L0_gnn_b_self, L0_gnn_W_nb, L0_gnn_b_nb, L0_gnn_W_comb, L0_gnn_b_comb), axis=-1)
    x = _layernorm(x + _L1_gnn_ref(x, adj, L1_gnn_WQ, L1_gnn_WK, L1_gnn_WV, L1_gnn_we, L1_gnn_be), axis=-1)
    x = _layernorm(x + _L2_gnn_ref(x, adj, L2_gnn_Wq, L2_gnn_Wk, L2_gnn_Wv, L2_gnn_Wo, L2_gnn_bo), axis=-1)
    x = _layernorm(x + _L3_gnn_ref(x, adj, L3_gnn_w_self, L3_gnn_w_neigh), axis=-1)
    return x

_drawn_inputs = setup_inputs


def setup_inputs(seed=0):
    import zlib

    import numpy as np

    out = dict(_drawn_inputs(seed))
    spreads = {'L2_gnn_bo': (0.0, 0.1)}
    factors = {'L0_gnn_b_self': 3.144}
    for name, (base, spread) in spreads.items():
        noise = np.random.default_rng([zlib.crc32(name.encode()), seed]).standard_normal(out[name].shape)
        drawn = base * np.exp(spread * noise) if base else spread * noise
        out[name] = jnp.asarray(drawn.astype(out[name].dtype))
    for name, factor in factors.items():
        out[name] = (out[name] * factor).astype(out[name].dtype)
    return out
```

```python
from contextlib import ExitStack

import concourse.bass as bass
from concourse import mybir
from concourse.alu_op_type import AluOpType as ALU

F32 = mybir.dt.float32
I32 = mybir.dt.int32
BF16 = mybir.dt.bfloat16
FP8 = mybir.dt.float8e4
U8 = mybir.dt.uint8
ACT = mybir.ActivationFunctionType
AX = mybir.AxisListType

P = 128
N = 4096
D = 256
T = N // P
KD = D // P
H = 8
HD = D // H
EPS = 1e-5
SCALE1 = float(HD) ** -0.5
SCALE2 = 1.0 / 16.0
MASKED = -1.0e30

ONE8 = 56.0
WORD = 16
WPC = P // WORD
WORDS = N // WORD
SLOTS = 16
TAB = 40
XP = 3 * D + 2
XM, XL = D + 2, 2 * D + 2

CAPS = [16] + [9] * 2 + [8] * 2 + [7] * 4 + [6] * 4 + [5] * 6 + [4] * 8 + [3] * 5
KV_SLOTS = 9

C_IDENT, C_UPPER, C_PACK, C_GROUP = 0, P, 2 * P, 2 * P + WPC
C_CLASS = C_GROUP + WORDS
C_LIMIT, C_BIT = C_CLASS + SLOTS, C_CLASS + 2 * SLOTS
C_F32 = C_BIT + WORD
C_POW, C_OWN = 0, WORD
C_I32 = WORD + T

STEPS_A = 26


class Steps:

    def __init__(self, eng, sem, done, paced):
        self.eng, self.sem, self.done, self.paced, self.count = eng, sem, done, paced, 0

    def __call__(self, ins):
        ins.then_inc(self.sem, 1)
        self.count += 1
        return ins

    def wait(self, alone=False):
        self.eng.wait_ge(self.sem, self.done + self.count)
        if alone:
            self.eng.sem_inc(self.paced, 1)


def build_program(nc, dram, out):
    with ExitStack() as ctx:
        def sb(name, shape, dt):
            return ctx.enter_context(nc.sbuf_tensor("s_" + name, shape, dt))

        def sem(name):
            return ctx.enter_context(nc.semaphore(name))

        r1 = nc.dram_tensor("row1", [N, 2 * D], F32, kind="Internal").ap()
        kv1 = nc.dram_tensor("kv1", [N, 2 * D], F32, kind="Internal").ap()
        r2 = nc.dram_tensor("row2", [N, 2 * D], F32, kind="Internal").ap()
        kv2 = nc.dram_tensor("kv2", [N, 2 * D], F32, kind="Internal").ap()
        yst = nc.dram_tensor("yst", [N, D + 2], F32, kind="Internal").ap()
        table = nc.dram_tensor("table", [N, TAB], I32, kind="Internal").ap()

        adj8 = sb("adj8", [P, T, T, P], FP8)
        adjbytes = adj8[:, :, :, :].rearrange("p t c i -> p t (c i)").bitcast(U8)
        KEPT = T - 4
        stage = [adj8[:, KEPT + 2 * u:KEPT + 2 * u + 2, :, :].rearrange("p t c i -> p (t c i)").bitcast(BF16)
                 .rearrange("p (c i) -> p c i", i=P) for u in range(2)]
        cf = sb("cf", [P, C_F32], F32)
        ci = sb("ci", [P, C_I32], I32)
        packb = sb("packb", [P, WPC], BF16)
        listf = sb("listf", [P, T, SLOTS], F32)
        degree = sb("degree", [P, T], F32)
        stat = sb("stat", [P, 48], F32)
        REGION = 63616
        region = sb("region", [P, REGION // 4], F32)

        def carve(at, n):
            assert (at + n) <= REGION // 4, (at, n)
            return region[:, at:at + n]

        ident = cf[:, C_IDENT:C_IDENT + P]
        ps = ctx.enter_context(nc.psum_tensor("ps", [P, 8, 512], F32))

        xp = carve(0, T * XP // 2).bitcast(BF16).rearrange("p (c n) -> p c n", n=XP)
        a0 = T * XP // 2
        gword = carve(a0, WORDS // 2).bitcast(BF16)
        a0 += WORDS // 2
        work_at = a0
        xs = [carve(work_at + u * 1024, 1024) for u in range(2)]
        xr = carve(work_at + 2048, 1024)
        xt = [carve(work_at + u * 256, 256) for u in range(2)]
        aggs = carve(work_at + 512, 256)
        axT = carve(work_at + 768, 512)
        x1T = carve(work_at + 1280, 256)
        row1 = carve(work_at + 1536, 512)
        kvr1 = carve(work_at + 2048, 512)
        key = [carve(work_at + 2560 + 256 * k, 256) for k in range(2)]
        REG_A = work_at + 3072
        assert REG_A <= REGION // 4

        weights = sb("weights", [P, 3 * KD * D], F32)
        wqkv = weights[:, :].rearrange("p (k n) -> p k n", k=KD)
        comb = sb("comb", [P, 2 * KD * D], F32)
        wnc = comb[:, 0:KD * D].rearrange("p (k n) -> p k n", k=KD)
        wsc = comb[:, KD * D:].rearrange("p (k n) -> p k n", k=KD)
        biasb = sb("biasb", [P, D], F32)
        raw = carve(T * XP // 2 - 2048 - 260, 2048)
        wsT = raw[:, 0:512].rearrange("p (k n) -> p k n", k=KD)
        wnT = raw[:, 512:1024].rearrange("p (k n) -> p k n", k=KD)
        wc = raw[:, 1024:2048].rearrange("p (k n) -> p k n", k=2 * KD)
        RAW_FREE_CHUNKS = (T * XP // 2 - 2048 - 260) // (4 * XP // 2)
        bcol = sb("bcol", [P, 2 * KD], F32)
        web = sb("web", [P, D], F32)
        beb = sb("beb", [P, 1], F32)

        BANK_A = [ps[:, 0, :], ps[:, 1, :]]
        BANK_W, BANK_T, BANK_X, BANK_O = ps[:, 2, :], ps[:, 3, :], ps[:, 4, :], ps[:, 5, :]
        BANK_K, BANK_QV = ps[:, 6, :], ps[:, 7, :]

        s = {n: sem(n) for n in (
            "const_in", "raw_in", "w1_in", "comb_ready", "comb_done", "xs_in0", "xs_in1", "x_high", "x_mid", "x_r1", "x_r2",
            "xp_ready", "pack_ready", "adj_in0", "adj_in1", "agg_done", "rdeg_ready", "aggs_ready",
            "ax_turned", "axT_ready", "o_done", "x1_ready", "x1_turned", "x1T_ready", "qkv_done",
            "qv_ready", "k_ready", "words_taken", "var_ready", "rstd_ready", "xt_in0", "xt_in1", "row1_out", "kv1_out",
            "dve_step", "bias_in", "kept")}
        paced, tail_in = sem("paced"), sem("tail_in")
        adj_in = [s["adj_in0"], s["adj_in1"]]
        xs_in = [s["xs_in0"], s["xs_in1"]]
        xt_in = [s["xt_in0"], s["xt_in1"]]
        XC = 4

        RDEG, BN, MV, RSTD, NEWT, DEG = (stat[:, 0:1], stat[:, 2:8], stat[:, 8:10], stat[:, 10:11], stat[:, 11:12], stat[:, 12:13])
        k16 = stat[:, 16:32]
        n16 = stat[:, 32:48]
        smalli = sb("smalli", [P, 2 * SLOTS], I32)
        kint, kgrp = smalli[:, 0:SLOTS], smalli[:, SLOTS:]
        kgrpf = sb("kgrpf", [P, SLOTS], F32)

        def tiles_of_a(eng, body):
            body(0, 0, 0)
            with eng.Fori(0, T // 2 - 1) as i:
                body(i * 2 + 1, i, 1)
                body(i * 2 + 2, i + 1, 0)
            body(T - 1, T // 2 - 1, 1)

        def rows(ap, t):
            return ap[bass.ds(t * P, P), :]

        with nc.Block() as block:
            @block.gpsimd
            def _(pool):
                def load(t, q, u, kept=True):
                    if not (isinstance(t, int) and t < 2):
                        pool.wait_ge(s["agg_done"], t - 1)
                        if kept:
                            pool.wait_ge(s["kept"], t - 1)
                    src = dram["adj_tiles"][bass.ds(t, 1)].rearrange("a p n -> (a p) n")
                    pool.dma_start(stage[u].rearrange("p c i -> p (c i)"), src).then_inc(adj_in[u], 16)
                load(0, 0, 0)
                load(1, 0, 1)
                with pool.Fori(1, KEPT // 2 + 1) as i:
                    load(i * 2, i, 0)
                    load(i * 2 + 1, i, 1)
                load(T - 2, T // 2 - 1, 0, False)
                load(T - 1, T // 2 - 1, 1, False)
                for t in range(KEPT, T):
                    pool.wait_ge(s["agg_done"], T - 1 if t < KEPT + 2 else T)
                    pool.dma_start(adj8[:, t, :, :].rearrange("p c i -> p (c i)"), dram["adj_tiles"][t]).then_inc(tail_in, 16)

            @block.sync
            def _(sp):
                sp.dma_start(cf[:, :], dram["const_f32"]).then_inc(s["const_in"], 16)
                sp.dma_start(ci[:, :], dram["const_i32"]).then_inc(s["const_in"], 16)
                sp.dma_start(wsT, dram["w_selfT0"].rearrange("(k p) n -> p k n", p=P)).then_inc(s["raw_in"], 16)
                sp.dma_start(wnT, dram["w_nbT0"].rearrange("(k p) n -> p k n", p=P)).then_inc(s["raw_in"], 16)
                sp.dma_start(wc, dram["W_comb"].rearrange("(k p) n -> p k n", p=P)).then_inc(s["raw_in"], 16)
                sp.dma_start(bcol[:, 0:KD], dram["b_self"]).then_inc(s["raw_in"], 16)
                sp.dma_start(bcol[:, KD:], dram["b_nb"]).then_inc(s["raw_in"], 16)
                for n in range(T // XC):
                    if n >= 2:
                        sp.wait_ge(s["x_r1"], n - 1)
                    src = dram["x"][n * XC * P:(n + 1) * XC * P, :].rearrange("(c p) d -> p c d", p=P)
                    sp.dma_start(xs[n % 2].rearrange("p (c d) -> p c d", d=D), src).then_inc(xs_in[n % 2], 16)
                    if n == 1:
                        sp.dma_start(biasb[:, :], dram["b_comb"].to_broadcast([P, D])).then_inc(s["bias_in"], 16)
                        sp.dma_start(web[:, 0:HD], dram["we"].to_broadcast([P, HD])).then_inc(s["w1_in"], 16)
                        sp.dma_start(beb[:, :], dram["be"].to_broadcast([P, 1])).then_inc(s["w1_in"], 16)
                        for j, name in enumerate(("WK1T", "WQ1T", "WV1T")):
                            sp.dma_start(wqkv[:, :, j * D:(j + 1) * D],
                                         dram[name].rearrange("(k p) n -> p k n", p=P)).then_inc(s["w1_in"], 16)
                sp.wait_ge(s["xp_ready"], T // XC)

                def body(t, q, u):
                    if not (isinstance(t, int) and t == 0):
                        sp.wait_ge(s["x1_ready"], t)
                    sp.dma_start(xt[u], rows(dram["x"], t)).then_inc(xt_in[u], 16)
                    if not (isinstance(t, int) and t == 0):
                        store(t - 1)

                def store(t):
                    sp.wait_ge(s["qv_ready"], t + 1)
                    sp.wait_ge(s["x1_ready"], t + 1)
                    sp.dma_start(rows(r1, t), row1).then_inc(s["row1_out"], 16)
                    sp.wait_ge(s["k_ready"], t + 1)
                    sp.dma_start(rows(kv1, t), kvr1).then_inc(s["kv1_out"], 16)

                tiles_of_a(sp, body)
                store(T - 1)
                sp.wait_ge(s["row1_out"], 16 * T)
                sp.wait_ge(s["kv1_out"], 16 * T)

            @block.tensor
            def _(pe):
                pe.wait_ge(s["raw_in"], 80)
                pe.wait_ge(s["comb_ready"], 1)
                for half, (w, o) in enumerate(((wnT, 1), (wsT, 0))):
                    for k in range(KD):
                        for m in range(KD):
                            mm = pe.matmul(ps[:, half, k * D:(k + 1) * D], w[:, m, k * P:(k + 1) * P],
                                           wc[:, o * KD + m, :], start=(m == 0), stop=(m == KD - 1))
                mm.then_inc(s["comb_done"], 1)
                for m in range(2 * KD):
                    mm = pe.matmul(BANK_W[:, 0:D], xr[:, m * P:(m + 1) * P], wc[:, m, :],
                                   start=(m == 0), stop=(m == 2 * KD - 1))
                mm.then_inc(s["comb_done"], 1)
                pe.wait_ge(s["pack_ready"], 1)
                pe.wait_ge(s["comb_ready"], 4)

                def aggregate(t, q, u, tail):
                    at = {8: turn_ax, 14: layer0, 22: turn_x1, 28: project}
                    pe.wait_ge(adj_in[u], 16 * q + 16)
                    for c in range(T):
                        if isinstance(t, int) and t == 0 and c % XC == 0:
                            pe.wait_ge(s["xp_ready"], c // XC + 1)
                        if tail and c in at:
                            at[c](t - 1, q if u else q - 1, 1 - u)
                        mask = stage[u][:, c, :]
                        for m in range(3):
                            at_x, w = ((0, D + 1), (XM, D), (XL, D))[m]
                            pe.matmul(BANK_A[u][:, 0:w], mask, xp[:, c, at_x:at_x + w],
                                      start=(c == 0 and m == 0), stop=(c == T - 1 and m == 2))
                    if not (isinstance(t, int) and t == 0):
                        pe.wait_ge(s["words_taken"], t)
                    for c in range(T):
                        mask = stage[u][:, c, :]
                        mm = pe.matmul(BANK_W[:, c * WPC:(c + 1) * WPC], mask, packb[:, :], start=True, stop=True)
                    mm.then_inc(s["agg_done"], 1)

                def turn_ax(t, q, u):
                    pe.wait_ge(s["aggs_ready"], t + 1)
                    pe.wait_ge(xt_in[u], 16 * q + 16)
                    for k in range(KD):
                        pe.transpose(BANK_T[:, k * P:(k + 1) * P], aggs[:, k * P:(k + 1) * P], ident)
                    for k in range(KD):
                        mm = pe.transpose(BANK_T[:, (KD + k) * P:(KD + k + 1) * P], xt[u][:, k * P:(k + 1) * P], ident)
                    mm.then_inc(s["ax_turned"], 1)

                def layer0(t, q, u):
                    pe.wait_ge(s["axT_ready"], t + 1)
                    for k in range(2 * KD):
                        w = wnc[:, k, :] if k < KD else wsc[:, k - KD, :]
                        mm = pe.matmul(BANK_O[:, 0:D], axT[:, k * P:(k + 1) * P], w, start=(k == 0), stop=(k == 2 * KD - 1))
                    mm.then_inc(s["o_done"], 1)

                def turn_x1(t, q, u):
                    pe.wait_ge(s["x1_ready"], t + 1)
                    for k in range(KD):
                        mm = pe.transpose(BANK_X[:, k * P:(k + 1) * P], row1[:, k * P:(k + 1) * P], ident)
                    mm.then_inc(s["x1_turned"], 1)

                def project(t, q, u):
                    if isinstance(t, int) and t == 0:
                        pe.wait_ge(s["w1_in"], 80)
                    pe.wait_ge(s["x1T_ready"], t + 1)
                    if not (isinstance(t, int) and t == 0):
                        pe.wait_ge(s["k_ready"], t)
                        pe.wait_ge(s["qv_ready"], t)
                    for k in range(KD):
                        pe.matmul(BANK_K[:, 0:D], x1T[:, k * P:(k + 1) * P], wqkv[:, k, 0:D], start=(k == 0), stop=(k == KD - 1))
                    for k in range(KD):
                        mm = pe.matmul(BANK_QV, x1T[:, k * P:(k + 1) * P], wqkv[:, k, D:3 * D], start=(k == 0), stop=(k == KD - 1))
                    mm.then_inc(s["qkv_done"], 1)

                aggregate(0, 0, 0, False)
                with pe.Fori(0, T // 2 - 1) as i:
                    aggregate(i * 2 + 1, i, 1, True)
                    aggregate(i * 2 + 2, i + 1, 0, True)
                aggregate(T - 1, T // 2 - 1, 1, True)
                for step in (turn_ax, layer0, turn_x1, project):
                    step(T - 1, T // 2 - 1, 1)

            @block.scalar
            def _(act):
                act.wait_ge(s["comb_done"], 1)
                act.activation(comb[:, :], ps[:, 0:2, :].rearrange("p a n -> p (a n)"), ACT.Copy).then_inc(s["comb_ready"], 1)
                for n in range(T // XC):
                    if n == RAW_FREE_CHUNKS:
                        act.wait_ge(s["comb_done"], 2)
                    if n == 0:
                        act.wait_ge(s["comb_ready"], 3)
                    view = xp[:, n * XC:(n + 1) * XC, :]
                    act.wait_ge(xs_in[n % 2], 16 * (n // 2 + 1))
                    act.activation(view[:, :, 0:D], xs[n % 2].rearrange("p (c d) -> p c d", d=D), ACT.Copy).then_inc(s["x_high"], 1)
                    act.wait_ge(s["x_r1"], n + 1)
                    act.activation(view[:, :, XM:XM + D], xr.rearrange("p (c d) -> p c d", d=D), ACT.Copy).then_inc(s["x_mid"], 1)

                def keep(t, q, u):
                    act.wait_ge(adj_in[u], 16 * q + 16)
                    act.activation(adjbytes[:, bass.ds(t, 1), :].rearrange("p a n -> p (a n)"),
                                   stage[u].rearrange("p c i -> p (c i)"), ACT.Copy, scale=ONE8).then_inc(s["kept"], 1)

                def body(t, q, u):
                    first = isinstance(t, int) and t == 0
                    act.wait_ge(s["rdeg_ready"], t + 1)
                    act.activation(aggs, BANK_A[u][:, 0:D], ACT.Copy, scale=RDEG).then_inc(s["aggs_ready"], 1)
                    act.wait_ge(s["ax_turned"], t + 1)
                    act.activation(axT, BANK_T, ACT.Copy).then_inc(s["axT_ready"], 1)
                    act.wait_ge(s["var_ready"], t + 1)
                    act.activation(RSTD, RSTD, ACT.Sqrt).then_inc(s["rstd_ready"], 1)
                    act.wait_ge(s["x1_turned"], t + 1)
                    act.activation(x1T, BANK_X[:, 0:D], ACT.Copy).then_inc(s["x1T_ready"], 1)
                    act.wait_ge(s["qkv_done"], t + 1)
                    if not first:
                        act.wait_ge(s["row1_out"], 16 * t)
                        act.wait_ge(s["kv1_out"], 16 * t)
                    act.activation(row1[:, D:2 * D], BANK_QV[:, 0:D], ACT.Copy)
                    act.activation(kvr1[:, D:2 * D], BANK_QV[:, D:2 * D], ACT.Copy).then_inc(s["qv_ready"], 1)

                act.wait_ge(s["xp_ready"], T // XC)
                keep(0, 0, 0)
                keep(1, 0, 1)
                body(0, 0, 0)
                with act.Fori(0, KEPT // 2 - 1) as i:
                    keep(i * 2 + 2, i + 1, 0)
                    body(i * 2 + 1, i, 1)
                    keep(i * 2 + 3, i + 1, 1)
                    body(i * 2 + 2, i + 1, 0)
                with act.Fori(KEPT // 2 - 1, T // 2 - 1) as i:
                    body(i * 2 + 1, i, 1)
                    body(i * 2 + 2, i + 1, 0)
                body(T - 1, T // 2 - 1, 1)

            @block.vector
            def _(dve):
                st = Steps(dve, s["dve_step"], 0, paced)
                dve.wait_ge(s["const_in"], 32)
                st(dve.tensor_copy(packb[:, :], cf[:, C_PACK:C_PACK + WPC]))
                st(dve.tensor_copy(gword, cf[:, C_GROUP:C_GROUP + WORDS]))
                dve.wait_ge(s["raw_in"], 80)
                for m in range(2 * KD):
                    ins = dve.tensor_copy(xr[:, m * P:(m + 1) * P], bcol[:, m:m + 1].to_broadcast([P, P]))
                    st(ins)
                st.wait()
                dve.sem_inc(s["pack_ready"], 1)
                dve.sem_inc(s["comb_ready"], 1)
                dve.wait_ge(s["w1_in"], 80)
                for h in range(1, H):
                    st(dve.tensor_copy(web[:, h * HD:(h + 1) * HD], web[:, 0:HD]))
                dve.wait_ge(s["comb_done"], 2)
                dve.wait_ge(s["bias_in"], 16)
                st(dve.tensor_tensor(biasb[:, :], BANK_W[:, 0:D], biasb[:, :], ALU.add))
                st(dve.memset(xp[:, 0:RAW_FREE_CHUNKS * XC, D:D + 2], 1.0))
                st(dve.memset(xp[:, RAW_FREE_CHUNKS * XC:T, D:D + 2], 1.0))
                st.wait()
                dve.sem_inc(s["comb_ready"], 2)
                for n in range(T // XC):
                    view = xp[:, n * XC:(n + 1) * XC, :]
                    r = xr.rearrange("p (c d) -> p c d", d=D)
                    dve.wait_ge(s["x_high"], n + 1)
                    dve.tensor_tensor(r, xs[n % 2].rearrange("p (c d) -> p c d", d=D), view[:, :, 0:D], ALU.subtract).then_inc(s["x_r1"], 1)
                    dve.wait_ge(s["x_mid"], n + 1)
                    dve.tensor_tensor(view[:, :, XL:XL + D], r, view[:, :, XM:XM + D], ALU.subtract).then_inc(s["xp_ready"], 1)
                    dve.wait_ge(s["xp_ready"], n + 1)
                base = st.count

                def body(t, q, u):
                    first = isinstance(t, int) and t == 0
                    st = Steps(dve, s["dve_step"], base + t * STEPS_A, paced)
                    dve.wait_ge(s["agg_done"], t + 1)
                    st(dve.tensor_copy(DEG, BANK_A[u][:, D:D + 1]))
                    st.wait()
                    st(dve.tensor_copy(degree[:, bass.ds(t, 1)], DEG))
                    st(dve.tensor_scalar(RDEG, DEG, 1.0, None, ALU.max))
                    st.wait()
                    dve.reciprocal(RDEG, RDEG).then_inc(s["rdeg_ready"], 1)
                    st(dve.scalar_tensor_tensor(out=key[0], in0=BANK_W[:, 0:WORDS], scalar=0.0, in1=gword, op0=ALU.is_gt, op1=ALU.mult))
                    st.wait()
                    st(dve.tensor_tensor(key[0], BANK_W[:, 0:WORDS], key[0], ALU.add))
                    st.wait()
                    dve.sem_inc(s["words_taken"], 1)
                    top16(st, k16, key[0], key[1])
                    st(dve.tensor_copy(kint, k16))
                    st.wait()
                    st(dve.tensor_scalar(kgrp, kint, WORD, 4, ALU.logical_shift_right, ALU.logical_shift_left))
                    cand = key[0].bitcast(I32).rearrange("p (s b) -> p s b", b=WORD)
                    node = key[1].rearrange("p (s b) -> p s b", b=WORD)
                    st(dve.tensor_tensor(cand, kint.rearrange("p (s o) -> p s o", o=1).to_broadcast([P, SLOTS, WORD]),
                                         ci[:, C_POW:C_POW + WORD].rearrange("p (o b) -> p o b", o=1).to_broadcast([P, SLOTS, WORD]),
                                         ALU.bitwise_and))
                    st.wait()
                    st(dve.tensor_copy(kgrpf[:, :], kgrp))
                    st.wait()
                    st(dve.tensor_tensor(node, kgrpf[:, :].rearrange("p (s o) -> p s o", o=1).to_broadcast([P, SLOTS, WORD]),
                                         cf[:, C_BIT:C_BIT + WORD].rearrange("p (o b) -> p o b", o=1).to_broadcast([P, SLOTS, WORD]), ALU.add))
                    st.wait()
                    st(dve.scalar_tensor_tensor(out=key[1], in0=key[0].bitcast(I32), scalar=0.0, in1=key[1],
                                                op0=ALU.is_gt, op1=ALU.mult))
                    st.wait()
                    top16(st, n16, key[1], key[0])
                    st(dve.tensor_copy(listf[:, bass.ds(t, 1), :].rearrange("p a k -> p (a k)"), n16))
                    dve.wait_ge(s["o_done"], t + 1)
                    if not first:
                        dve.wait_ge(s["row1_out"], 16 * t)
                    y = row1[:, 0:D]
                    st(dve.tensor_tensor(y, BANK_O[:, 0:D], biasb[:, :], ALU.add))
                    st.wait()
                    dve.wait_ge(xt_in[u], 16 * q + 16)
                    st(dve.scalar_tensor_tensor(out=y, in0=y, scalar=0.0, in1=xt[u], op0=ALU.max, op1=ALU.add))
                    st.wait()
                    layernorm(st, y, s["var_ready"], s["rstd_ready"], t)
                    dve.tensor_scalar(y, y, MV[:, 0:1], RSTD, ALU.subtract, ALU.mult).then_inc(s["x1_ready"], 1)
                    dve.wait_ge(s["qkv_done"], t + 1)
                    if not first:
                        dve.wait_ge(s["kv1_out"], 16 * t)
                    dve.scalar_tensor_tensor(out=kvr1[:, 0:D], in0=BANK_K[:, 0:D], scalar=SCALE1, in1=web[:, :],
                                             op0=ALU.mult, op1=ALU.add).then_inc(s["k_ready"], 1)
                    assert st.count == STEPS_A, st.count

                def top16(st, out16, values, spare):
                    st.wait(alone=True)
                    st(dve.max(out16[:, 0:8], values))
                    st.wait(alone=True)
                    st(dve.match_replace(spare, out16[:, 0:8], values, 0.0))
                    st.wait(alone=True)
                    st(dve.max(out16[:, 8:16], spare))
                    st.wait()

                def layernorm(st, y, var_ready, rstd_ready, t):
                    st(dve.bn_stats(BN, y))
                    st.wait(alone=True)
                    st(dve.bn_aggr(MV, BN))
                    st.wait()
                    st(dve.tensor_scalar(NEWT, MV[:, 1:2], EPS, None, ALU.add))
                    st.wait()
                    dve.reciprocal(RSTD, NEWT).then_inc(var_ready, 1)
                    dve.wait_ge(rstd_ready, t + 1)
                    st(dve.tensor_scalar(NEWT, NEWT, RSTD, RSTD, ALU.mult, ALU.mult))
                    st.wait()
                    st(dve.tensor_scalar(NEWT, NEWT, -0.5, 1.5, ALU.mult, ALU.add))
                    st.wait()
                    st(dve.tensor_tensor(RSTD, RSTD, NEWT, ALU.mult))
                    st.wait()

                tiles_of_a(dve, body)


        tabw = carve(14400, (T + 1) * TAB).bitcast(I32).rearrange("p (t n) -> p t n", n=TAB)
        cls = carve(0, 256).bitcast(BF16)
        cls3 = cls.rearrange("p (c t) -> p c t", t=T)
        upperb = carve(256, P // 2).bitcast(BF16)
        onesb = carve(320, P // 2).bitcast(BF16)
        tot, incl, posw, zero = (carve(512 * k + 512, 512) for k in range(4))
        lst = listf[:, :, :].rearrange("p t k -> p (t k)")
        over = carve(2560, SLOTS + 1)
        mid = carve(2600, T * SLOTS)
        rank = sb("rank", [P, T], I32)
        flag = sb("flag", [P, 1], I32)
        s_cls, s_rank, s_rstep = sem("classes_ready"), sem("ranks_counted"), sem("rank_step")

        with nc.Block() as block:
            @block.vector
            def _(dve):
                st = Steps(dve, s_rstep, 0, paced)
                st(dve.tensor_tensor(cls3, degree[:, :].rearrange("p (o t) -> p o t", o=1).to_broadcast([P, SLOTS, T]),
                                     cf[:, C_CLASS:C_CLASS + SLOTS].rearrange("p (c o) -> p c o", o=1).to_broadcast([P, SLOTS, T]),
                                     ALU.is_equal))
                st(dve.tensor_copy(upperb, cf[:, C_UPPER:C_UPPER + P]))
                st(dve.memset(onesb, 1.0))
                st.wait()
                dve.sem_inc(s_cls, 1)
                st(dve.memset(zero, 0.0))
                st(dve.memset(tabw.rearrange("p t n -> p (t n)"), 0))
                st(dve.tensor_scalar(mid, lst, 0.0, 2.0 ** 20, ALU.is_equal, ALU.mult))
                st.wait()
                list3, mid3 = listf[:, :, :], mid.rearrange("p (t k) -> p t k", k=SLOTS)
                st(dve.scalar_tensor_tensor(out=tabw[:, 0:T, 0:SLOTS], in0=list3, scalar=-1.0, in1=mid3, op0=ALU.add, op1=ALU.add))
                st(dve.tensor_scalar(tabw[:, 0:T, SLOTS:2 * SLOTS].bitcast(F32), list3, 0.0, MASKED, ALU.is_equal, ALU.mult))
                st(dve.tensor_copy(tabw[:, 0:T, 2 * SLOTS:2 * SLOTS + 1], ci[:, C_OWN:C_OWN + T].rearrange("p (t o) -> p t o", o=1)))
                dve.wait_ge(s_rank, 1)
                st(dve.tensor_copy(tot, ps[:, 1, :]))
                st.wait()
                st(dve.tensor_tensor_scan(incl, tot, zero, 0.0, ALU.add, ALU.add))
                st.wait()
                st(dve.tensor_tensor(posw, incl, tot, ALU.subtract))
                st(dve.tensor_tensor(over[:, 0:SLOTS], incl.rearrange("p (c t) -> p c t", t=T)[:, :, T - 1],
                                     cf[:, C_LIMIT:C_LIMIT + SLOTS], ALU.subtract))
                st(dve.tensor_scalar(over[:, SLOTS:SLOTS + 1], incl[:, 511:512], -1.0, float(N), ALU.mult, ALU.add))
                st.wait()
                st(dve.tensor_tensor(posw, posw, ps[:, 0, :], ALU.add))
                st(dve.tensor_reduce(stat[:, 0:1], over, AX.X, ALU.max))
                st.wait()
                st(dve.tensor_scalar(flag[:, :], stat[:, 0:1], 0.0, None, ALU.is_gt))
                st(dve.tensor_tensor(posw, posw, cls, ALU.mult))
                st.wait()
                st(dve.tensor_reduce(mid[:, 0:T], posw.rearrange("p (c t) -> p t c", t=T), AX.X, ALU.add))
                st.wait()
                st(dve.tensor_copy(rank[:, :], mid[:, 0:T]))
                st.wait()

            @block.tensor
            def _(pe):
                pe.wait_ge(s_cls, 1)
                pe.matmul(ps[:, 0, :], upperb, cls, start=True, stop=True)
                pe.matmul(ps[:, 1, :], onesb, cls, start=True, stop=True).then_inc(s_rank, 1)

        rowo = [carve(11520 + 512 * k, 512) for k in range(2)]
        kvo = [carve(12544 + 512 * k, 512) for k in range(2)]
        turnT = carve(13568, 256)
        biaso = biasb[:, :]
        stat2 = sb("stat2", [P, 64], F32)
        l_BN, l_MV = stat2[:, 0:6], stat2[:, 6:8]
        l_R, l_N = stat2[:, 8:9], stat2[:, 9:10]
        l_max, l_cmax = stat2[:, 16:24], stat2[:, 24:32]
        l_sum, l_csum, l_nmax = stat2[:, 32:33], stat2[:, 33:34], stat2[:, 34:35]

        d_own = carve(0, 512)
        d_kv = carve(512, 512)
        d_qT, d_kT = carve(1024, 256), carve(1280, 256)
        d_neg = carve(1536, P)
        d_score = carve(1664, H * P)
        d_prob = carve(2688, H * P)
        d_probT = carve(3712, H * P)
        d_acc = carve(4736, D)
        identb = carve(4992, P // 2).bitcast(BF16)
        d_mask = carve(5056, P // 2).bitcast(BF16)

        class LayerSems(dict):

            def __init__(self, layer):
                self.layer = layer

            def __missing__(self, name):
                self[name] = sem("l%d_%s" % (self.layer, name))
                return self[name]

        layer_sems = {1: LayerSems(1), 2: LayerSems(2)}

        def dense_layer(block_no, heads, src_row, src_kv, w_names):
            L = layer_sems[block_no]
            hardmax = heads > 1
            width = heads * P
            wide = [ps[:, 2 + k, :] for k in range(4)] if hardmax else [ps[:, 2, 0:P]]
            widep = [ps[:, 2, :], ps[:, 3, :]] if hardmax else [ps[:, 2, 0:P]]
            score, prob, probT = d_score[:, 0:width], d_prob[:, 0:width], d_probT[:, 0:width]

            def sync(sp):
                for j, name in enumerate(w_names):
                    sp.dma_start(wqkv[:, :, j * D:(j + 1) * D], dram[name].rearrange("(k p) n -> p k n", p=P)).then_inc(L["w_in"], 16)
                if not hardmax:
                    sp.dma_start(biaso, dram["bo2"].to_broadcast([P, D])).then_inc(L["w_in"], 16)
                with sp.Fori(0, T) as t:
                    sp.wait_ge(L["free"], t * (2 * T + 1) + 1)
                    sp.dma_start(d_own, rows(src_row, t)).then_inc(L["own_in"], 16)
                    with sp.Fori(0, 2 * T) as c:
                        sp.wait_ge(L["free"], t * (2 * T + 1) + c + 1)
                        chunk = c % T
                        sp.dma_start(d_kv, src_kv[bass.ds(chunk * P, P), :]).then_inc(L["kv_in"], 16)
                    sp.wait_ge(L["x_ready"], t + 1)
                    if hardmax:
                        sp.wait_ge(L["rowq"], t + 1)
                        sp.dma_start(rows(r2, t), rowo[0]).then_inc(L["row_out"], 16)
                        sp.dma_start(rows(kv2, t), kvo[0]).then_inc(L["row_out"], 16)
                        sp.wait_ge(L["row_out"], t * 32 + 32)
                        sp.sem_inc(paced, 1)
                    else:
                        sp.dma_start(rows(yst, t), rowo[0][:, 0:D + 2]).then_inc(L["row_out"], 16)
                        sp.wait_ge(L["row_out"], t * 16 + 16)
                        sp.sem_inc(paced, 1)

            def tensor(pe):
                pe.wait_ge(L["w_in"], 48 if hardmax else 32)
                pe.wait_ge(L["identb"], 1)
                with pe.Fori(0, T) as t:
                    pe.wait_ge(L["own_in"], t * 16 + 16)
                    for k in range(KD):
                        mm = pe.transpose(ps[:, 0, k * P:(k + 1) * P], d_own[:, D + k * P:D + (k + 1) * P], ident)
                    mm.then_inc(L["turned_q"], 1)
                    pe.wait_ge(L["qT"], t + 1)
                    pe.sem_inc(paced, 1)

                    def scores(t, c, n):
                        pe.wait_ge(L["kv_in"], n * 16 + 16)
                        for k in range(KD):
                            pe.transpose(ps[:, 0, k * P:(k + 1) * P], d_kv[:, k * P:(k + 1) * P], ident)
                        pe.wait_ge(L["mask"], n + 1)
                        pe.matmul(ps[:, 1, 0:P], d_mask, identb, start=True, stop=True).then_inc(L["turned"], 1)
                        pe.wait_ge(L["kT"], n + 1)
                        for h in range(heads):
                            if hardmax:
                                at = HD * (h % 4)
                                k = h // 4
                                mm = pe.matmul(wide[h % 4][:, k * P:(k + 1) * P], d_qT[at:at + HD, k * P:(k + 1) * P],
                                               d_kT[at:at + HD, k * P:(k + 1) * P], start=True, stop=True)
                            else:
                                for k in range(KD):
                                    mm = pe.matmul(wide[0], d_qT[:, k * P:(k + 1) * P], d_kT[:, k * P:(k + 1) * P],
                                                   start=(k == 0), stop=(k == KD - 1))
                        mm.then_inc(L["scored"], 1)

                    with pe.Fori(0, T) as c:
                        scores(t, c, t * (2 * T) + c)
                    with pe.Fori(0, T) as c:
                        scores(t, c, t * (2 * T) + c + T)
                        pe.wait_ge(L["prob"], t * T + c + 1)
                        for h in range(heads):
                            mm = pe.transpose(widep[h // 4][:, (h % 4) * P:(h % 4 + 1) * P], prob[:, h * P:(h + 1) * P], ident)
                        mm.then_inc(L["turned_p"], 1)
                        pe.wait_ge(L["probT"], t * T + c + 1)
                        w = D // heads
                        for h in range(heads):
                            mm = pe.matmul(ps[:, 6, h * w:(h + 1) * w], probT[:, h * P:(h + 1) * P], d_kv[:, D + h * w:D + (h + 1) * w],
                                           start=True, stop=True)
                        mm.then_inc(L["pv"], 1)
                    pe.wait_ge(L["normed"], t + 1)
                    src = rowo[0][:, 0:D] if hardmax else d_acc
                    for k in range(KD):
                        mm = pe.transpose(ps[:, 0, k * P:(k + 1) * P], src[:, k * P:(k + 1) * P], ident)
                    mm.then_inc(L["y_turned"], 1)
                    pe.wait_ge(L["yT"], t + 1)
                    for k in range(KD):
                        if hardmax:
                            pe.matmul(ps[:, 2, :], turnT[:, k * P:(k + 1) * P], wqkv[:, k, 0:2 * D], start=(k == 0), stop=(k == KD - 1))
                        else:
                            mm = pe.matmul(ps[:, 2, 0:D], turnT[:, k * P:(k + 1) * P], wqkv[:, k, 0:D], start=(k == 0), stop=(k == KD - 1))
                    if hardmax:
                        for k in range(KD):
                            mm = pe.matmul(ps[:, 3, 0:D], turnT[:, k * P:(k + 1) * P], wqkv[:, k, 2 * D:3 * D], start=(k == 0), stop=(k == KD - 1))
                    mm.then_inc(L["proj"], 1)

            def scalar(act):
                def mask(t, c, step):
                    act.wait_ge(L["free"], t * (2 * T + 1) + step + 1)
                    src = adjbytes[:, bass.ds(t, 1), bass.ds(c * P, P)].rearrange("p a i -> p (a i)")
                    act.activation(d_mask, src, ACT.Copy, scale=1.0 / ONE8).then_inc(L["mask"], 1)

                act.wait_ge(tail_in, 64)
                with act.Fori(0, T) as t:
                    act.wait_ge(L["turned_q"], t + 1)
                    act.activation(d_qT, ps[:, 0, 0:D], ACT.Copy).then_inc(L["qT"], 1)
                    with act.Fori(0, T) as c:
                        mask(t, c, c)
                        act.wait_ge(L["turned"], t * (2 * T) + c + 1)
                        act.activation(d_kT, ps[:, 0, 0:D], ACT.Copy).then_inc(L["kT"], 1)
                    with act.Fori(0, T) as c:
                        mask(t, c, c + T)
                        act.wait_ge(L["turned"], t * (2 * T) + c + T + 1)
                        act.activation(d_kT, ps[:, 0, 0:D], ACT.Copy).then_inc(L["kT"], 1)
                        if not hardmax:
                            act.wait_ge(L["nmax"], t * T + c + 1)
                            act.activation(prob, score, ACT.Exp, bias=l_nmax, scale=SCALE2, accum_out=l_csum).then_inc(L["prob"], 1)
                        act.wait_ge(L["turned_p"], t * T + c + 1)
                        src = ps[:, 2:4, :].rearrange("p a n -> p (a n)") if hardmax else widep[0]
                        act.activation(probT, src, ACT.Copy).then_inc(L["probT"], 1)
                    if hardmax:
                        act.wait_ge(L["var"], t + 1)
                        act.activation(l_R, l_R, ACT.Sqrt).then_inc(L["rstd"], 1)
                    act.wait_ge(L["y_turned"], t + 1)
                    act.activation(turnT, ps[:, 0, 0:D], ACT.Copy).then_inc(L["yT"], 1)
                    if hardmax:
                        act.wait_ge(L["proj"], t + 1)
                        act.activation(kvo[0], ps[:, 2, :], ACT.Copy).then_inc(L["kvrow"], 1)
                        act.wait_ge(L["kvrow"], t + 1)
                        act.activation(rowo[0][:, D:2 * D], ps[:, 3, 0:D], ACT.Copy).then_inc(L["rowq"], 1)

            def vector(dve):
                FRONT, ONE, TWO, END = 2, 5 if hardmax else 4, 5 if hardmax else 6, 8 if hardmax else 6
                per = FRONT + T * (ONE + TWO) + END
                st = Steps(dve, L["step"], 0, paced)
                st(dve.tensor_copy(identb, ident))
                st.wait()
                dve.sem_inc(L["identb"], 1)
                dve.sem_inc(L["free"], 1)
                base = 1

                def masked(st, n):
                    dve.wait_ge(L["turned"], n + 1)
                    st(dve.tensor_scalar(d_neg, ps[:, 1, 0:P], -MASKED, MASKED, ALU.mult, ALU.add))
                    st.wait()
                    if hardmax:
                        st(dve.tensor_scalar(d_neg, d_neg, beb[:, 0:1], None, ALU.add))
                        st.wait()
                    dve.wait_ge(L["scored"], n + 1)
                    if hardmax:
                        st(dve.tensor_tensor(score.rearrange("p (k a n) -> p a k n", k=KD, n=P),
                                             ps[:, 2:6, 0:KD * P].rearrange("p a (k n) -> p a k n", n=P),
                                             d_neg.rearrange("p (b o n) -> p b o n", o=1, b=1).to_broadcast([P, 4, KD, P]), ALU.add))
                    else:
                        st(dve.tensor_tensor(score, wide[0], d_neg, ALU.add))
                    st.wait()

                with dve.Fori(0, T) as t:
                    tb = base + t * per
                    st = Steps(dve, L["step"], tb, paced)
                    st(dve.memset(l_max[:, 0:heads], -3.0e38))
                    st(dve.memset(d_acc, 0.0))
                    st.wait(alone=True)
                    with dve.Fori(0, T) as c:
                        st = Steps(dve, L["step"], tb + c * ONE + FRONT, paced)
                        masked(st, t * (2 * T) + c)
                        st(dve.tensor_reduce(l_cmax[:, 0:heads], score.rearrange("p (h n) -> p h n", n=P), AX.X, ALU.max))
                        st.wait()
                        st(dve.tensor_tensor(l_max[:, 0:heads], l_max[:, 0:heads], l_cmax[:, 0:heads], ALU.max))
                        st.wait()
                        dve.sem_inc(L["free"], 1)
                        assert st.count == ONE, st.count
                    if not hardmax:
                        dve.memset(l_sum, 0.0).then_inc(L["var"], 1)
                        dve.wait_ge(L["var"], t + 1)
                        dve.sem_inc(paced, 1)
                    with dve.Fori(0, T) as c:
                        st = Steps(dve, L["step"], tb + c * TWO + (FRONT + T * ONE), paced)
                        masked(st, t * (2 * T) + c + T)
                        if hardmax:
                            st(dve.tensor_tensor(prob.rearrange("p (h n) -> p h n", n=P), score.rearrange("p (h n) -> p h n", n=P),
                                                 l_max.rearrange("p (h o) -> p h o", o=1).to_broadcast([P, heads, P]), ALU.is_equal))
                            st.wait()
                            dve.sem_inc(L["prob"], 1)
                        else:
                            st(dve.tensor_scalar(l_nmax, l_max[:, 0:1], -SCALE2, None, ALU.mult))
                            st.wait()
                            dve.sem_inc(L["nmax"], 1)
                            dve.wait_ge(L["prob"], t * T + c + 1)
                            st(dve.tensor_tensor(l_sum, l_sum, l_csum, ALU.add))
                            st.wait()
                        dve.wait_ge(L["pv"], t * T + c + 1)
                        st(dve.tensor_tensor(d_acc, d_acc, ps[:, 6, 0:D], ALU.add))
                        st.wait()
                        if not hardmax:
                            st(dve.memset(l_cmax[:, 0:1], 0.0))
                            st.wait()
                        dve.sem_inc(L["free"], 1)
                        assert st.count == TWO, st.count
                    st = Steps(dve, L["step"], tb + (FRONT + T * (ONE + TWO)), paced)
                    if hardmax:
                        y = rowo[0][:, 0:D]
                        st(dve.scalar_tensor_tensor(out=y, in0=d_acc, scalar=1.0 / H, in1=d_own[:, 0:D], op0=ALU.mult, op1=ALU.add))
                        st.wait()
                        statistics(dve, st, y, L["var"])
                        newton(dve, st, L["rstd"], t)
                        st(dve.tensor_scalar(y, y, l_MV[:, 0:1], l_R, ALU.subtract, ALU.mult))
                        st.wait()
                        dve.sem_inc(L["normed"], 1)
                        dve.wait_ge(L["rowq"], t + 1)
                        dve.sem_inc(L["x_ready"], 1)
                    else:
                        st(dve.reciprocal(l_sum, l_sum))
                        st.wait()
                        st(dve.tensor_scalar(d_acc, d_acc, l_sum, None, ALU.mult))
                        st.wait()
                        dve.sem_inc(L["normed"], 1)
                        dve.wait_ge(L["w_in"], 32)
                        y = rowo[0][:, 0:D]
                        st(dve.tensor_tensor(y, d_own[:, 0:D], biaso, ALU.add))
                        st.wait()
                        dve.wait_ge(L["proj"], t + 1)
                        st(dve.tensor_tensor(y, y, ps[:, 2, 0:D], ALU.add))
                        st.wait()
                        st(dve.bn_stats(l_BN, y))
                        st.wait(alone=True)
                        st(dve.bn_aggr(rowo[0][:, D:D + 2], l_BN))
                        st.wait()
                        dve.sem_inc(L["x_ready"], 1)
                    dve.wait_ge(L["row_out"], t * (32 if hardmax else 16) + (32 if hardmax else 16))
                    dve.sem_inc(L["free"], 1)
                    assert st.count == END, st.count

            return sync, tensor, scalar, vector

        def statistics(dve, st, y, var_ready):
            st(dve.bn_stats(l_BN, y))
            st.wait(alone=True)
            st(dve.bn_aggr(l_MV, l_BN))
            st.wait()
            st(dve.tensor_scalar(l_N, l_MV[:, 1:2], EPS, None, ALU.add))
            st.wait()
            dve.reciprocal(l_R, l_N).then_inc(var_ready, 1)

        def newton(dve, st, rstd_ready, t):
            dve.wait_ge(rstd_ready, t + 1)
            st(dve.tensor_scalar(l_N, l_N, l_R, l_R, ALU.mult, ALU.mult))
            st.wait()
            st(dve.tensor_scalar(l_N, l_N, -0.5, 1.5, ALU.mult, ALU.add))
            st.wait()
            st(dve.tensor_tensor(l_R, l_R, l_N, ALU.mult))
            st.wait()

        dense = [dense_layer(1, H, r1, kv1, ("WK2T", "WV2T", "WQ2T")), dense_layer(2, 1, r2, kv2, ("WO2T",))]
        kvbuf = carve(0, 2 * KV_SLOTS * 2 * D).rearrange("p (s n) -> p s n", n=2 * D)
        prod = carve(9216, KV_SLOTS * D)
        g_own = [comb[:, 512 * k:512 * k + 512] for k in range(2)]
        xb = [carve(12544 + 256 * k, 256) for k in range(2)]
        attn = carve(13056, 256)
        logit = carve(13824, SLOTS * H)
        picked = carve(13952, SLOTS * H)
        negb = carve(14080, SLOTS)
        prob2 = [carve(14096 + SLOTS * k, SLOTS) for k in range(2)]
        s_idx = [carve(14128 + 20 * k, SLOTS + 1).bitcast(I32) for k in range(2)]
        sid = sb("sid", [P, 2], I32)
        s_sum = stat2[:, 36:38]
        s_inv = stat2[:, 38:39]
        RUNS = []
        for t in range(1, T - 1, 2):
            c = CAPS[t]
            assert CAPS[t + 1] <= c <= KV_SLOTS
            if RUNS and RUNS[-1][2] == c:
                RUNS[-1][1] += 2
            else:
                RUNS.append([t, 2, c])

        def ranked_tiles(eng, body):
            body(0, 0, 0, CAPS[0], 0)
            before = [CAPS[0], 0]
            for first, count, slots in RUNS:
                q = (first - 1) // 2
                if count == 2:
                    body(first, q, 1, slots, before[1])
                    body(first + 1, q + 1, 0, slots, before[0])
                else:
                    with eng.Fori(0, count // 2) as i:
                        body(i * 2 + first, i + q, 1, slots, i * slots + before[1])
                        body(i * 2 + (first + 1), i + (q + 1), 0, slots, i * slots + before[0])
                before = [b + count // 2 * slots for b in before]
            body(T - 1, T // 2 - 1, 1, CAPS[T - 1], before[1])

        def kv_of(u, slots):
            at = KV_SLOTS * u if slots <= KV_SLOTS else 0
            return kvbuf[:, at:at + slots, :]

        def below(t, k):
            return isinstance(t, int) and t < k

        def back(t, q, u, k):
            if k % 2 == 0:
                return t - k, q - k // 2, u
            return t - k, (q - (k - 1) // 2 if u else q - (k + 1) // 2), 1 - u

        def sparse_layer(layer):
            S = layer_sems[layer]
            one = layer == 1
            src_kv = kv1 if one else kv2

            def sync(sp):
                names = ("WK2T", "WV2T", "WQ2T") if one else ("WO2T",)
                for j, name in enumerate(names):
                    sp.dma_start(wqkv[:, :, j * D:(j + 1) * D], dram[name].rearrange("(k p) n -> p k n", p=P)).then_inc(S["w_in"], 16)
                if one:
                    sp.wait_ge(S["table_out"], 16 * T)
                    sp.dma_start(tabw[:, 0:T, :], table.rearrange("(t p) n -> p t n", p=P)).then_inc(S["tab_in"], 16)

                    def store(t, q, u):
                        sp.wait_ge(S["x_ready"], t + 1)
                        sp.wait_ge(S["rowq"], t + 1)
                        sp.dma_start(rows(r2, t), rowo[u]).then_inc(S["row_out%d" % u], 16)

                    with sp.Fori(0, T // 2) as i:
                        store(i * 2, i, 0)
                        store(i * 2 + 1, i, 1)
                    sp.wait_ge(S["row_out0"], 16 * T // 2)
                    sp.wait_ge(S["row_out1"], 16 * T // 2)
                else:
                    sp.dma_start(biaso, dram["bo2"].to_broadcast([P, D])).then_inc(S["w_in"], 16)

                    def load(t, q, u):
                        if not below(t, 2):
                            sp.wait_ge(S["own_free"], t - 1)
                        sp.dma_start(g_own[u], rows(r2, t)).then_inc(S["own_in%d" % u], 16)

                    load(0, 0, 0)
                    load(1, 0, 1)
                    with sp.Fori(1, T // 2) as i:
                        load(i * 2, i, 0)
                        load(i * 2 + 1, i, 1)

            def gpsimd(pool):
                if one:
                    for t in range(T):
                        pool.indirect_dma_start(
                            out=table, out_offset=bass.IndirectOffsetOnAxis(ap=rank[:, t:t + 1], axis=0),
                            in_=tabw[:, t, :], in_offset=None).then_inc(S["table_out"], 16)
                    pool.wait_ge(S["mem"], 1)

                def gather(out_ap, src, idx, s_in, skip):
                    pool.indirect_dma_start(out=out_ap, out_offset=None, in_=src,
                                            in_offset=bass.IndirectOffsetOnAxis(ap=idx, axis=0),
                                            bounds_check=N - 1, oob_is_err=not skip).then_inc(s_in, 16)

                def scatter(t, q, u):
                    pool.wait_ge(S["kvrow"] if one else S["x_ready"], t + 1)
                    pool.wait_ge(S["sid_ready"], t + 1)
                    pool.sem_inc(paced, 1)
                    src, dst = (kvo[u], kv2) if one else (rowo[u][:, 0:D + 2], yst)
                    pool.indirect_dma_start(out=dst, out_offset=bass.IndirectOffsetOnAxis(ap=sid[:, u:u + 1], axis=0),
                                            in_=src, in_offset=None).then_inc(S["kv_out%d" % u], 16)

                late = 2 if one else 3

                def body(t, q, u, slots, g):
                    pool.wait_ge(S["idx_ready"], t + 1)
                    if not below(t, 1):
                        pool.wait_ge(S["summed"], 1 if below(t, 2) else t - 1)
                    pool.sem_inc(paced, 1)
                    kv = kv_of(u, slots)
                    for k in range(slots):
                        gather(kv[:, k, :], src_kv, s_idx[u][:, k:k + 1], S["kv_in%d" % u], True)
                    if one:
                        if not below(t, 2):
                            pool.wait_ge(S["y_done"], t - 1)
                            pool.sem_inc(paced, 1)
                        gather(g_own[u], r1, s_idx[u][:, SLOTS:SLOTS + 1], S["own_in%d" % u], False)
                    if not below(t, late):
                        scatter(*back(t, q, u, late))

                ranked_tiles(pool, body)
                for k in range(late - 1, -1, -1):
                    scatter(*back(T - 1, T // 2 - 1, 1, k))
                pool.wait_ge(S["kv_out0"], 16 * T // 2)
                pool.wait_ge(S["kv_out1"], 16 * T // 2)

            def tensor(pe):
                pe.wait_ge(S["w_in"], 48 if one else 32)

                def total(t, q, u, slots):
                    pe.wait_ge(S["v_ready"], t + 1)
                    if not below(t, 2):
                        pe.wait_ge(S["y_done"], t - 1)
                    kv = kv_of(u, slots)
                    for k in range(slots):
                        mm = pe.matmul(ps[:, 6 + u, 0:D], ident, kv[:, k, D:2 * D], start=(k == 0), stop=(k == slots - 1))
                    mm.then_inc(S["summed"], 1)

                def project(t, q, u):
                    pe.wait_ge(S["x_ready"] if one else S["attn"], t + 1)
                    src = rowo[u][:, 0:D] if one else attn
                    for k in range(KD):
                        mm = pe.transpose(ps[:, 0, k * P:(k + 1) * P], src[:, k * P:(k + 1) * P], ident)
                    mm.then_inc(S["turned"], 1)
                    pe.wait_ge(S["turn_out"], t + 1)
                    if one:
                        if not below(t, 1):
                            pe.wait_ge(S["kvrow"], t)
                            pe.wait_ge(S["rowq"], t)
                        for k in range(KD):
                            pe.matmul(ps[:, 2, :], turnT[:, k * P:(k + 1) * P], wqkv[:, k, 0:2 * D], start=(k == 0), stop=(k == KD - 1))
                        for k in range(KD):
                            mm = pe.matmul(ps[:, 3, 0:D], turnT[:, k * P:(k + 1) * P], wqkv[:, k, 2 * D:3 * D], start=(k == 0), stop=(k == KD - 1))
                    else:
                        if not below(t, 1):
                            pe.wait_ge(S["x_ready"], t)
                        for k in range(KD):
                            mm = pe.matmul(ps[:, 2, 0:D], turnT[:, k * P:(k + 1) * P], wqkv[:, k, 0:D], start=(k == 0), stop=(k == KD - 1))
                    mm.then_inc(S["proj"], 1)

                def body(t, q, u, slots, g):
                    if one:
                        total(t, q, u, slots)
                    if not below(t, 1):
                        project(*back(t, q, u, 1))
                    if not one:
                        total(t, q, u, slots)

                ranked_tiles(pe, body)
                project(T - 1, T // 2 - 1, 1)

            def scalar(act):
                def project(t, q, u):
                    if one:
                        act.wait_ge(S["var"], t + 1)
                        act.activation(l_R, l_R, ACT.Sqrt).then_inc(S["rstd"], 1)
                    act.wait_ge(S["turned"], t + 1)
                    act.activation(turnT, ps[:, 0, 0:D], ACT.Copy).then_inc(S["turn_out"], 1)
                    if one:
                        act.wait_ge(S["proj"], t + 1)
                        if not below(t, 2):
                            act.wait_ge(S["kv_out%d" % u], 16 * q)
                            act.wait_ge(S["row_out%d" % u], 16 * q)
                        act.activation(kvo[u], ps[:, 2, :], ACT.Copy).then_inc(S["kvrow"], 1)
                        act.activation(rowo[u][:, D:2 * D], ps[:, 3, 0:D], ACT.Copy).then_inc(S["rowq"], 1)

                def body(t, q, u, slots, g):
                    if not one:
                        act.wait_ge(S["nmax"], t + 1)
                        act.activation(prob2[u][:, 0:slots], logit[:, 0:slots], ACT.Exp, bias=l_nmax, scale=SCALE2,
                                       accum_out=s_sum[:, u:u + 1]).then_inc(S["prob"], 1)
                    if not below(t, 1):
                        project(*back(t, q, u, 1))

                ranked_tiles(act, body)
                project(T - 1, T // 2 - 1, 1)

            def vector(dve):
                FRONT = 7 if one else 6
                BACK = 6 if one else 7
                heads = H if one else 1

                def index(t, u):
                    src = tabw[:, bass.ds(t, 1), :].rearrange("p a n -> p (a n)")
                    dve.tensor_copy(s_idx[u][:, 0:SLOTS], src[:, 0:SLOTS]).then_inc(S["front"], 1)
                    dve.tensor_copy(s_idx[u][:, SLOTS:SLOTS + 1], src[:, 2 * SLOTS:2 * SLOTS + 1]).then_inc(S["front"], 1)

                if one:
                    dve.memset(kvbuf.rearrange("p s n -> p (s n)"), 0.0).then_inc(S["mem"], 1)
                    dve.wait_ge(S["tab_in"], 16)
                index(0, 0)
                index(1, 1)
                dve.wait_ge(S["front"], 4)
                dve.sem_inc(S["idx_ready"], 2)
                base = 4
                if not one:
                    dve.wait_ge(S["w_in"], 32)

                def product(t, q, u, slots, g):
                    st = Steps(dve, S["front"], t * FRONT + base, paced)
                    kv = kv_of(u, slots)
                    dve.wait_ge(S["kv_in%d" % u], g * 16 + 16 * slots)
                    dve.wait_ge(S["own_in%d" % u], 16 * q + 16)
                    out = prod.rearrange("p (s n) -> p s n", n=D)[:, 0:slots, :] if slots <= KV_SLOTS else kv[:, :, 0:D]
                    qv = g_own[u][:, D:2 * D].rearrange("p (o n) -> p o n", o=1).to_broadcast([P, slots, D])
                    st(dve.tensor_tensor(out, kv[:, :, 0:D], qv, ALU.mult))
                    index(min(t + 2, T) if isinstance(t, int) else t + 2, u)
                    st.count += 2
                    st.wait()
                    dve.sem_inc(S["idx_ready"], 1)
                    if one:
                        st(dve.tensor_scalar(negb[:, 0:slots], neg_of(t, slots), beb[:, 0:1], None, ALU.add))
                        return st.count
                    st(dve.tensor_reduce(logit[:, 0:slots], out, AX.X, ALU.add))
                    st.wait()
                    st(dve.tensor_tensor(logit[:, 0:slots], logit[:, 0:slots], neg_of(t, slots), ALU.add))
                    st.wait()
                    st(dve.tensor_reduce(l_max[:, 0:1], logit[:, 0:slots], AX.X, ALU.max))
                    st.wait()
                    dve.tensor_scalar(l_nmax, l_max[:, 0:1], -SCALE2, None, ALU.mult).then_inc(S["nmax"], 1)
                    return st.count

                def neg_of(t, slots):
                    return tabw[:, bass.ds(t, 1), SLOTS:SLOTS + slots].bitcast(F32).rearrange("p a n -> p (a n)")

                def weigh(t, q, u, slots, done):
                    kv = kv_of(u, slots)
                    if one:
                        st = Steps(dve, S["front"], t * FRONT + (base + done), paced)
                        out = prod.rearrange("p (s n) -> p s n", n=D)[:, 0:slots, :] if slots <= KV_SLOTS else kv[:, :, 0:D]
                        lg = logit[:, 0:slots * H].rearrange("p (s h) -> p s h", h=H)
                        pk = picked[:, 0:slots * H].rearrange("p (s h) -> p s h", h=H)
                        st(dve.tensor_reduce(lg, out.rearrange("p s (h n) -> p s h n", n=HD), AX.X, ALU.add))
                        st.wait()
                        st(dve.tensor_tensor(lg, lg, negb[:, 0:slots].rearrange("p (s o) -> p s o", o=1).to_broadcast([P, slots, H]), ALU.add))
                        st.wait()
                        st(dve.tensor_reduce(l_max, lg.rearrange("p s h -> p h s"), AX.X, ALU.max))
                        st.wait()
                        weight_step(dve, pk, lg, slots).then_inc(S["prob"], 1)
                        dve.wait_ge(S["prob"], t + 1)
                        v = kv[:, :, D:2 * D].rearrange("p s (h n) -> p s h n", n=HD)
                        w = pk.rearrange("p s (h o) -> p s h o", o=1).to_broadcast([P, slots, H, HD])
                        dve.tensor_tensor(v, v, w, ALU.mult).then_inc(S["v_ready"], 1)
                        assert done + st.count == FRONT, (done, st.count)
                    else:
                        dve.wait_ge(S["prob"], t + 1)
                        w = prob2[u][:, 0:slots].rearrange("p (s o) -> p s o", o=1).to_broadcast([P, slots, D])
                        dve.tensor_tensor(kv[:, :, D:2 * D], kv[:, :, D:2 * D], w, ALU.mult).then_inc(S["v_ready"], 1)
                        dve.tensor_tensor(xb[u], g_own[u][:, 0:D], biaso, ALU.add).then_inc(S["own_free"], 1)

                def weight_step(dve, pk, lg, slots):
                    return dve.tensor_tensor(pk, lg, l_max.rearrange("p (o h) -> p o h", o=1).to_broadcast([P, slots, H]), ALU.is_equal)

                def name(t, q, u):
                    if not below(t, 2):
                        dve.wait_ge(S["kv_out%d" % u], 16 * q)
                    dve.tensor_copy(sid[:, u:u + 1], tabw[:, bass.ds(t, 1), 2 * SLOTS:2 * SLOTS + 1].rearrange("p a n -> p (a n)")).then_inc(S["sid_ready"], 1)

                def residual(t, q, u):
                    st = Steps(dve, S["back"], t * BACK, paced)
                    y = rowo[u][:, 0:D]
                    name(t, q, u)
                    dve.wait_ge(S["summed"], t + 1)
                    if not below(t, 2):
                        dve.wait_ge(S["row_out%d" % u], 16 * q)
                    dve.scalar_tensor_tensor(out=y, in0=ps[:, 6 + u, 0:D], scalar=1.0 / H, in1=g_own[u][:, 0:D],
                                             op0=ALU.mult, op1=ALU.add).then_inc(S["y_done"], 1)
                    dve.wait_ge(S["y_done"], t + 1)
                    statistics(dve, st, y, S["var"])
                    assert st.count == 3

                def normalize(t, q, u):
                    st = Steps(dve, S["back"], t * BACK + 3, paced)
                    y = rowo[u][:, 0:D]
                    newton(dve, st, S["rstd"], t)
                    dve.tensor_scalar(y, y, l_MV[:, 0:1], l_R, ALU.subtract, ALU.mult).then_inc(S["x_ready"], 1)
                    assert st.count == BACK - 3

                def finish(t, q, u):
                    st = Steps(dve, S["back"], t * 2, paced)
                    name(t, q, u)
                    y = rowo[u][:, 0:D]
                    dve.wait_ge(S["proj"], t + 1)
                    dve.wait_ge(S["own_free"], t + 1)
                    st(dve.tensor_tensor(y, ps[:, 2, 0:D], xb[u], ALU.add))
                    st.wait()
                    st(dve.bn_stats(l_BN, y))
                    st.wait(alone=True)
                    dve.bn_aggr(rowo[u][:, D:D + 2], l_BN).then_inc(S["x_ready"], 1)

                def divide(t, q, u):
                    dve.reciprocal(s_inv, s_sum[:, u:u + 1]).then_inc(S["mem"], 1)
                    dve.wait_ge(S["mem"], t + 1)
                    dve.wait_ge(S["summed"], t + 1)
                    dve.tensor_scalar(attn, ps[:, 6 + u, 0:D], s_inv, None, ALU.mult).then_inc(S["attn"], 1)
                    dve.wait_ge(S["attn"], t + 1)
                    dve.sem_inc(S["y_done"], 1)

                def body(t, q, u, slots, g):
                    done = product(t, q, u, slots, g)
                    if one:
                        if not below(t, 1):
                            residual(*back(t, q, u, 1))
                        weigh(t, q, u, slots, done)
                        if not below(t, 1):
                            normalize(*back(t, q, u, 1))
                    else:
                        assert done == FRONT
                        if not below(t, 2):
                            finish(*back(t, q, u, 2))
                        if not below(t, 1):
                            divide(*back(t, q, u, 1))
                        weigh(t, q, u, slots, done)

                ranked_tiles(dve, body)
                last = (T - 1, T // 2 - 1, 1)
                if one:
                    residual(*last)
                    normalize(*last)
                else:
                    finish(*back(*last, 1))
                    divide(*last)
                    finish(*last)

            return sync, tensor, scalar, vector, gpsimd

        sparse = [sparse_layer(1), sparse_layer(2)]
        for n in range(2):
            ways = (sparse[n], dense[n])

            def either(eng, k):
                overflow = eng.value_load(flag[0:1, 0:1], min_val=0, max_val=1)
                with eng.If(overflow == 0):
                    ways[0][k](eng)
                with eng.Else():
                    ways[1][k](eng)

            with nc.Block() as block:
                @block.gpsimd
                def _(pool):
                    overflow = pool.value_load(flag[0:1, 0:1], min_val=0, max_val=1)
                    with pool.If(overflow == 0):
                        ways[0][4](pool)

                @block.sync
                def _(sp):
                    either(sp, 0)

                @block.tensor
                def _(pe):
                    either(pe, 1)

                @block.scalar
                def _(act):
                    either(act, 2)

                @block.vector
                def _(dve):
                    either(dve, 3)
        PARTS = 3
        ys = carve(0, T * (D + 2)).rearrange("p (t n) -> p t n", n=D + 2)
        b3 = T * (D + 2)
        rstd = carve(b3, T)
        newt = carve(b3 + T, T)
        vr = carve(b3 + 2 * T, T)
        vp = carve(b3 + 3 * T, T * 4 // 2).bitcast(BF16).rearrange("p (t n) -> p t n", n=4)
        b3 += 3 * T + T * 2
        x3T = [carve(b3 + 256 * k, 256) for k in range(2)]
        outb = [carve(b3 + 512 + 256 * k, 256) for k in range(2)]
        srow = carve(b3 + 1024, N)
        wsumr = carve(b3 + 1024 + N, 256)
        onesf = carve(b3 + 1280 + N, 4)
        x3b = [carve(b3 + 1284 + N + 256 * k, 256) for k in range(2)]
        s_tile = [carve(b3 + 1796 + N + P * k, P) for k in range(2)]
        w3s = weights[:, 0:KD * D].rearrange("p (k n) -> p k n", k=KD)
        w3n = weights[:, KD * D:2 * KD * D].rearrange("p (k n) -> p k n", k=KD)
        BN3 = [stat[:, 0:6], stat[:, 6:12]]
        MV3 = [stat[:, 12:14], stat[:, 14:16]]
        R3 = [stat[:, 16:17], stat[:, 17:18]]
        N3 = [stat[:, 18:19], stat[:, 19:20]]
        u3 = {n: sem("l3_" + n) for n in ("y_in", "w_in", "step", "a3", "sq", "parts", "wsum", "wsum_out", "s_done", "s_out",
                                         "turned", "x3T", "proj", "var", "rstd", "out_ready", "out0", "out1", "norm", "s_tile")}
        GROUP = 4

        with nc.Block() as block:
            @block.sync
            def _(sp):
                src = yst.rearrange("(t p) n -> p t n", p=P)
                for k in range(4):
                    sp.dma_start(ys[:, 8 * k:8 * k + 8, :], src[:, 8 * k:8 * k + 8, :]).then_inc(u3["y_in"], 16)
                sp.dma_start(w3s, dram["WS3T"].rearrange("(k p) n -> p k n", p=P)).then_inc(u3["w_in"], 16)
                sp.dma_start(w3n, dram["WN3T"].rearrange("(k p) n -> p k n", p=P)).then_inc(u3["w_in"], 16)
                with sp.Fori(0, T // 2) as i:
                    for u in range(2):
                        sp.wait_ge(u3["out_ready"], i * 2 + u + 1)
                        sp.dma_start(rows(out, i * 2 + u), outb[u]).then_inc(u3["out%d" % u], 16)
                sp.wait_ge(u3["out0"], 16 * T // 2)
                sp.wait_ge(u3["out1"], 16 * T // 2)

            @block.tensor
            def _(pe):
                pe.wait_ge(u3["w_in"], 32)
                pe.wait_ge(u3["wsum"], 1)
                for k in range(KD):
                    mm = pe.matmul(ps[0:PARTS, 0, 0:D], onesf[:, 0:PARTS], w3n[:, k, :], start=(k == 0), stop=(k == KD - 1))
                mm.then_inc(u3["wsum_out"], 1)
                pe.wait_ge(u3["parts"], 1)
                pe.wait_ge(u3["wsum"], 2)

                pe.wait_ge(tail_in, 64)
                for g in range(T // GROUP):
                    for c in range(T):
                        mask = adj8[:, g * GROUP:(g + 1) * GROUP, c, :]
                        mm = pe.matmul(ps[0:PARTS, g, :], vp[:, c, 0:PARTS], mask, start=(c == 0), stop=(c == T - 1))
                    mm.then_inc(u3["s_done"], 1)
                pe.wait_ge(u3["s_out"], T // GROUP)

                def turn(t, v):
                    pe.wait_ge(u3["norm"], t + 1)
                    for k in range(KD):
                        mm = pe.transpose(ps[:, 2 + v, k * P:(k + 1) * P], x3b[v][:, k * P:(k + 1) * P], ident)
                    mm.then_inc(u3["turned"], 1)

                def project(t, v):
                    pe.wait_ge(u3["x3T"], t + 1)
                    if not (isinstance(t, int) and t < 2):
                        pe.wait_ge(u3["a3"], t - 1)
                    bank = ps[:, 4 + v, 0:D]
                    for k in range(KD):
                        pe.matmul(bank, x3T[v][:, k * P:(k + 1) * P], w3s[:, k, :], start=(k == 0), stop=False)
                    pe.wait_ge(u3["s_tile"], t + 1)
                    pe.matmul(bank, s_tile[v][0:PARTS, :], wsumr[0:PARTS, :], start=False, stop=True).then_inc(u3["proj"], 1)

                turn(0, 0)
                turn(1, 1)
                project(0, 0)
                turn(2, 0)
                project(1, 1)
                with pe.Fori(1, T // 2 - 1) as i:
                    turn(i * 2 + 1, 1)
                    project(i * 2, 0)
                    turn(i * 2 + 2, 0)
                    project(i * 2 + 1, 1)
                turn(T - 1, 1)
                project(T - 2, 0)
                project(T - 1, 1)

            @block.scalar
            def _(act):
                act.wait_ge(u3["step"], 2)
                act.activation(rstd, rstd, ACT.Sqrt).then_inc(u3["sq"], 1)
                act.wait_ge(u3["wsum_out"], 1)
                act.activation(wsumr[0:PARTS, :], ps[0:PARTS, 0, 0:D], ACT.Copy).then_inc(u3["wsum"], 1)

                for g in range(T // GROUP):
                    act.wait_ge(u3["s_done"], g + 1)
                    act.activation(srow[0:PARTS, g * GROUP * P:(g + 1) * GROUP * P], ps[0:PARTS, g, :], ACT.Copy).then_inc(u3["s_out"], 1)

                def turned(t, v):
                    act.wait_ge(u3["turned"], t + 1)
                    act.activation(x3T[v], ps[:, 2 + v, 0:D], ACT.Copy).then_inc(u3["x3T"], 1)
                    act.activation(s_tile[v][0:PARTS, :], srow[0:PARTS, bass.ds(t * P, P)], ACT.Copy).then_inc(u3["s_tile"], 1)

                def root(t, v):
                    act.wait_ge(u3["var"], t + 1)
                    act.activation(R3[v], R3[v], ACT.Sqrt).then_inc(u3["rstd"], 1)

                turned(0, 0)
                with act.Fori(0, T // 2 - 1) as i:
                    turned(i * 2 + 1, 1)
                    root(i * 2, 0)
                    turned(i * 2 + 2, 0)
                    root(i * 2 + 1, 1)
                turned(T - 1, 1)
                root(T - 2, 0)
                root(T - 1, 1)

            @block.vector
            def _(dve):
                st = Steps(dve, u3["step"], 0, paced)
                dve.wait_ge(u3["y_in"], 64)
                mean, var = ys[:, :, D:D + 1].rearrange("p t o -> p (t o)"), ys[:, :, D + 1:D + 2].rearrange("p t o -> p (t o)")
                st(dve.tensor_scalar(newt, var, EPS, None, ALU.add))
                st.wait()
                st(dve.reciprocal(rstd, newt))
                dve.memset(onesf, 1.0).then_inc(u3["wsum"], 1)
                dve.wait_ge(u3["sq"], 1)
                st(dve.tensor_tensor(newt, newt, rstd, ALU.mult))
                st.wait()
                st(dve.tensor_tensor(newt, newt, rstd, ALU.mult))
                st.wait()
                st(dve.tensor_scalar(newt, newt, -0.5, 1.5, ALU.mult, ALU.add))
                st.wait()
                st(dve.tensor_tensor(rstd, rstd, newt, ALU.mult))
                st.wait()
                first = ys[:, :, 0:1].rearrange("p t o -> p (t o)")
                st(dve.tensor_tensor(vr, first, mean, ALU.subtract))
                st.wait()
                st(dve.tensor_tensor(vr, vr, rstd, ALU.mult))
                st.wait()
                for part in range(PARTS):
                    st(dve.tensor_copy(vp[:, :, part:part + 1].rearrange("p t o -> p (t o)"), vr))
                    st.wait()
                    if part < PARTS - 1:
                        st(dve.tensor_tensor(vr, vr, vp[:, :, part:part + 1].rearrange("p t o -> p (t o)"), ALU.subtract))
                        st.wait()
                dve.sem_inc(u3["parts"], 1)
                base = st.count
                STEPS_N, STEPS_3 = 1, 7

                def normalize(t, v):
                    y = ys[:, bass.ds(t, 1), 0:D].rearrange("p a n -> p (a n)")
                    dve.tensor_scalar(x3b[v], y, ys[:, bass.ds(t, 1), D:D + 1].rearrange("p a n -> p (a n)"),
                                      rstd[:, bass.ds(t, 1)], ALU.subtract, ALU.mult).then_inc(u3["norm"], 1)

                def finish(t, q, v, first):
                    st = Steps(dve, u3["step"], base + t * STEPS_3, paced)
                    x3, y = x3b[v], outb[v]
                    dve.wait_ge(u3["proj"], t + 1)
                    if not first:
                        dve.wait_ge(u3["out%d" % v], 16 * q)
                    dve.scalar_tensor_tensor(out=y, in0=ps[:, 4 + v, 0:D], scalar=0.0, in1=x3, op0=ALU.max, op1=ALU.add).then_inc(u3["a3"], 1)
                    dve.wait_ge(u3["a3"], t + 1)
                    st(dve.bn_stats(BN3[v], y))
                    st.wait(alone=True)
                    st(dve.bn_aggr(MV3[v], BN3[v]))
                    st.wait()
                    st(dve.tensor_scalar(N3[v], MV3[v][:, 1:2], EPS, None, ALU.add))
                    st.wait()
                    st(dve.reciprocal(R3[v], N3[v]))
                    st.wait()
                    dve.sem_inc(u3["var"], 1)
                    dve.wait_ge(u3["rstd"], t + 1)
                    st(dve.tensor_scalar(N3[v], N3[v], R3[v], R3[v], ALU.mult, ALU.mult))
                    st.wait()
                    st(dve.tensor_scalar(N3[v], N3[v], -0.5, 1.5, ALU.mult, ALU.add))
                    st.wait()
                    st(dve.tensor_tensor(R3[v], R3[v], N3[v], ALU.mult))
                    st.wait()
                    assert st.count == STEPS_3
                    dve.tensor_scalar(y, y, MV3[v][:, 0:1], R3[v], ALU.subtract, ALU.mult).then_inc(u3["out_ready"], 1)

                normalize(0, 0)
                normalize(1, 1)
                finish(0, 0, 0, True)
                normalize(2, 0)
                finish(1, 0, 1, True)
                normalize(3, 1)
                finish(2, 1, 0, False)
                with dve.Fori(2, T // 2) as i:
                    normalize(i * 2, 0)
                    finish(i * 2 - 1, i - 1, 1, False)
                    normalize(i * 2 + 1, 1)
                    finish(i * 2, i, 0, False)
                finish(T - 1, T // 2 - 1, 1, False)


def constants():
    import numpy as np
    f = np.zeros((P, C_F32), np.float32)
    f[:, C_IDENT:C_IDENT + P] = np.eye(P)
    f[:, C_UPPER:C_UPPER + P] = np.triu(np.ones((P, P)), 1)
    j = np.arange(P)
    f[j, C_PACK + j // WORD] = 2.0 ** (j % WORD)
    f[:, C_GROUP:C_GROUP + WORDS] = np.arange(WORDS) * 2.0 ** WORD
    f[:, C_CLASS:C_CLASS + SLOTS] = np.arange(SLOTS, 0, -1)
    f[:, C_LIMIT:C_LIMIT + SLOTS] = [P * sum(c >= k for c in CAPS) for k in range(SLOTS, 0, -1)]
    f[:, C_BIT:C_BIT + WORD] = np.arange(WORD) + 1
    i = np.zeros((P, C_I32), np.int32)
    i[:, C_POW:C_POW + WORD] = 1 << np.arange(WORD)
    i[:, C_OWN:C_OWN + T] = np.arange(T)[None, :] * P + j[:, None]
    return f, i


def layout(x, adj, L0_gnn_W_self, L0_gnn_b_self, L0_gnn_W_nb, L0_gnn_b_nb, L0_gnn_W_comb, L0_gnn_b_comb,
           L1_gnn_WQ, L1_gnn_WK, L1_gnn_WV, L1_gnn_we, L1_gnn_be,
           L2_gnn_Wq, L2_gnn_Wk, L2_gnn_Wv, L2_gnn_Wo, L2_gnn_bo, L3_gnn_w_self, L3_gnn_w_neigh):
    import numpy as np
    c = np.ascontiguousarray
    a = np.asarray
    f, i = constants()
    return {
        "x": c(a(x)),
        "adj_tiles": c(a(adj).reshape(T, P, T, P).transpose(0, 3, 2, 1)).reshape(T, P, T * P),
        "w_selfT0": c(a(L0_gnn_W_self).T), "w_nbT0": c(a(L0_gnn_W_nb).T), "W_comb": c(a(L0_gnn_W_comb)),
        "b_self": c(a(L0_gnn_b_self).reshape(KD, P).T), "b_nb": c(a(L0_gnn_b_nb).reshape(KD, P).T),
        "b_comb": c(a(L0_gnn_b_comb).reshape(1, D)),
        "WQ1T": c(a(L1_gnn_WQ).T), "WK1T": c(a(L1_gnn_WK).T), "WV1T": c(a(L1_gnn_WV).T),
        "we": c(a(L1_gnn_we)), "be": c(a(L1_gnn_be).reshape(1, 1)),
        "WQ2T": c(a(L2_gnn_Wq).T), "WK2T": c(a(L2_gnn_Wk).T), "WV2T": c(a(L2_gnn_Wv).T),
        "WO2T": c(a(L2_gnn_Wo).T), "bo2": c(a(L2_gnn_bo).reshape(1, D)),
        "WS3T": c(a(L3_gnn_w_self).T), "WN3T": c(a(L3_gnn_w_neigh).T),
        "const_f32": f, "const_i32": i,
    }


def kernel(**inputs):
    import concourse.bacc as bacc
    from concourse.bass_utils import run_bass_kernel_spmd

    arrays = {f"in_{k}": v for k, v in layout(**inputs).items()}
    nc = bacc.Bacc("TRN2", target_bir_lowering=False, num_devices=1)
    dram = {k[3:]: nc.dram_tensor(k, v.shape, mybir.dt.from_np(v.dtype), kind="ExternalInput").ap()
            for k, v in arrays.items()}
    out = nc.dram_tensor("out_x", (N, D), F32, kind="ExternalOutput").ap()
    build_program(nc, dram, out)
    return run_bass_kernel_spmd(nc, [arrays], core_ids=[0]).results[0]["out_x"]
```

```python
from contextlib import ExitStack

import concourse.bass as bass
from concourse import mybir
from concourse.alu_op_type import AluOpType as ALU

F32 = mybir.dt.float32
I32 = mybir.dt.int32
BF16 = mybir.dt.bfloat16
FP8 = mybir.dt.float8e4
U8 = mybir.dt.uint8
ACT = mybir.ActivationFunctionType
AX = mybir.AxisListType

P = 128
N = 4096
D = 256
T = N // P
KD = D // P
H = 8
HD = D // H
EPS = 1e-5
SCALE1 = float(HD) ** -0.5
SCALE2 = 1.0 / 16.0
MASKED = -1.0e30

ONE8 = 56.0
WORD = 16
WPC = P // WORD
WORDS = N // WORD
SLOTS = 16
TAB = 40
XP = 3 * D + 2
XM, XL = D + 2, 2 * D + 2

CAPS = [16] + [9] * 2 + [8] * 2 + [7] * 4 + [6] * 4 + [5] * 6 + [4] * 8 + [3] * 5
KV_SLOTS = 9

C_IDENT, C_UPPER, C_PACK, C_GROUP = 0, P, 2 * P, 2 * P + WPC
C_CLASS = C_GROUP + WORDS
C_LIMIT, C_BIT = C_CLASS + SLOTS, C_CLASS + 2 * SLOTS
C_F32 = C_BIT + WORD
C_POW, C_OWN = 0, WORD
C_I32 = WORD + T

STEPS_A = 26


class Steps:

    def __init__(self, eng, sem, done, paced):
        self.eng, self.sem, self.done, self.paced, self.count = eng, sem, done, paced, 0

    def __call__(self, ins):
        ins.then_inc(self.sem, 1)
        self.count += 1
        return ins

    def wait(self, alone=False):
        self.eng.wait_ge(self.sem, self.done + self.count)
        if alone:
            self.eng.sem_inc(self.paced, 1)


def build_program(nc, dram, out):
    with ExitStack() as ctx:
        def sb(name, shape, dt):
            return ctx.enter_context(nc.sbuf_tensor("s_" + name, shape, dt))

        def sem(name):
            return ctx.enter_context(nc.semaphore(name))

        r1 = nc.dram_tensor("row1", [N, 2 * D], F32, kind="Internal").ap()
        kv1 = nc.dram_tensor("kv1", [N, 2 * D], F32, kind="Internal").ap()
        r2 = nc.dram_tensor("row2", [N, 2 * D], F32, kind="Internal").ap()
        kv2 = nc.dram_tensor("kv2", [N, 2 * D], F32, kind="Internal").ap()
        yst = nc.dram_tensor("yst", [N, D + 2], F32, kind="Internal").ap()
        table = nc.dram_tensor("table", [N, TAB], I32, kind="Internal").ap()

        adj8 = sb("adj8", [P, T, T, P], FP8)
        adjbytes = adj8[:, :, :, :].rearrange("p t c i -> p t (c i)").bitcast(U8)
        KEPT = T - 4
        stage = [adj8[:, KEPT + 2 * u:KEPT + 2 * u + 2, :, :].rearrange("p t c i -> p (t c i)").bitcast(BF16)
                 .rearrange("p (c i) -> p c i", i=P) for u in range(2)]
        cf = sb("cf", [P, C_F32], F32)
        ci = sb("ci", [P, C_I32], I32)
        packb = sb("packb", [P, WPC], BF16)
        listf = sb("listf", [P, T, SLOTS], F32)
        degree = sb("degree", [P, T], F32)
        stat = sb("stat", [P, 48], F32)
        REGION = 63616
        region = sb("region", [P, REGION // 4], F32)

        def carve(at, n):
            assert (at + n) <= REGION // 4, (at, n)
            return region[:, at:at + n]

        ident = cf[:, C_IDENT:C_IDENT + P]
        ps = ctx.enter_context(nc.psum_tensor("ps", [P, 8, 512], F32))

        xp = carve(0, T * XP // 2).bitcast(BF16).rearrange("p (c n) -> p c n", n=XP)
        a0 = T * XP // 2
        gword = carve(a0, WORDS // 2).bitcast(BF16)
        a0 += WORDS // 2
        work_at = a0
        xs = [carve(work_at + u * 1024, 1024) for u in range(2)]
        xr = carve(work_at + 2048, 1024)
        xt = [carve(work_at + u * 256, 256) for u in range(2)]
        aggs = carve(work_at + 512, 256)
        axT = carve(work_at + 768, 512)
        x1T = carve(work_at + 1280, 256)
        row1 = carve(work_at + 1536, 512)
        kvr1 = carve(work_at + 2048, 512)
        key = [carve(work_at + 2560 + 256 * k, 256) for k in range(2)]
        REG_A = work_at + 3072
        assert REG_A <= REGION // 4

        weights = sb("weights", [P, 3 * KD * D], F32)
        wqkv = weights[:, :].rearrange("p (k n) -> p k n", k=KD)
        comb = sb("comb", [P, 2 * KD * D], F32)
        wnc = comb[:, 0:KD * D].rearrange("p (k n) -> p k n", k=KD)
        wsc = comb[:, KD * D:].rearrange("p (k n) -> p k n", k=KD)
        biasb = sb("biasb", [P, D], F32)
        raw = carve(T * XP // 2 - 2048 - 260, 2048)
        wsT = raw[:, 0:512].rearrange("p (k n) -> p k n", k=KD)
        wnT = raw[:, 512:1024].rearrange("p (k n) -> p k n", k=KD)
        wc = raw[:, 1024:2048].rearrange("p (k n) -> p k n", k=2 * KD)
        RAW_FREE_CHUNKS = (T * XP // 2 - 2048 - 260) // (4 * XP // 2)
        bcol = sb("bcol", [P, 2 * KD], F32)
        web = sb("web", [P, D], F32)
        beb = sb("beb", [P, 1], F32)

        BANK_A = [ps[:, 0, :], ps[:, 1, :]]
        BANK_W, BANK_T, BANK_X, BANK_O = ps[:, 2, :], ps[:, 3, :], ps[:, 4, :], ps[:, 5, :]
        BANK_K, BANK_QV = ps[:, 6, :], ps[:, 7, :]

        class Sems(dict):

            def __init__(self, stage):
                self.stage = stage

            def __missing__(self, name):
                self[name] = sem(self.stage + "_" + name)
                return self[name]

        s = Sems("a")
        paced = sem("paced")
        adj_in = [s["adj_in0"], s["adj_in1"]]
        xs_in = [s["xs_in0"], s["xs_in1"]]
        xt_in = [s["xt_in0"], s["xt_in1"]]
        XC = 4

        RDEG, BN, MV, RSTD, NEWT, DEG = (stat[:, 0:1], stat[:, 2:8], stat[:, 8:10], stat[:, 10:11], stat[:, 11:12], stat[:, 12:13])
        k16 = stat[:, 16:32]
        n16 = stat[:, 32:48]
        smalli = sb("smalli", [P, 2 * SLOTS], I32)
        kint, kgrp = smalli[:, 0:SLOTS], smalli[:, SLOTS:]
        kgrpf = sb("kgrpf", [P, SLOTS], F32)

        def tiles_of_a(eng, body):
            body(0, 0, 0)
            with eng.Fori(0, T // 2 - 1) as i:
                body(i * 2 + 1, i, 1)
                body(i * 2 + 2, i + 1, 0)
            body(T - 1, T // 2 - 1, 1)

        def load_tail(pool, done):
            for t in range(KEPT, T):
                pool.dma_start(adj8[:, t, :, :].rearrange("p c i -> p (c i)"), dram["adj_tiles"][t]).then_inc(done, 16)

        def rows(ap, t):
            return ap[bass.ds(t * P, P), :]

        with nc.Block() as block:
            @block.gpsimd
            def _(pool):
                def load(t, q, u, kept=True):
                    if not (isinstance(t, int) and t < 2):
                        pool.wait_ge(s["agg_done"], t - 1)
                        if kept:
                            pool.wait_ge(s["kept"], t * 2 - 2)
                    src = dram["adj_tiles"][bass.ds(t, 1)].rearrange("a p n -> (a p) n")
                    pool.dma_start(stage[u].rearrange("p c i -> p (c i)"), src).then_inc(adj_in[u], 16)
                load(0, 0, 0)
                load(1, 0, 1)
                with pool.Fori(1, KEPT // 2 + 1) as i:
                    load(i * 2, i, 0)
                    load(i * 2 + 1, i, 1)
                load(T - 2, T // 2 - 1, 0, False)
                load(T - 1, T // 2 - 1, 1, False)

            @block.sync
            def _(sp):
                sp.dma_start(cf[:, :], dram["const_f32"]).then_inc(s["const_in"], 16)
                sp.dma_start(ci[:, :], dram["const_i32"]).then_inc(s["const_in"], 16)
                sp.dma_start(wsT, dram["w_selfT0"].rearrange("(k p) n -> p k n", p=P)).then_inc(s["raw_in"], 16)
                sp.dma_start(wnT, dram["w_nbT0"].rearrange("(k p) n -> p k n", p=P)).then_inc(s["raw_in"], 16)
                sp.dma_start(wc, dram["W_comb"].rearrange("(k p) n -> p k n", p=P)).then_inc(s["raw_in"], 16)
                sp.dma_start(bcol[:, 0:KD], dram["b_self"]).then_inc(s["raw_in"], 16)
                sp.dma_start(bcol[:, KD:], dram["b_nb"]).then_inc(s["raw_in"], 16)
                for n in range(T // XC):
                    if n >= 2:
                        sp.wait_ge(s["x_r1"], n - 1)
                    src = dram["x"][n * XC * P:(n + 1) * XC * P, :].rearrange("(c p) d -> p c d", p=P)
                    sp.dma_start(xs[n % 2].rearrange("p (c d) -> p c d", d=D), src).then_inc(xs_in[n % 2], 16)
                    if n == 1:
                        sp.dma_start(biasb[:, :], dram["b_comb"].to_broadcast([P, D])).then_inc(s["bias_in"], 16)
                        sp.dma_start(web[:, 0:HD], dram["we"].to_broadcast([P, HD])).then_inc(s["w1_in"], 16)
                        sp.dma_start(beb[:, :], dram["be"].to_broadcast([P, 1])).then_inc(s["w1_in"], 16)
                        for j, name in enumerate(("WK1T", "WQ1T", "WV1T")):
                            sp.dma_start(wqkv[:, :, j * D:(j + 1) * D],
                                         dram[name].rearrange("(k p) n -> p k n", p=P)).then_inc(s["w1_in"], 16)
                sp.wait_ge(s["xp_ready"], T // XC)

                def body(t, q, u):
                    if not (isinstance(t, int) and t == 0):
                        sp.wait_ge(s["x1_ready"], t)
                    sp.dma_start(xt[u], rows(dram["x"], t)).then_inc(xt_in[u], 16)
                    if not (isinstance(t, int) and t == 0):
                        store(t - 1)

                def store(t):
                    sp.wait_ge(s["qv_ready"], t + 1)
                    sp.wait_ge(s["x1_ready"], t + 1)
                    sp.dma_start(rows(r1, t), row1).then_inc(s["row1_out"], 16)
                    sp.wait_ge(s["k_ready"], t + 1)
                    sp.dma_start(rows(kv1, t), kvr1).then_inc(s["kv1_out"], 16)

                tiles_of_a(sp, body)
                store(T - 1)
                sp.wait_ge(s["row1_out"], 16 * T)
                sp.wait_ge(s["kv1_out"], 16 * T)

            @block.tensor
            def _(pe):
                pe.wait_ge(s["raw_in"], 80)
                pe.wait_ge(s["comb_ready"], 1)
                for half, (w, o) in enumerate(((wnT, 1), (wsT, 0))):
                    for k in range(KD):
                        for m in range(KD):
                            mm = pe.matmul(ps[:, half, k * D:(k + 1) * D], w[:, m, k * P:(k + 1) * P],
                                           wc[:, o * KD + m, :], start=(m == 0), stop=(m == KD - 1))
                mm.then_inc(s["comb_done"], 1)
                for m in range(2 * KD):
                    mm = pe.matmul(BANK_W[:, 0:D], xr[:, m * P:(m + 1) * P], wc[:, m, :],
                                   start=(m == 0), stop=(m == 2 * KD - 1))
                mm.then_inc(s["comb_done"], 1)
                pe.wait_ge(s["pack_ready"], 1)
                pe.wait_ge(s["comb_ready"], 4)

                def aggregate(t, q, u, tail):
                    at = {6: turn_ax, 10: layer0, 24: turn_x1, 28: project}
                    pe.wait_ge(adj_in[u], 16 * q + 16)
                    for c in range(T):
                        if isinstance(t, int) and t == 0 and c % XC == 0:
                            pe.wait_ge(s["xp_ready"], c // XC + 1)
                        if tail and c in at:
                            at[c](t - 1, q if u else q - 1, 1 - u)
                        mask = stage[u][:, c, :]
                        for m in range(3):
                            at_x, w = ((0, D + 1), (XM, D), (XL, D))[m]
                            pe.matmul(BANK_A[u][:, 0:w], mask, xp[:, c, at_x:at_x + w],
                                      start=(c == 0 and m == 0), stop=(c == T - 1 and m == 2))
                    if not (isinstance(t, int) and t == 0):
                        pe.wait_ge(s["words_taken"], t)
                    for c in range(T):
                        mask = stage[u][:, c, :]
                        mm = pe.matmul(BANK_W[:, c * WPC:(c + 1) * WPC], mask, packb[:, :], start=True, stop=True)
                    mm.then_inc(s["agg_done"], 1)

                def turn_ax(t, q, u):
                    pe.wait_ge(s["aggs_ready"], t + 1)
                    pe.wait_ge(xt_in[u], 16 * q + 16)
                    for k in range(KD):
                        pe.transpose(BANK_T[:, k * P:(k + 1) * P], aggs[:, k * P:(k + 1) * P], ident)
                    for k in range(KD):
                        mm = pe.transpose(BANK_T[:, (KD + k) * P:(KD + k + 1) * P], xt[u][:, k * P:(k + 1) * P], ident)
                    mm.then_inc(s["ax_turned"], 1)

                def layer0(t, q, u):
                    pe.wait_ge(s["axT_ready"], t + 1)
                    for k in range(2 * KD):
                        w = wnc[:, k, :] if k < KD else wsc[:, k - KD, :]
                        mm = pe.matmul(BANK_O[:, 0:D], axT[:, k * P:(k + 1) * P], w, start=(k == 0), stop=(k == 2 * KD - 1))
                    mm.then_inc(s["o_done"], 1)

                def turn_x1(t, q, u):
                    pe.wait_ge(s["x1_ready"], t + 1)
                    for k in range(KD):
                        mm = pe.transpose(BANK_X[:, k * P:(k + 1) * P], row1[:, k * P:(k + 1) * P], ident)
                    mm.then_inc(s["x1_turned"], 1)

                def project(t, q, u):
                    if isinstance(t, int) and t == 0:
                        pe.wait_ge(s["w1_in"], 80)
                    pe.wait_ge(s["x1T_ready"], t + 1)
                    if not (isinstance(t, int) and t == 0):
                        pe.wait_ge(s["k_ready"], t)
                        pe.wait_ge(s["qv_ready"], t)
                    for k in range(KD):
                        pe.matmul(BANK_K[:, 0:D], x1T[:, k * P:(k + 1) * P], wqkv[:, k, 0:D], start=(k == 0), stop=(k == KD - 1))
                    for k in range(KD):
                        mm = pe.matmul(BANK_QV, x1T[:, k * P:(k + 1) * P], wqkv[:, k, D:3 * D], start=(k == 0), stop=(k == KD - 1))
                    mm.then_inc(s["qkv_done"], 1)

                aggregate(0, 0, 0, False)
                with pe.Fori(0, T // 2 - 1) as i:
                    aggregate(i * 2 + 1, i, 1, True)
                    aggregate(i * 2 + 2, i + 1, 0, True)
                aggregate(T - 1, T // 2 - 1, 1, True)
                for step in (turn_ax, layer0, turn_x1, project):
                    step(T - 1, T // 2 - 1, 1)

            @block.scalar
            def _(act):
                act.wait_ge(s["comb_done"], 1)
                act.activation(comb[:, :], ps[:, 0:2, :].rearrange("p a n -> p (a n)"), ACT.Copy).then_inc(s["comb_ready"], 1)
                for n in range(T // XC):
                    if n == RAW_FREE_CHUNKS:
                        act.wait_ge(s["comb_done"], 2)
                    if n == 0:
                        act.wait_ge(s["comb_ready"], 3)
                    view = xp[:, n * XC:(n + 1) * XC, :]
                    act.wait_ge(xs_in[n % 2], 16 * (n // 2 + 1))
                    act.activation(view[:, :, 0:D], xs[n % 2].rearrange("p (c d) -> p c d", d=D), ACT.Copy).then_inc(s["x_high"], 1)
                    act.wait_ge(s["x_r1"], n + 1)
                    act.activation(view[:, :, XM:XM + D], xr.rearrange("p (c d) -> p c d", d=D), ACT.Copy).then_inc(s["x_mid"], 1)

                def keep(t, q, u, half):
                    w = T * P // 2
                    act.wait_ge(adj_in[u], 16 * q + 16)
                    act.activation(adjbytes[:, bass.ds(t, 1), half * w:half * w + w].rearrange("p a n -> p (a n)"),
                                   stage[u].rearrange("p c i -> p (c i)")[:, half * w:half * w + w], ACT.Copy,
                                   scale=ONE8).then_inc(s["kept"], 1)

                def body(t, q, u, kept):
                    first = isinstance(t, int) and t == 0
                    act.wait_ge(s["rdeg_ready"], t + 1)
                    act.activation(aggs, BANK_A[u][:, 0:D], ACT.Copy, scale=RDEG).then_inc(s["aggs_ready"], 1)
                    act.wait_ge(s["ax_turned"], t + 1)
                    act.activation(axT, BANK_T, ACT.Copy).then_inc(s["axT_ready"], 1)
                    if kept:
                        keep(t + 1, q + u, 1 - u, 0)
                    act.wait_ge(s["var_ready"], t + 1)
                    act.activation(RSTD, RSTD, ACT.Sqrt).then_inc(s["rstd_ready"], 1)
                    act.wait_ge(s["x1_turned"], t + 1)
                    act.activation(x1T, BANK_X[:, 0:D], ACT.Copy).then_inc(s["x1T_ready"], 1)
                    if kept:
                        keep(t + 1, q + u, 1 - u, 1)
                    act.wait_ge(s["qkv_done"], t + 1)
                    if not first:
                        act.wait_ge(s["row1_out"], 16 * t)
                        act.wait_ge(s["kv1_out"], 16 * t)
                    act.activation(row1[:, D:2 * D], BANK_QV[:, 0:D], ACT.Copy)
                    act.activation(kvr1[:, D:2 * D], BANK_QV[:, D:2 * D], ACT.Copy).then_inc(s["qv_ready"], 1)

                act.wait_ge(s["xp_ready"], T // XC)
                keep(0, 0, 0, 0)
                keep(0, 0, 0, 1)
                body(0, 0, 0, True)
                with act.Fori(0, KEPT // 2 - 1) as i:
                    body(i * 2 + 1, i, 1, True)
                    body(i * 2 + 2, i + 1, 0, True)
                with act.Fori(KEPT // 2 - 1, T // 2 - 1) as i:
                    body(i * 2 + 1, i, 1, False)
                    body(i * 2 + 2, i + 1, 0, False)
                body(T - 1, T // 2 - 1, 1, False)

            @block.vector
            def _(dve):
                st = Steps(dve, s["dve_step"], 0, paced)
                dve.wait_ge(s["const_in"], 32)
                st(dve.tensor_copy(packb[:, :], cf[:, C_PACK:C_PACK + WPC]))
                st(dve.tensor_copy(gword, cf[:, C_GROUP:C_GROUP + WORDS]))
                dve.wait_ge(s["raw_in"], 80)
                for m in range(2 * KD):
                    ins = dve.tensor_copy(xr[:, m * P:(m + 1) * P], bcol[:, m:m + 1].to_broadcast([P, P]))
                    st(ins)
                st.wait()
                dve.sem_inc(s["pack_ready"], 1)
                dve.sem_inc(s["comb_ready"], 1)
                dve.wait_ge(s["w1_in"], 80)
                for h in range(1, H):
                    st(dve.tensor_copy(web[:, h * HD:(h + 1) * HD], web[:, 0:HD]))
                dve.wait_ge(s["comb_done"], 2)
                dve.wait_ge(s["bias_in"], 16)
                st(dve.tensor_tensor(biasb[:, :], BANK_W[:, 0:D], biasb[:, :], ALU.add))
                st(dve.memset(xp[:, 0:RAW_FREE_CHUNKS * XC, D:D + 2], 1.0))
                st(dve.memset(xp[:, RAW_FREE_CHUNKS * XC:T, D:D + 2], 1.0))
                st.wait()
                dve.sem_inc(s["comb_ready"], 2)
                for n in range(T // XC):
                    view = xp[:, n * XC:(n + 1) * XC, :]
                    r = xr.rearrange("p (c d) -> p c d", d=D)
                    dve.wait_ge(s["x_high"], n + 1)
                    dve.tensor_tensor(r, xs[n % 2].rearrange("p (c d) -> p c d", d=D), view[:, :, 0:D], ALU.subtract).then_inc(s["x_r1"], 1)
                    dve.wait_ge(s["x_mid"], n + 1)
                    dve.tensor_tensor(view[:, :, XL:XL + D], r, view[:, :, XM:XM + D], ALU.subtract).then_inc(s["xp_ready"], 1)
                    dve.wait_ge(s["xp_ready"], n + 1)
                base = st.count

                def body(t, q, u):
                    first = isinstance(t, int) and t == 0
                    st = Steps(dve, s["dve_step"], base + t * STEPS_A, paced)
                    dve.wait_ge(s["agg_done"], t + 1)
                    st(dve.tensor_copy(DEG, BANK_A[u][:, D:D + 1]))
                    st.wait()
                    st(dve.tensor_copy(degree[:, bass.ds(t, 1)], DEG))
                    st(dve.tensor_scalar(RDEG, DEG, 1.0, None, ALU.max))
                    st.wait()
                    dve.reciprocal(RDEG, RDEG).then_inc(s["rdeg_ready"], 1)
                    st(dve.scalar_tensor_tensor(out=key[0], in0=BANK_W[:, 0:WORDS], scalar=0.0, in1=gword, op0=ALU.is_gt, op1=ALU.mult))
                    st.wait()
                    st(dve.tensor_tensor(key[0], BANK_W[:, 0:WORDS], key[0], ALU.add))
                    st.wait()
                    dve.sem_inc(s["words_taken"], 1)
                    top16(st, k16, key[0], key[1])
                    dve.wait_ge(s["o_done"], t + 1)
                    if not first:
                        dve.wait_ge(s["row1_out"], 16 * t)
                    y = row1[:, 0:D]
                    st(dve.tensor_tensor(y, BANK_O[:, 0:D], biasb[:, :], ALU.add))
                    st.wait()
                    dve.wait_ge(xt_in[u], 16 * q + 16)
                    st(dve.scalar_tensor_tensor(out=y, in0=y, scalar=0.0, in1=xt[u], op0=ALU.max, op1=ALU.add))
                    st.wait()
                    layernorm(st, y, s["var_ready"], s["rstd_ready"], t)
                    dve.tensor_scalar(y, y, MV[:, 0:1], RSTD, ALU.subtract, ALU.mult).then_inc(s["x1_ready"], 1)
                    st(dve.tensor_copy(kint, k16))
                    st.wait()
                    st(dve.tensor_scalar(kgrp, kint, WORD, 4, ALU.logical_shift_right, ALU.logical_shift_left))
                    cand = key[0].bitcast(I32).rearrange("p (s b) -> p s b", b=WORD)
                    node = key[1].rearrange("p (s b) -> p s b", b=WORD)
                    st(dve.tensor_tensor(cand, kint.rearrange("p (s o) -> p s o", o=1).to_broadcast([P, SLOTS, WORD]),
                                         ci[:, C_POW:C_POW + WORD].rearrange("p (o b) -> p o b", o=1).to_broadcast([P, SLOTS, WORD]),
                                         ALU.bitwise_and))
                    st.wait()
                    st(dve.tensor_copy(kgrpf[:, :], kgrp))
                    st.wait()
                    st(dve.tensor_tensor(node, kgrpf[:, :].rearrange("p (s o) -> p s o", o=1).to_broadcast([P, SLOTS, WORD]),
                                         cf[:, C_BIT:C_BIT + WORD].rearrange("p (o b) -> p o b", o=1).to_broadcast([P, SLOTS, WORD]), ALU.add))
                    st.wait()
                    st(dve.scalar_tensor_tensor(out=key[1], in0=key[0].bitcast(I32), scalar=0.0, in1=key[1],
                                                op0=ALU.is_gt, op1=ALU.mult))
                    st.wait()
                    top16(st, n16, key[1], key[0])
                    st(dve.tensor_copy(listf[:, bass.ds(t, 1), :].rearrange("p a k -> p (a k)"), n16))
                    dve.wait_ge(s["qkv_done"], t + 1)
                    if not first:
                        dve.wait_ge(s["kv1_out"], 16 * t)
                    dve.scalar_tensor_tensor(out=kvr1[:, 0:D], in0=BANK_K[:, 0:D], scalar=SCALE1, in1=web[:, :],
                                             op0=ALU.mult, op1=ALU.add).then_inc(s["k_ready"], 1)
                    assert st.count == STEPS_A, st.count

                def top16(st, out16, values, spare):
                    st.wait(alone=True)
                    st(dve.max(out16[:, 0:8], values))
                    st.wait(alone=True)
                    st(dve.match_replace(spare, out16[:, 0:8], values, 0.0))
                    st.wait(alone=True)
                    st(dve.max(out16[:, 8:16], spare))
                    st.wait()

                def layernorm(st, y, var_ready, rstd_ready, t):
                    st(dve.bn_stats(BN, y))
                    st.wait(alone=True)
                    st(dve.bn_aggr(MV, BN))
                    st.wait()
                    st(dve.tensor_scalar(NEWT, MV[:, 1:2], EPS, None, ALU.add))
                    st.wait()
                    dve.reciprocal(RSTD, NEWT).then_inc(var_ready, 1)
                    dve.wait_ge(rstd_ready, t + 1)
                    st(dve.tensor_scalar(NEWT, NEWT, RSTD, RSTD, ALU.mult, ALU.mult))
                    st.wait()
                    st(dve.tensor_scalar(NEWT, NEWT, -0.5, 1.5, ALU.mult, ALU.add))
                    st.wait()
                    st(dve.tensor_tensor(RSTD, RSTD, NEWT, ALU.mult))
                    st.wait()

                tiles_of_a(dve, body)


        tabw = carve(14400, (T + 1) * TAB).bitcast(I32).rearrange("p (t n) -> p t n", n=TAB)
        cls = carve(0, 256).bitcast(BF16)
        cls3 = cls.rearrange("p (c t) -> p c t", t=T)
        upperb = carve(256, P // 2).bitcast(BF16)
        onesb = carve(320, P // 2).bitcast(BF16)
        tot, incl, posw, zero = (carve(512 * k + 512, 512) for k in range(4))
        lst = listf[:, :, :].rearrange("p t k -> p (t k)")
        over = carve(2560, SLOTS + 1)
        mid = carve(2600, T * SLOTS)
        rank = sb("rank", [P, T], I32)
        flag = sb("flag", [P, 1], I32)
        s_cls, s_rank, s_rstep = sem("classes_ready"), sem("ranks_counted"), sem("rank_step")

        with nc.Block() as block:
            @block.vector
            def _(dve):
                st = Steps(dve, s_rstep, 0, paced)
                st(dve.tensor_tensor(cls3, degree[:, :].rearrange("p (o t) -> p o t", o=1).to_broadcast([P, SLOTS, T]),
                                     cf[:, C_CLASS:C_CLASS + SLOTS].rearrange("p (c o) -> p c o", o=1).to_broadcast([P, SLOTS, T]),
                                     ALU.is_equal))
                st(dve.tensor_copy(upperb, cf[:, C_UPPER:C_UPPER + P]))
                st(dve.memset(onesb, 1.0))
                st.wait()
                dve.sem_inc(s_cls, 1)
                st(dve.memset(zero, 0.0))
                st(dve.memset(tabw.rearrange("p t n -> p (t n)"), 0))
                st(dve.tensor_scalar(mid, lst, 0.0, 2.0 ** 20, ALU.is_equal, ALU.mult))
                st.wait()
                list3, mid3 = listf[:, :, :], mid.rearrange("p (t k) -> p t k", k=SLOTS)
                st(dve.scalar_tensor_tensor(out=tabw[:, 0:T, 0:SLOTS], in0=list3, scalar=-1.0, in1=mid3, op0=ALU.add, op1=ALU.add))
                st(dve.tensor_scalar(tabw[:, 0:T, SLOTS:2 * SLOTS].bitcast(F32), list3, 0.0, MASKED, ALU.is_equal, ALU.mult))
                st(dve.tensor_copy(tabw[:, 0:T, 2 * SLOTS:2 * SLOTS + 1], ci[:, C_OWN:C_OWN + T].rearrange("p (t o) -> p t o", o=1)))
                dve.wait_ge(s_rank, 1)
                st(dve.tensor_copy(tot, ps[:, 1, :]))
                st.wait()
                st(dve.tensor_tensor_scan(incl, tot, zero, 0.0, ALU.add, ALU.add))
                st.wait()
                st(dve.tensor_tensor(posw, incl, tot, ALU.subtract))
                st(dve.tensor_tensor(over[:, 0:SLOTS], incl.rearrange("p (c t) -> p c t", t=T)[:, :, T - 1],
                                     cf[:, C_LIMIT:C_LIMIT + SLOTS], ALU.subtract))
                st(dve.tensor_scalar(over[:, SLOTS:SLOTS + 1], incl[:, 511:512], -1.0, float(N), ALU.mult, ALU.add))
                st.wait()
                st(dve.tensor_tensor(posw, posw, ps[:, 0, :], ALU.add))
                st(dve.tensor_reduce(stat[:, 0:1], over, AX.X, ALU.max))
                st.wait()
                st(dve.tensor_scalar(flag[:, :], stat[:, 0:1], 0.0, None, ALU.is_gt))
                st(dve.tensor_tensor(posw, posw, cls, ALU.mult))
                st.wait()
                st(dve.tensor_reduce(mid[:, 0:T], posw.rearrange("p (c t) -> p t c", t=T), AX.X, ALU.add))
                st.wait()
                st(dve.tensor_copy(rank[:, :], mid[:, 0:T]))
                st.wait()

            @block.tensor
            def _(pe):
                pe.wait_ge(s_cls, 1)
                pe.matmul(ps[:, 0, :], upperb, cls, start=True, stop=True)
                pe.matmul(ps[:, 1, :], onesb, cls, start=True, stop=True).then_inc(s_rank, 1)

        rowo = [carve(11520 + 512 * k, 512) for k in range(2)]
        kvo = [carve(12544 + 512 * k, 512) for k in range(2)]
        turnT = carve(13568, 256)
        biaso = biasb[:, :]
        stat2 = sb("stat2", [P, 64], F32)
        l_BN, l_MV = stat2[:, 0:6], stat2[:, 6:8]
        l_R, l_N = stat2[:, 8:9], stat2[:, 9:10]
        l_max, l_cmax = stat2[:, 16:24], stat2[:, 24:32]
        l_sum, l_csum, l_nmax = stat2[:, 32:33], stat2[:, 33:34], stat2[:, 34:35]

        d_own = carve(0, 512)
        d_kv = carve(512, 512)
        d_qT, d_kT = carve(1024, 256), carve(1280, 256)
        d_neg = carve(1536, P)
        d_score = carve(1664, H * P)
        d_prob = carve(2688, H * P)
        d_probT = carve(3712, H * P)
        d_acc = carve(4736, D)
        identb = carve(4992, P // 2).bitcast(BF16)
        d_mask = carve(5056, P // 2).bitcast(BF16)

        layer_sems = {1: Sems("l1"), 2: Sems("l2")}

        def dense_layer(block_no, heads, src_row, src_kv, w_names):
            L = layer_sems[block_no]
            hardmax = heads > 1
            width = heads * P
            wide = [ps[:, 2 + k, :] for k in range(4)] if hardmax else [ps[:, 2, 0:P]]
            widep = [ps[:, 2, :], ps[:, 3, :]] if hardmax else [ps[:, 2, 0:P]]
            score, prob, probT = d_score[:, 0:width], d_prob[:, 0:width], d_probT[:, 0:width]

            def sync(sp):
                for j, name in enumerate(w_names):
                    sp.dma_start(wqkv[:, :, j * D:(j + 1) * D], dram[name].rearrange("(k p) n -> p k n", p=P)).then_inc(L["w_in"], 16)
                if not hardmax:
                    sp.dma_start(biaso, dram["bo2"].to_broadcast([P, D])).then_inc(L["w_in"], 16)
                with sp.Fori(0, T) as t:
                    sp.wait_ge(L["free"], t * (2 * T + 1) + 1)
                    sp.dma_start(d_own, rows(src_row, t)).then_inc(L["own_in"], 16)
                    with sp.Fori(0, 2 * T) as c:
                        sp.wait_ge(L["free"], t * (2 * T + 1) + c + 1)
                        chunk = c % T
                        sp.dma_start(d_kv, src_kv[bass.ds(chunk * P, P), :]).then_inc(L["kv_in"], 16)
                    sp.wait_ge(L["x_ready"], t + 1)
                    if hardmax:
                        sp.wait_ge(L["rowq"], t + 1)
                        sp.dma_start(rows(r2, t), rowo[0]).then_inc(L["row_out"], 16)
                        sp.dma_start(rows(kv2, t), kvo[0]).then_inc(L["row_out"], 16)
                        sp.wait_ge(L["row_out"], t * 32 + 32)
                        sp.sem_inc(paced, 1)
                    else:
                        sp.dma_start(rows(yst, t), rowo[0][:, 0:D + 2]).then_inc(L["row_out"], 16)
                        sp.wait_ge(L["row_out"], t * 16 + 16)
                        sp.sem_inc(paced, 1)

            def tensor(pe):
                pe.wait_ge(L["w_in"], 48 if hardmax else 32)
                pe.wait_ge(L["identb"], 1)
                with pe.Fori(0, T) as t:
                    pe.wait_ge(L["own_in"], t * 16 + 16)
                    for k in range(KD):
                        mm = pe.transpose(ps[:, 0, k * P:(k + 1) * P], d_own[:, D + k * P:D + (k + 1) * P], ident)
                    mm.then_inc(L["turned_q"], 1)
                    pe.wait_ge(L["qT"], t + 1)
                    pe.sem_inc(paced, 1)

                    def scores(t, c, n):
                        pe.wait_ge(L["kv_in"], n * 16 + 16)
                        for k in range(KD):
                            pe.transpose(ps[:, 0, k * P:(k + 1) * P], d_kv[:, k * P:(k + 1) * P], ident)
                        pe.wait_ge(L["mask"], n + 1)
                        pe.matmul(ps[:, 1, 0:P], d_mask, identb, start=True, stop=True).then_inc(L["turned"], 1)
                        pe.wait_ge(L["kT"], n + 1)
                        for h in range(heads):
                            if hardmax:
                                at = HD * (h % 4)
                                k = h // 4
                                mm = pe.matmul(wide[h % 4][:, k * P:(k + 1) * P], d_qT[at:at + HD, k * P:(k + 1) * P],
                                               d_kT[at:at + HD, k * P:(k + 1) * P], start=True, stop=True)
                            else:
                                for k in range(KD):
                                    mm = pe.matmul(wide[0], d_qT[:, k * P:(k + 1) * P], d_kT[:, k * P:(k + 1) * P],
                                                   start=(k == 0), stop=(k == KD - 1))
                        mm.then_inc(L["scored"], 1)

                    with pe.Fori(0, T) as c:
                        scores(t, c, t * (2 * T) + c)
                    with pe.Fori(0, T) as c:
                        scores(t, c, t * (2 * T) + c + T)
                        pe.wait_ge(L["prob"], t * T + c + 1)
                        for h in range(heads):
                            mm = pe.transpose(widep[h // 4][:, (h % 4) * P:(h % 4 + 1) * P], prob[:, h * P:(h + 1) * P], ident)
                        mm.then_inc(L["turned_p"], 1)
                        pe.wait_ge(L["probT"], t * T + c + 1)
                        w = D // heads
                        for h in range(heads):
                            mm = pe.matmul(ps[:, 6, h * w:(h + 1) * w], probT[:, h * P:(h + 1) * P], d_kv[:, D + h * w:D + (h + 1) * w],
                                           start=True, stop=True)
                        mm.then_inc(L["pv"], 1)
                    pe.wait_ge(L["normed"], t + 1)
                    src = rowo[0][:, 0:D] if hardmax else d_acc
                    for k in range(KD):
                        mm = pe.transpose(ps[:, 0, k * P:(k + 1) * P], src[:, k * P:(k + 1) * P], ident)
                    mm.then_inc(L["y_turned"], 1)
                    pe.wait_ge(L["yT"], t + 1)
                    for k in range(KD):
                        if hardmax:
                            pe.matmul(ps[:, 2, :], turnT[:, k * P:(k + 1) * P], wqkv[:, k, 0:2 * D], start=(k == 0), stop=(k == KD - 1))
                        else:
                            mm = pe.matmul(ps[:, 2, 0:D], turnT[:, k * P:(k + 1) * P], wqkv[:, k, 0:D], start=(k == 0), stop=(k == KD - 1))
                    if hardmax:
                        for k in range(KD):
                            mm = pe.matmul(ps[:, 3, 0:D], turnT[:, k * P:(k + 1) * P], wqkv[:, k, 2 * D:3 * D], start=(k == 0), stop=(k == KD - 1))
                    mm.then_inc(L["proj"], 1)

            def scalar(act):
                def mask(t, c, step):
                    act.wait_ge(L["free"], t * (2 * T + 1) + step + 1)
                    src = adjbytes[:, bass.ds(t, 1), bass.ds(c * P, P)].rearrange("p a i -> p (a i)")
                    act.activation(d_mask, src, ACT.Copy, scale=1.0 / ONE8).then_inc(L["mask"], 1)

                if hardmax:
                    act.wait_ge(L["tail_in"], 64)
                with act.Fori(0, T) as t:
                    act.wait_ge(L["turned_q"], t + 1)
                    act.activation(d_qT, ps[:, 0, 0:D], ACT.Copy).then_inc(L["qT"], 1)
                    with act.Fori(0, T) as c:
                        mask(t, c, c)
                        act.wait_ge(L["turned"], t * (2 * T) + c + 1)
                        act.activation(d_kT, ps[:, 0, 0:D], ACT.Copy).then_inc(L["kT"], 1)
                    with act.Fori(0, T) as c:
                        mask(t, c, c + T)
                        act.wait_ge(L["turned"], t * (2 * T) + c + T + 1)
                        act.activation(d_kT, ps[:, 0, 0:D], ACT.Copy).then_inc(L["kT"], 1)
                        if not hardmax:
                            act.wait_ge(L["nmax"], t * T + c + 1)
                            act.activation(prob, score, ACT.Exp, bias=l_nmax, scale=SCALE2, accum_out=l_csum).then_inc(L["prob"], 1)
                        act.wait_ge(L["turned_p"], t * T + c + 1)
                        src = ps[:, 2:4, :].rearrange("p a n -> p (a n)") if hardmax else widep[0]
                        act.activation(probT, src, ACT.Copy).then_inc(L["probT"], 1)
                    if hardmax:
                        act.wait_ge(L["var"], t + 1)
                        act.activation(l_R, l_R, ACT.Sqrt).then_inc(L["rstd"], 1)
                    act.wait_ge(L["y_turned"], t + 1)
                    act.activation(turnT, ps[:, 0, 0:D], ACT.Copy).then_inc(L["yT"], 1)
                    if hardmax:
                        act.wait_ge(L["proj"], t + 1)
                        act.activation(kvo[0], ps[:, 2, :], ACT.Copy).then_inc(L["kvrow"], 1)
                        act.wait_ge(L["kvrow"], t + 1)
                        act.activation(rowo[0][:, D:2 * D], ps[:, 3, 0:D], ACT.Copy).then_inc(L["rowq"], 1)

            def vector(dve):
                FRONT, ONE, TWO, END = 2, 5 if hardmax else 4, 5 if hardmax else 6, 8 if hardmax else 6
                per = FRONT + T * (ONE + TWO) + END
                st = Steps(dve, L["step"], 0, paced)
                st(dve.tensor_copy(identb, ident))
                st.wait()
                dve.sem_inc(L["identb"], 1)
                dve.sem_inc(L["free"], 1)
                base = 1

                def masked(st, n):
                    dve.wait_ge(L["turned"], n + 1)
                    st(dve.tensor_scalar(d_neg, ps[:, 1, 0:P], -MASKED, MASKED, ALU.mult, ALU.add))
                    st.wait()
                    if hardmax:
                        st(dve.tensor_scalar(d_neg, d_neg, beb[:, 0:1], None, ALU.add))
                        st.wait()
                    dve.wait_ge(L["scored"], n + 1)
                    if hardmax:
                        st(dve.tensor_tensor(score.rearrange("p (k a n) -> p a k n", k=KD, n=P),
                                             ps[:, 2:6, 0:KD * P].rearrange("p a (k n) -> p a k n", n=P),
                                             d_neg.rearrange("p (b o n) -> p b o n", o=1, b=1).to_broadcast([P, 4, KD, P]), ALU.add))
                    else:
                        st(dve.tensor_tensor(score, wide[0], d_neg, ALU.add))
                    st.wait()

                with dve.Fori(0, T) as t:
                    tb = base + t * per
                    st = Steps(dve, L["step"], tb, paced)
                    st(dve.memset(l_max[:, 0:heads], -3.0e38))
                    st(dve.memset(d_acc, 0.0))
                    st.wait(alone=True)
                    with dve.Fori(0, T) as c:
                        st = Steps(dve, L["step"], tb + c * ONE + FRONT, paced)
                        masked(st, t * (2 * T) + c)
                        st(dve.tensor_reduce(l_cmax[:, 0:heads], score.rearrange("p (h n) -> p h n", n=P), AX.X, ALU.max))
                        st.wait()
                        st(dve.tensor_tensor(l_max[:, 0:heads], l_max[:, 0:heads], l_cmax[:, 0:heads], ALU.max))
                        st.wait()
                        dve.sem_inc(L["free"], 1)
                        assert st.count == ONE, st.count
                    if not hardmax:
                        dve.memset(l_sum, 0.0).then_inc(L["var"], 1)
                        dve.wait_ge(L["var"], t + 1)
                        dve.sem_inc(paced, 1)
                    with dve.Fori(0, T) as c:
                        st = Steps(dve, L["step"], tb + c * TWO + (FRONT + T * ONE), paced)
                        masked(st, t * (2 * T) + c + T)
                        if hardmax:
                            st(dve.tensor_tensor(prob.rearrange("p (h n) -> p h n", n=P), score.rearrange("p (h n) -> p h n", n=P),
                                                 l_max.rearrange("p (h o) -> p h o", o=1).to_broadcast([P, heads, P]), ALU.is_equal))
                            st.wait()
                            dve.sem_inc(L["prob"], 1)
                        else:
                            st(dve.tensor_scalar(l_nmax, l_max[:, 0:1], -SCALE2, None, ALU.mult))
                            st.wait()
                            dve.sem_inc(L["nmax"], 1)
                            dve.wait_ge(L["prob"], t * T + c + 1)
                            st(dve.tensor_tensor(l_sum, l_sum, l_csum, ALU.add))
                            st.wait()
                        dve.wait_ge(L["pv"], t * T + c + 1)
                        st(dve.tensor_tensor(d_acc, d_acc, ps[:, 6, 0:D], ALU.add))
                        st.wait()
                        if not hardmax:
                            st(dve.memset(l_cmax[:, 0:1], 0.0))
                            st.wait()
                        dve.sem_inc(L["free"], 1)
                        assert st.count == TWO, st.count
                    st = Steps(dve, L["step"], tb + (FRONT + T * (ONE + TWO)), paced)
                    if hardmax:
                        y = rowo[0][:, 0:D]
                        st(dve.scalar_tensor_tensor(out=y, in0=d_acc, scalar=1.0 / H, in1=d_own[:, 0:D], op0=ALU.mult, op1=ALU.add))
                        st.wait()
                        statistics(dve, st, y, L["var"])
                        newton(dve, st, L["rstd"], t)
                        st(dve.tensor_scalar(y, y, l_MV[:, 0:1], l_R, ALU.subtract, ALU.mult))
                        st.wait()
                        dve.sem_inc(L["normed"], 1)
                        dve.wait_ge(L["rowq"], t + 1)
                        dve.sem_inc(L["x_ready"], 1)
                    else:
                        st(dve.reciprocal(l_sum, l_sum))
                        st.wait()
                        st(dve.tensor_scalar(d_acc, d_acc, l_sum, None, ALU.mult))
                        st.wait()
                        dve.sem_inc(L["normed"], 1)
                        dve.wait_ge(L["w_in"], 32)
                        y = rowo[0][:, 0:D]
                        st(dve.tensor_tensor(y, d_own[:, 0:D], biaso, ALU.add))
                        st.wait()
                        dve.wait_ge(L["proj"], t + 1)
                        st(dve.tensor_tensor(y, y, ps[:, 2, 0:D], ALU.add))
                        st.wait()
                        st(dve.bn_stats(l_BN, y))
                        st.wait(alone=True)
                        st(dve.bn_aggr(rowo[0][:, D:D + 2], l_BN))
                        st.wait()
                        dve.sem_inc(L["x_ready"], 1)
                    dve.wait_ge(L["row_out"], t * (32 if hardmax else 16) + (32 if hardmax else 16))
                    dve.sem_inc(L["free"], 1)
                    assert st.count == END, st.count

            return sync, tensor, scalar, vector

        def statistics(dve, st, y, var_ready):
            st(dve.bn_stats(l_BN, y))
            st.wait(alone=True)
            st(dve.bn_aggr(l_MV, l_BN))
            st.wait()
            st(dve.tensor_scalar(l_N, l_MV[:, 1:2], EPS, None, ALU.add))
            st.wait()
            dve.reciprocal(l_R, l_N).then_inc(var_ready, 1)

        def newton(dve, st, rstd_ready, t):
            dve.wait_ge(rstd_ready, t + 1)
            st(dve.tensor_scalar(l_N, l_N, l_R, l_R, ALU.mult, ALU.mult))
            st.wait()
            st(dve.tensor_scalar(l_N, l_N, -0.5, 1.5, ALU.mult, ALU.add))
            st.wait()
            st(dve.tensor_tensor(l_R, l_R, l_N, ALU.mult))
            st.wait()

        dense = [dense_layer(1, H, r1, kv1, ("WK2T", "WV2T", "WQ2T")), dense_layer(2, 1, r2, kv2, ("WO2T",))]
        kvbuf = carve(0, 2 * KV_SLOTS * 2 * D).rearrange("p (s n) -> p s n", n=2 * D)
        more = (adj8[:, KEPT:T, :, :].rearrange("p t c i -> p (t c i)").bitcast(F32).rearrange("p (s n) -> p s n", n=2 * D))
        prod = carve(9216, KV_SLOTS * D)
        g_own = [comb[:, 512 * k:512 * k + 512] for k in range(2)]
        xb = [carve(12544 + 256 * k, 256) for k in range(2)]
        attn = carve(13056, 256)
        logit = carve(13824, SLOTS * H)
        picked = carve(13952, SLOTS * H)
        negb = carve(14080, SLOTS)
        prob2 = [carve(14096 + SLOTS * k, SLOTS) for k in range(2)]
        s_idx = [carve(14128 + 20 * k, SLOTS + 1).bitcast(I32) for k in range(2)]
        sid = sb("sid", [P, 2], I32)
        s_sum = stat2[:, 36:38]
        s_inv = stat2[:, 38:39]
        RUNS = []
        for t in range(1, T - 1, 2):
            c = CAPS[t]
            assert CAPS[t + 1] <= c <= KV_SLOTS
            if RUNS and RUNS[-1][2] == c:
                RUNS[-1][1] += 2
            else:
                RUNS.append([t, 2, c])

        def ranked_tiles(eng, body):
            body(0, 0, 0, CAPS[0], 0, 0)
            before = [CAPS[0], 0]
            for first, count, slots in RUNS:
                q = (first - 1) // 2
                if count == 2:
                    body(first, q, 1, slots, before[1], before[1] - q)
                    body(first + 1, q + 1, 0, slots, before[0], before[0] - (q + 1))
                else:
                    with eng.Fori(0, count // 2) as i:
                        body(i * 2 + first, i + q, 1, slots, i * slots + before[1], i * (slots - 1) + (before[1] - q))
                        body(i * 2 + (first + 1), i + (q + 1), 0, slots, i * slots + before[0],
                             i * (slots - 1) + (before[0] - (q + 1)))
                before = [b + count // 2 * slots for b in before]
            body(T - 1, T // 2 - 1, 1, CAPS[T - 1], before[1], before[1] - (T // 2 - 1))

        def pieces(u, slots):
            near = min(slots, KV_SLOTS)
            out = [(0, kvbuf[:, KV_SLOTS * u:KV_SLOTS * u + near, :])]
            if slots > near:
                out.append((near, more[:, 0:slots - near, :]))
            return out

        def slot(u, k):
            return kvbuf[:, KV_SLOTS * u + k, :] if k < KV_SLOTS else more[:, k - KV_SLOTS, :]

        def products(rows_, slots):
            return prod.rearrange("p (s n) -> p s n", n=D)[:, 0:slots, :] if slots <= KV_SLOTS else rows_[:, :, 0:D]

        def below(t, k):
            return isinstance(t, int) and t < k

        def back(t, q, u, k):
            if k % 2 == 0:
                return t - k, q - k // 2, u
            return t - k, (q - (k - 1) // 2 if u else q - (k + 1) // 2), 1 - u

        def sparse_layer(layer):
            S = layer_sems[layer]
            one = layer == 1
            src_kv = kv1 if one else kv2

            def sync(sp):
                names = ("WK2T", "WV2T", "WQ2T") if one else ("WO2T",)
                for j, name in enumerate(names):
                    sp.dma_start(wqkv[:, :, j * D:(j + 1) * D], dram[name].rearrange("(k p) n -> p k n", p=P)).then_inc(S["w_in"], 16)
                if one:
                    sp.wait_ge(S["table_out"], 16 * T)
                    sp.dma_start(tabw[:, 0:T, :], table.rearrange("(t p) n -> p t n", p=P)).then_inc(S["tab_in"], 16)

                    def store(t, q, u):
                        sp.wait_ge(S["x_ready"], t + 1)
                        sp.wait_ge(S["rowq"], t + 1)
                        sp.dma_start(rows(r2, t), rowo[u]).then_inc(S["row_out%d" % u], 16)

                    with sp.Fori(0, T // 2) as i:
                        store(i * 2, i, 0)
                        store(i * 2 + 1, i, 1)
                    sp.wait_ge(S["row_out0"], 16 * T // 2)
                    sp.wait_ge(S["row_out1"], 16 * T // 2)
                else:
                    sp.dma_start(biaso, dram["bo2"].to_broadcast([P, D])).then_inc(S["w_in"], 16)

                    def load(t, q, u):
                        if not below(t, 2):
                            sp.wait_ge(S["own_free"], t - 1)
                        sp.dma_start(g_own[u], rows(r2, t)).then_inc(S["own_in%d" % u], 16)

                    load(0, 0, 0)
                    load(1, 0, 1)
                    with sp.Fori(1, T // 2) as i:
                        load(i * 2, i, 0)
                        load(i * 2 + 1, i, 1)

            def gpsimd(pool):
                if one:
                    for t in range(T):
                        pool.indirect_dma_start(
                            out=table, out_offset=bass.IndirectOffsetOnAxis(ap=rank[:, t:t + 1], axis=0),
                            in_=tabw[:, t, :], in_offset=None).then_inc(S["table_out"], 16)
                    pool.wait_ge(S["mem"], 1)

                def gather(out_ap, src, idx, s_in, skip):
                    pool.indirect_dma_start(out=out_ap, out_offset=None, in_=src,
                                            in_offset=bass.IndirectOffsetOnAxis(ap=idx, axis=0),
                                            bounds_check=N - 1, oob_is_err=not skip).then_inc(s_in, 16)

                def scatter(t, q, u):
                    pool.wait_ge(S["kvrow"] if one else S["x_ready"], t + 1)
                    pool.wait_ge(S["sid_ready"], t + 1)
                    pool.sem_inc(paced, 1)
                    src, dst = (kvo[u], kv2) if one else (rowo[u][:, 0:D + 2], yst)
                    pool.indirect_dma_start(out=dst, out_offset=bass.IndirectOffsetOnAxis(ap=sid[:, u:u + 1], axis=0),
                                            in_=src, in_offset=None).then_inc(S["kv_out%d" % u], 16)

                late = 3

                def body(t, q, u, slots, g, others):
                    pool.wait_ge(S["idx_ready"], t + 1)
                    pool.sem_inc(paced, 1)
                    for k in range(slots):
                        if not below(t, 2) and k % 2 == 0:
                            if k + 2 < slots:
                                pool.wait_ge(S["slots_summed%d" % u], others + (k + 3 - slots))
                            else:
                                pool.wait_ge(S["summed"], t - 1)
                            pool.sem_inc(paced, 1)
                        gather(slot(u, k), src_kv, s_idx[u][:, k:k + 1], S["kv_in%d" % u], True)
                    if one:
                        if not below(t, 2):
                            pool.wait_ge(S["y_done"], t - 1)
                            pool.sem_inc(paced, 1)
                        gather(g_own[u], r1, s_idx[u][:, SLOTS:SLOTS + 1], S["own_in%d" % u], False)
                    if not below(t, late):
                        scatter(*back(t, q, u, late))

                ranked_tiles(pool, body)
                for k in range(late - 1, -1, -1):
                    scatter(*back(T - 1, T // 2 - 1, 1, k))
                pool.wait_ge(S["kv_out0"], 16 * T // 2)
                pool.wait_ge(S["kv_out1"], 16 * T // 2)

            def tensor(pe):
                pe.wait_ge(S["w_in"], 48 if one else 32)

                def total(t, q, u, slots, g):
                    if one:
                        pe.wait_ge(S["v_ready"], t + 1)
                    if not below(t, 2):
                        pe.wait_ge(S["y_done"], t - 1)
                    for k in range(slots):
                        if not one:
                            pe.wait_ge(S["weighed%d" % u], g + k + 1)
                        done = S["summed"] if k == slots - 1 else S["slots_summed%d" % u]
                        pe.matmul(ps[:, 6 + u, 0:D], ident, slot(u, k)[:, D:2 * D], start=(k == 0), stop=(k == slots - 1)).then_inc(done, 1)

                def project(t, q, u):
                    pe.wait_ge(S["x_ready"] if one else S["attn"], t + 1)
                    src = rowo[u][:, 0:D] if one else attn
                    for k in range(KD):
                        mm = pe.transpose(ps[:, 0, k * P:(k + 1) * P], src[:, k * P:(k + 1) * P], ident)
                    mm.then_inc(S["turned"], 1)
                    pe.wait_ge(S["turn_out"], t + 1)
                    if one:
                        if not below(t, 1):
                            pe.wait_ge(S["kvrow"], t)
                            pe.wait_ge(S["rowq"], t)
                        for k in range(KD):
                            pe.matmul(ps[:, 2, :], turnT[:, k * P:(k + 1) * P], wqkv[:, k, 0:2 * D], start=(k == 0), stop=(k == KD - 1))
                        for k in range(KD):
                            mm = pe.matmul(ps[:, 3, 0:D], turnT[:, k * P:(k + 1) * P], wqkv[:, k, 2 * D:3 * D], start=(k == 0), stop=(k == KD - 1))
                    else:
                        if not below(t, 1):
                            pe.wait_ge(S["x_ready"], t)
                        for k in range(KD):
                            mm = pe.matmul(ps[:, 2, 0:D], turnT[:, k * P:(k + 1) * P], wqkv[:, k, 0:D], start=(k == 0), stop=(k == KD - 1))
                    mm.then_inc(S["proj"], 1)

                def body(t, q, u, slots, g, others):
                    total(t, q, u, slots, g)
                    if not below(t, 1):
                        project(*back(t, q, u, 1))

                ranked_tiles(pe, body)
                project(T - 1, T // 2 - 1, 1)

            def scalar(act):
                def project(t, q, u):
                    if one:
                        act.wait_ge(S["var"], t + 1)
                        act.activation(l_R, l_R, ACT.Sqrt).then_inc(S["rstd"], 1)
                    act.wait_ge(S["turned"], t + 1)
                    act.activation(turnT, ps[:, 0, 0:D], ACT.Copy).then_inc(S["turn_out"], 1)
                    if one:
                        act.wait_ge(S["proj"], t + 1)
                        if not below(t, 2):
                            act.wait_ge(S["kv_out%d" % u], 16 * q)
                            act.wait_ge(S["row_out%d" % u], 16 * q)
                        act.activation(kvo[u], ps[:, 2, :], ACT.Copy).then_inc(S["kvrow"], 1)
                        act.activation(rowo[u][:, D:2 * D], ps[:, 3, 0:D], ACT.Copy).then_inc(S["rowq"], 1)

                def body(t, q, u, slots, g, others):
                    if not one:
                        act.wait_ge(S["nmax"], t + 1)
                        act.activation(prob2[u][:, 0:slots], logit[:, 0:slots], ACT.Exp, bias=l_nmax, scale=SCALE2,
                                       accum_out=s_sum[:, u:u + 1]).then_inc(S["prob"], 1)
                        act.wait_ge(S["prob"], t + 1)
                        for k in range(slots):
                            v = slot(u, k)[:, D:2 * D]
                            act.activation(v, v, ACT.Copy, scale=prob2[u][:, k:k + 1]).then_inc(S["weighed%d" % u], 1)
                    if not below(t, 1):
                        project(*back(t, q, u, 1))

                ranked_tiles(act, body)
                project(T - 1, T // 2 - 1, 1)

            def vector(dve):
                FRONT = 7 if one else 5
                BACK = 6 if one else 7
                heads = H if one else 1

                def index(t, u):
                    src = tabw[:, bass.ds(t, 1), :].rearrange("p a n -> p (a n)")
                    dve.tensor_copy(s_idx[u][:, 0:SLOTS], src[:, 0:SLOTS]).then_inc(S["front"], 1)
                    dve.tensor_copy(s_idx[u][:, SLOTS:SLOTS + 1], src[:, 2 * SLOTS:2 * SLOTS + 1]).then_inc(S["front"], 1)

                if one:
                    dve.memset(kvbuf.rearrange("p s n -> p (s n)"), 0.0)
                    dve.memset(more.rearrange("p s n -> p (s n)"), 0.0).then_inc(S["mem"], 1)
                    dve.wait_ge(S["tab_in"], 16)
                index(0, 0)
                index(1, 1)
                dve.wait_ge(S["front"], 4)
                dve.sem_inc(S["idx_ready"], 2)
                base = 4
                if not one:
                    dve.wait_ge(S["w_in"], 32)

                def product(t, q, u, slots, g):
                    st = Steps(dve, S["front"], t * FRONT + base, paced)
                    dve.wait_ge(S["kv_in%d" % u], g * 16 + 16 * slots)
                    dve.wait_ge(S["own_in%d" % u], 16 * q + 16)
                    if not one and not below(t, 1):
                        dve.wait_ge(S["prob"], t)
                    q_row = g_own[u][:, D:2 * D]
                    for at, kv in pieces(u, slots):
                        out, n = products(kv, slots), min(slots - at, KV_SLOTS)
                        if one:
                            qv = q_row.rearrange("p (o n) -> p o n", o=1).to_broadcast([P, n, D])
                            ins = dve.tensor_tensor(out, kv[:, :, 0:D], qv, ALU.mult)
                        else:
                            for k in range(n):
                                ins = dve.tensor_tensor_reduce(out[:, k, :], kv[:, k, 0:D], q_row, 1.0, 0.0,
                                                               ALU.mult, ALU.add, logit[:, at + k:at + k + 1])
                    st(ins)
                    index(min(t + 2, T) if isinstance(t, int) else t + 2, u)
                    st.count += 2
                    st.wait()
                    dve.sem_inc(S["idx_ready"], 1)
                    if one:
                        st(dve.tensor_scalar(negb[:, 0:slots], neg_of(t, slots), beb[:, 0:1], None, ALU.add))
                        return st.count
                    st(dve.tensor_tensor(logit[:, 0:slots], logit[:, 0:slots], neg_of(t, slots), ALU.add))
                    st.wait()
                    st(dve.tensor_reduce(l_max[:, 0:1], logit[:, 0:slots], AX.X, ALU.max))
                    st.wait()
                    dve.tensor_scalar(l_nmax, l_max[:, 0:1], -SCALE2, None, ALU.mult).then_inc(S["nmax"], 1)
                    return st.count

                def neg_of(t, slots):
                    return tabw[:, bass.ds(t, 1), SLOTS:SLOTS + slots].bitcast(F32).rearrange("p a n -> p (a n)")

                def weigh(t, q, u, slots, done):
                    if one:
                        st = Steps(dve, S["front"], t * FRONT + (base + done), paced)
                        lg = logit[:, 0:slots * H].rearrange("p (s h) -> p s h", h=H)
                        pk = picked[:, 0:slots * H].rearrange("p (s h) -> p s h", h=H)
                        for at, kv in pieces(u, slots):
                            out, n = products(kv, slots), min(slots - at, KV_SLOTS)
                            ins = dve.tensor_reduce(lg[:, at:at + n, :], out.rearrange("p s (h n) -> p s h n", n=HD), AX.X, ALU.add)
                        st(ins)
                        st.wait()
                        st(dve.tensor_tensor(lg, lg, negb[:, 0:slots].rearrange("p (s o) -> p s o", o=1).to_broadcast([P, slots, H]), ALU.add))
                        st.wait()
                        st(dve.tensor_reduce(l_max, lg.rearrange("p s h -> p h s"), AX.X, ALU.max))
                        st.wait()
                        weight_step(dve, pk, lg, slots).then_inc(S["prob"], 1)
                        dve.wait_ge(S["prob"], t + 1)
                        for at, kv in pieces(u, slots):
                            n = min(slots - at, KV_SLOTS)
                            v = kv[:, :, D:2 * D].rearrange("p s (h n) -> p s h n", n=HD)
                            w = pk[:, at:at + n, :].rearrange("p s (h o) -> p s h o", o=1).to_broadcast([P, n, H, HD])
                            ins = dve.tensor_tensor(v, v, w, ALU.mult)
                        ins.then_inc(S["v_ready"], 1)
                        assert done + st.count == FRONT, (done, st.count)
                    else:
                        dve.tensor_tensor(xb[u], g_own[u][:, 0:D], biaso, ALU.add).then_inc(S["own_free"], 1)

                def weight_step(dve, pk, lg, slots):
                    return dve.tensor_tensor(pk, lg, l_max.rearrange("p (o h) -> p o h", o=1).to_broadcast([P, slots, H]), ALU.is_equal)

                def name(t, q, u):
                    if not below(t, 2):
                        dve.wait_ge(S["kv_out%d" % u], 16 * q)
                    dve.tensor_copy(sid[:, u:u + 1], tabw[:, bass.ds(t, 1), 2 * SLOTS:2 * SLOTS + 1].rearrange("p a n -> p (a n)")).then_inc(S["sid_ready"], 1)

                def residual(t, q, u):
                    st = Steps(dve, S["back"], t * BACK, paced)
                    y = rowo[u][:, 0:D]
                    name(t, q, u)
                    dve.wait_ge(S["summed"], t + 1)
                    if not below(t, 2):
                        dve.wait_ge(S["row_out%d" % u], 16 * q)
                    dve.scalar_tensor_tensor(out=y, in0=ps[:, 6 + u, 0:D], scalar=1.0 / H, in1=g_own[u][:, 0:D],
                                             op0=ALU.mult, op1=ALU.add).then_inc(S["y_done"], 1)
                    dve.wait_ge(S["y_done"], t + 1)
                    statistics(dve, st, y, S["var"])
                    assert st.count == 3

                def normalize(t, q, u):
                    st = Steps(dve, S["back"], t * BACK + 3, paced)
                    y = rowo[u][:, 0:D]
                    newton(dve, st, S["rstd"], t)
                    dve.tensor_scalar(y, y, l_MV[:, 0:1], l_R, ALU.subtract, ALU.mult).then_inc(S["x_ready"], 1)
                    assert st.count == BACK - 3

                def finish(t, q, u):
                    st = Steps(dve, S["back"], t * 2, paced)
                    name(t, q, u)
                    y = rowo[u][:, 0:D]
                    dve.wait_ge(S["proj"], t + 1)
                    dve.wait_ge(S["own_free"], t + 1)
                    st(dve.tensor_tensor(y, ps[:, 2, 0:D], xb[u], ALU.add))
                    st.wait()
                    st(dve.bn_stats(l_BN, y))
                    st.wait(alone=True)
                    dve.bn_aggr(rowo[u][:, D:D + 2], l_BN).then_inc(S["x_ready"], 1)

                def divide(t, q, u):
                    dve.reciprocal(s_inv, s_sum[:, u:u + 1]).then_inc(S["mem"], 1)
                    dve.wait_ge(S["mem"], t + 1)
                    dve.wait_ge(S["summed"], t + 1)
                    dve.tensor_scalar(attn, ps[:, 6 + u, 0:D], s_inv, None, ALU.mult).then_inc(S["attn"], 1)
                    dve.wait_ge(S["attn"], t + 1)
                    dve.sem_inc(S["y_done"], 1)

                def body(t, q, u, slots, g, others):
                    done = product(t, q, u, slots, g)
                    if one:
                        if not below(t, 1):
                            residual(*back(t, q, u, 1))
                        weigh(t, q, u, slots, done)
                        if not below(t, 1):
                            normalize(*back(t, q, u, 1))
                    else:
                        assert done == FRONT
                        if not below(t, 2):
                            finish(*back(t, q, u, 2))
                        if not below(t, 1):
                            divide(*back(t, q, u, 1))
                        weigh(t, q, u, slots, done)

                ranked_tiles(dve, body)
                last = (T - 1, T // 2 - 1, 1)
                if one:
                    residual(*last)
                    normalize(*last)
                else:
                    finish(*back(*last, 1))
                    divide(*last)
                    finish(*last)

            return sync, tensor, scalar, vector, gpsimd

        sparse = [sparse_layer(1), sparse_layer(2)]
        for n in range(2):
            ways = (sparse[n], dense[n])

            def either(eng, k):
                overflow = eng.value_load(flag[0:1, 0:1], min_val=0, max_val=1)
                with eng.If(overflow == 0):
                    ways[0][k](eng)
                with eng.Else():
                    ways[1][k](eng)

            with nc.Block() as block:
                @block.gpsimd
                def _(pool):
                    overflow = pool.value_load(flag[0:1, 0:1], min_val=0, max_val=1)
                    with pool.If(overflow == 0):
                        ways[0][4](pool)
                    with pool.Else():
                        if n == 0:
                            load_tail(pool, layer_sems[1]["tail_in"])
                            pool.wait_ge(layer_sems[1]["tail_in"], 64)

                @block.sync
                def _(sp):
                    either(sp, 0)

                @block.tensor
                def _(pe):
                    either(pe, 1)

                @block.scalar
                def _(act):
                    either(act, 2)

                @block.vector
                def _(dve):
                    either(dve, 3)
        PARTS = 3
        GROUP = 4
        BATCH = 8
        ys = carve(0, T * (D + 2)).rearrange("p (t n) -> p t n", n=D + 2)
        b3 = T * (D + 2)
        rstd = carve(b3, T)
        newt = carve(b3 + T, T)
        vr = carve(b3 + 2 * T, T)
        vp = carve(b3 + 3 * T, T * 4 // 2).bitcast(BF16).rearrange("p (t n) -> p t n", n=4)
        b3 += 3 * T + T * 2
        x3T = [carve(b3 + 256 * k, 256) for k in range(2)]
        X3B = 4
        x3b = [carve(b3 + 512 + 256 * k, 256) for k in range(X3B)]
        term = carve(b3 + 512 + 256 * X3B, 256)
        b3 += 768 + 256 * X3B
        srow = carve(b3, N)
        b3 += N
        wsumb = carve(b3, 256)
        s_col = carve(b3 + 256, T)
        nmean = carve(b3 + 256 + T, T)
        mv3, w3, r3 = carve(b3 + 512, 2 * BATCH), carve(b3 + 544, BATCH), carve(b3 + 560, BATCH)
        rt3, nm3 = carve(b3 + 576, T), carve(b3 + 576 + T, T)
        onesf = carve(b3 + 576 + 2 * T, P)
        w3s = weights[:, 0:KD * D].rearrange("p (k n) -> p k n", k=KD)
        w3n = weights[:, KD * D:2 * KD * D].rearrange("p (k n) -> p k n", k=KD)
        BN3 = [stat[:, 0:6], stat[:, 6:12]]
        u3 = Sems("l3")

        def of_batch(ap, b):
            return ap[:, bass.ds(b * BATCH, BATCH)]

        with nc.Block() as block:
            @block.gpsimd
            def _(pool):
                load_tail(pool, u3["tail_in"])

            @block.sync
            def _(sp):
                src = yst.rearrange("(t p) n -> p t n", p=P)
                for k in range(4):
                    sp.dma_start(ys[:, 8 * k:8 * k + 8, :], src[:, 8 * k:8 * k + 8, :]).then_inc(u3["y_in"], 16)
                sp.dma_start(w3n, dram["WN3T"].rearrange("(k p) n -> p k n", p=P)).then_inc(u3["w_in"], 16)
                sp.dma_start(w3s, dram["WS3T"].rearrange("(k p) n -> p k n", p=P)).then_inc(u3["w_in"], 16)
                with sp.Fori(0, T // 2) as i:
                    sp.wait_ge(u3["out_ready"], i * 2 + 2)
                    dst = out[bass.ds(i * (2 * P), 2 * P), :].rearrange("(a p) n -> p a n", p=P)
                    sp.dma_start(dst, ys[:, bass.ds(i * 2, 2), 0:D]).then_inc(u3["out"], 16)
                sp.wait_ge(u3["out"], 16 * T // 2)

            @block.tensor
            def _(pe):
                pe.wait_ge(u3["w_in"], 32)
                pe.wait_ge(u3["wsum"], 1)
                for k in range(KD):
                    mm = pe.matmul(ps[:, 0, 0:D], onesf, w3n[:, k, :], start=(k == 0), stop=(k == KD - 1))
                mm.then_inc(u3["wsum_out"], 1)
                pe.wait_ge(u3["parts"], 1)
                pe.wait_ge(u3["wsum"], 2)

                for g in range(T // GROUP):
                    if g == KEPT // GROUP:
                        pe.wait_ge(u3["tail_in"], 64)
                    for c in range(T):
                        mask = adj8[:, g * GROUP:(g + 1) * GROUP, c, :]
                        mm = pe.matmul(ps[0:PARTS, g, :], vp[:, c, 0:PARTS], mask, start=(c == 0), stop=(c == T - 1))
                    mm.then_inc(u3["s_done"], 1)
                pe.wait_ge(u3["s_out"], T // GROUP)
                for t in range(T):
                    mm = pe.matmul(ps[:, 0, t:t + 1], srow[0:PARTS, t * P:(t + 1) * P], onesf[0:PARTS, 0:1], start=True, stop=True)
                mm.then_inc(u3["s_col"], 1)

                def turn(t, v, b):
                    pe.wait_ge(u3["norm"], t + 1)
                    for k in range(KD):
                        mm = pe.transpose(ps[:, 2 + v, k * P:(k + 1) * P], x3b[b][:, k * P:(k + 1) * P], ident)
                    mm.then_inc(u3["turned"], 1)

                def project(t, v):
                    pe.wait_ge(u3["x3T"], t + 1)
                    if not (isinstance(t, int) and t < 2):
                        pe.wait_ge(u3["combined"], t - 1)
                    bank = ps[:, 4 + v, 0:D]
                    for k in range(KD):
                        mm = pe.matmul(bank, x3T[v][:, k * P:(k + 1) * P], w3s[:, k, :], start=(k == 0), stop=(k == KD - 1))
                    mm.then_inc(u3["proj"], 1)

                turn(0, 0, 0)
                for j in range(X3B):
                    turn(j + 1, (j + 1) % 2, (j + 1) % X3B)
                    project(j, j % 2)
                with pe.Fori(1, T // X3B - 1) as i:
                    for j in range(X3B):
                        turn(i * X3B + (j + 1), (j + 1) % 2, (j + 1) % X3B)
                        project(i * X3B + j, j % 2)
                for j in range(X3B):
                    if j < X3B - 1:
                        turn(T - X3B + j + 1, (j + 1) % 2, (j + 1) % X3B)
                    project(T - X3B + j, j % 2)

            @block.scalar
            def _(act):
                act.wait_ge(u3["step"], 2)
                act.activation(rstd, rstd, ACT.Sqrt).then_inc(u3["sq"], 1)
                act.wait_ge(u3["wsum_out"], 1)
                act.activation(wsumb, ps[:, 0, 0:D], ACT.Copy).then_inc(u3["wsum"], 1)
                act.wait_ge(u3["parts"], 2)

                def normalize(t, b):
                    y = ys[:, bass.ds(t, 1), 0:D].rearrange("p a n -> p (a n)")
                    if not (isinstance(t, int) and t < X3B):
                        act.wait_ge(u3["combined"], t - (X3B - 1))
                    act.activation(x3b[b], y, ACT.Identity, bias=nmean[:, bass.ds(t, 1)], scale=rstd[:, bass.ds(t, 1)]).then_inc(u3["norm"], 1)

                for t in range(X3B):
                    normalize(t, t)
                for g in range(T // GROUP):
                    act.wait_ge(u3["s_done"], g + 1)
                    act.activation(srow[0:PARTS, g * GROUP * P:(g + 1) * GROUP * P], ps[0:PARTS, g, :], ACT.Copy).then_inc(u3["s_out"], 1)
                act.wait_ge(u3["s_col"], 1)
                act.activation(s_col, ps[:, 0, 0:T], ACT.Copy).then_inc(u3["s_col"], 1)

                def scale(t):
                    y = ys[:, bass.ds(t, 1), 0:D].rearrange("p a n -> p (a n)")
                    act.activation(y, y, ACT.Identity, bias=nm3[:, bass.ds(t, 1)], scale=rt3[:, bass.ds(t, 1)]).then_inc(u3["out_ready"], 1)

                def body(t, j, v):
                    act.wait_ge(u3["turned"], t + 1)
                    act.activation(x3T[v], ps[:, 2 + v, 0:D], ACT.Copy).then_inc(u3["x3T"], 1)

                def root(b):
                    act.wait_ge(u3["var"], b + 1)
                    act.activation(r3, r3, ACT.Sqrt).then_inc(u3["root"], 1)

                def batch(b):
                    for j in range(BATCH):
                        t = b * BATCH + j
                        body(t, j, j % 2)
                        if not (isinstance(t, int) and (t == 0 or t - 1 + X3B >= T)):
                            normalize(t - 1 + X3B, (j - 1) % X3B)
                        if j == 1 and not (isinstance(b, int) and b == 0):
                            act.wait_ge(u3["scaled"], b)
                        if j >= 1 and not (isinstance(b, int) and b == 0):
                            scale((b - 1) * BATCH + j - 1)
                    if not (isinstance(b, int) and b == 0):
                        scale((b - 1) * BATCH + BATCH - 1)
                    root(b)

                batch(0)
                with act.Fori(1, T // BATCH - 1) as b:
                    batch(b)
                batch(T // BATCH - 1)
                act.wait_ge(u3["scaled"], T // BATCH)
                for j in range(BATCH):
                    scale(T - BATCH + j)

            @block.vector
            def _(dve):
                st = Steps(dve, u3["step"], 0, paced)
                dve.memset(onesf, 1.0).then_inc(u3["wsum"], 1)
                dve.wait_ge(u3["y_in"], 64)
                mean, var = ys[:, :, D:D + 1].rearrange("p t o -> p (t o)"), ys[:, :, D + 1:D + 2].rearrange("p t o -> p (t o)")
                st(dve.tensor_scalar(newt, var, EPS, None, ALU.add))
                st.wait()
                st(dve.reciprocal(rstd, newt))
                dve.wait_ge(u3["sq"], 1)
                st(dve.tensor_tensor(newt, newt, rstd, ALU.mult))
                st.wait()
                st(dve.tensor_tensor(newt, newt, rstd, ALU.mult))
                st.wait()
                st(dve.tensor_scalar(newt, newt, -0.5, 1.5, ALU.mult, ALU.add))
                st.wait()
                st(dve.tensor_tensor(rstd, rstd, newt, ALU.mult))
                st.wait()
                first = ys[:, :, 0:1].rearrange("p t o -> p (t o)")
                st(dve.tensor_tensor(vr, first, mean, ALU.subtract))
                st.wait()
                st(dve.tensor_tensor(vr, vr, rstd, ALU.mult))
                st.wait()
                for part in range(PARTS):
                    st(dve.tensor_copy(vp[:, :, part:part + 1].rearrange("p t o -> p (t o)"), vr))
                    st.wait()
                    if part < PARTS - 1:
                        st(dve.tensor_tensor(vr, vr, vp[:, :, part:part + 1].rearrange("p t o -> p (t o)"), ALU.subtract))
                        st.wait()
                dve.sem_inc(u3["parts"], 1)
                st(dve.scalar_tensor_tensor(out=nmean, in0=mean, scalar=-1.0, in1=rstd, op0=ALU.mult, op1=ALU.mult))
                st.wait()
                dve.sem_inc(u3["parts"], 1)
                dve.wait_ge(u3["wsum"], 2)
                dve.wait_ge(u3["s_col"], 2)

                def combine(t, v, b):
                    y = ys[:, bass.ds(t, 1), 0:D].rearrange("p a n -> p (a n)")
                    dve.wait_ge(u3["proj"], t + 1)
                    dve.scalar_tensor_tensor(out=term, in0=wsumb, scalar=s_col[:, bass.ds(t, 1)], in1=ps[:, 4 + v, 0:D],
                                             op0=ALU.mult, op1=ALU.add).then_inc(u3["termed"], 1)
                    dve.wait_ge(u3["termed"], t + 1)
                    dve.wait_ge(u3["norm"], t + 1)
                    dve.scalar_tensor_tensor(out=y, in0=term, scalar=0.0, in1=x3b[b], op0=ALU.max, op1=ALU.add).then_inc(u3["combined"], 1)
                    dve.wait_ge(u3["combined"], t + 1)
                    dve.sem_inc(paced, 1)
                    dve.bn_stats(BN3[v], y).then_inc(u3["stats"], 1)

                def aggregate(t, j, v):
                    dve.wait_ge(u3["stats"], t + 1)
                    dve.sem_inc(paced, 1)
                    dve.bn_aggr(mv3[:, 2 * j:2 * j + 2], BN3[v]).then_inc(u3["norm_out"], 1)

                def batch(b):
                    for j in range(BATCH):
                        t = b * BATCH + j
                        combine(t, j % 2, j % X3B)
                        aggregate(t, j, j % 2)
                    st = Steps(dve, u3["batch"], b * 8, paced)
                    mv = mv3.rearrange("p (t n) -> p t n", n=2)
                    m, va = (mv[:, :, n:n + 1].rearrange("p t o -> p (t o)") for n in range(2))
                    r, w, rt, nm = r3, w3, of_batch(rt3, b), of_batch(nm3, b)
                    dve.wait_ge(u3["norm_out"], b * BATCH + BATCH)
                    st(dve.tensor_scalar(w, va, EPS, None, ALU.add))
                    st.wait()
                    dve.reciprocal(r, w).then_inc(u3["var"], 1)
                    dve.wait_ge(u3["root"], b + 1)
                    st(dve.tensor_tensor(w, w, r, ALU.mult))
                    st.wait()
                    st(dve.tensor_tensor(w, w, r, ALU.mult))
                    st.wait()
                    st(dve.tensor_scalar(w, w, -0.5, 1.5, ALU.mult, ALU.add))
                    st.wait()
                    st(dve.tensor_scalar(w, w, -1.0, None, ALU.mult))
                    st.wait()
                    st(dve.scalar_tensor_tensor(out=rt, in0=w, scalar=-1.0, in1=r, op0=ALU.mult, op1=ALU.mult))
                    st(dve.tensor_tensor(w, w, r, ALU.mult))
                    st.wait()
                    st(dve.tensor_tensor(nm, m, w, ALU.mult))
                    st.wait()
                    dve.sem_inc(u3["scaled"], 1)
                    assert st.count == 8, st.count

                with dve.Fori(0, T // BATCH) as b:
                    batch(b)


def constants():
    import numpy as np
    f = np.zeros((P, C_F32), np.float32)
    f[:, C_IDENT:C_IDENT + P] = np.eye(P)
    f[:, C_UPPER:C_UPPER + P] = np.triu(np.ones((P, P)), 1)
    j = np.arange(P)
    f[j, C_PACK + j // WORD] = 2.0 ** (j % WORD)
    f[:, C_GROUP:C_GROUP + WORDS] = np.arange(WORDS) * 2.0 ** WORD
    f[:, C_CLASS:C_CLASS + SLOTS] = np.arange(SLOTS, 0, -1)
    f[:, C_LIMIT:C_LIMIT + SLOTS] = [P * sum(c >= k for c in CAPS) for k in range(SLOTS, 0, -1)]
    f[:, C_BIT:C_BIT + WORD] = np.arange(WORD) + 1
    i = np.zeros((P, C_I32), np.int32)
    i[:, C_POW:C_POW + WORD] = 1 << np.arange(WORD)
    i[:, C_OWN:C_OWN + T] = np.arange(T)[None, :] * P + j[:, None]
    return f, i


def layout(x, adj, L0_gnn_W_self, L0_gnn_b_self, L0_gnn_W_nb, L0_gnn_b_nb, L0_gnn_W_comb, L0_gnn_b_comb,
           L1_gnn_WQ, L1_gnn_WK, L1_gnn_WV, L1_gnn_we, L1_gnn_be,
           L2_gnn_Wq, L2_gnn_Wk, L2_gnn_Wv, L2_gnn_Wo, L2_gnn_bo, L3_gnn_w_self, L3_gnn_w_neigh):
    import numpy as np
    c = np.ascontiguousarray
    a = np.asarray
    f, i = constants()
    return {
        "x": c(a(x)),
        "adj_tiles": c(a(adj).reshape(T, P, T, P).transpose(0, 3, 2, 1)).reshape(T, P, T * P),
        "w_selfT0": c(a(L0_gnn_W_self).T), "w_nbT0": c(a(L0_gnn_W_nb).T), "W_comb": c(a(L0_gnn_W_comb)),
        "b_self": c(a(L0_gnn_b_self).reshape(KD, P).T), "b_nb": c(a(L0_gnn_b_nb).reshape(KD, P).T),
        "b_comb": c(a(L0_gnn_b_comb).reshape(1, D)),
        "WQ1T": c(a(L1_gnn_WQ).T), "WK1T": c(a(L1_gnn_WK).T), "WV1T": c(a(L1_gnn_WV).T),
        "we": c(a(L1_gnn_we)), "be": c(a(L1_gnn_be).reshape(1, 1)),
        "WQ2T": c(a(L2_gnn_Wq).T), "WK2T": c(a(L2_gnn_Wk).T), "WV2T": c(a(L2_gnn_Wv).T),
        "WO2T": c(a(L2_gnn_Wo).T), "bo2": c(a(L2_gnn_bo).reshape(1, D)),
        "WS3T": c(a(L3_gnn_w_self).T), "WN3T": c(a(L3_gnn_w_neigh).T),
        "const_f32": f, "const_i32": i,
    }


def kernel(**inputs):
    import concourse.bacc as bacc
    from concourse.bass_utils import run_bass_kernel_spmd

    arrays = {f"in_{k}": v for k, v in layout(**inputs).items()}
    nc = bacc.Bacc("TRN2", target_bir_lowering=False, num_devices=1)
    dram = {k[3:]: nc.dram_tensor(k, v.shape, mybir.dt.from_np(v.dtype), kind="ExternalInput").ap()
            for k, v in arrays.items()}
    out = nc.dram_tensor("out_x", (N, D), F32, kind="ExternalOutput").ap()
    build_program(nc, dram, out)
    return run_bass_kernel_spmd(nc, [arrays], core_ids=[0]).results[0]["out_x"]
```

```python
from contextlib import ExitStack

import concourse.bass as bass
from concourse import mybir
from concourse.alu_op_type import AluOpType as ALU

F32 = mybir.dt.float32
I32 = mybir.dt.int32
BF16 = mybir.dt.bfloat16
F16 = mybir.dt.float16
FP8 = mybir.dt.float8e4
U8 = mybir.dt.uint8
ACT = mybir.ActivationFunctionType
AX = mybir.AxisListType

P = 128
N = 4096
D = 256
T = N // P
KD = D // P
H = 8
HD = D // H
EPS = 1e-5
SCALE1 = float(HD) ** -0.5
SCALE2 = 1.0 / 16.0
MASKED = -1.0e30

ONE8 = 56.0
WORD = 16
WPC = P // WORD
WORDS = N // WORD
SLOTS = 16
TAB = 40
WC = WPC + 1

TOP = 14
LOW = 2.0 ** 11
EXPONENT = 0x7F800000

CAPS = [16] + [9] * 2 + [8] * 2 + [7] * 4 + [6] * 4 + [5] * 6 + [4] * 8 + [3] * 5
KV_SLOTS = 9

C_IDENT, C_UPPER, C_PACK, C_GROUP = 0, P, 2 * P, 2 * P + WC
C_CLASS = C_GROUP + WORDS
C_LIMIT, C_BIT = C_CLASS + SLOTS, C_CLASS + 2 * SLOTS
C_F32 = C_BIT + WORD
C_POW, C_OWN = 0, WORD
C_I32 = WORD + T

STEPS_A = 28
STEPS_LISTS = 20


class Steps:

    def __init__(self, eng, sem, done, paced):
        self.eng, self.sem, self.done, self.paced, self.count = eng, sem, done, paced, 0

    def __call__(self, ins):
        ins.then_inc(self.sem, 1)
        self.count += 1
        return ins

    def wait(self, alone=False):
        self.eng.wait_ge(self.sem, self.done + self.count)
        if alone:
            self.eng.sem_inc(self.paced, 1)


def build_program(nc, dram, out):
    with ExitStack() as ctx:
        def sb(name, shape, dt):
            return ctx.enter_context(nc.sbuf_tensor("s_" + name, shape, dt))

        def sem(name):
            return ctx.enter_context(nc.semaphore(name))

        r1 = nc.dram_tensor("row1", [N, 2 * D], F32, kind="Internal").ap()
        kv1 = nc.dram_tensor("kv1", [N, 2 * D], F32, kind="Internal").ap()
        r2 = nc.dram_tensor("row2", [N, 2 * D], F32, kind="Internal").ap()
        kv2 = nc.dram_tensor("kv2", [N, 2 * D], F32, kind="Internal").ap()
        yst = nc.dram_tensor("yst", [N, D + 2], F32, kind="Internal").ap()
        table = nc.dram_tensor("table", [N, TAB], I32, kind="Internal").ap()

        adj8 = sb("adj8", [P, T, T, P], FP8)
        adjbytes = adj8[:, :, :, :].rearrange("p t c i -> p t (c i)").bitcast(U8)
        KEPT = T - 4
        stage = [adj8[:, KEPT + 2 * u:KEPT + 2 * u + 2, :, :].rearrange("p t c i -> p (t c i)").bitcast(F16)
                 .rearrange("p (c i) -> p c i", i=P) for u in range(2)]
        cf = sb("cf", [P, C_F32], F32)
        ci = sb("ci", [P, C_I32], I32)
        packb = sb("packb", [P, WC], F16)
        listf = sb("listf", [P, T, SLOTS], F32)
        degree = sb("degree", [P, T], F32)
        stat = sb("stat", [P, 48], F32)
        REGION = 63616
        region = sb("region", [P, REGION // 4], F32)

        def carve(at, n):
            assert (at + n) <= REGION // 4, (at, n)
            return region[:, at:at + n]

        ident = cf[:, C_IDENT:C_IDENT + P]
        ps = ctx.enter_context(nc.psum_tensor("ps", [P, 8, 512], F32))

        xp = carve(0, T * D).bitcast(F16).rearrange("p (c n) -> p c n", n=2 * D)
        a0 = T * D
        gword = carve(a0, WORDS // 2).bitcast(BF16)
        work_at = a0 + WORDS // 2
        xt = [carve(work_at + u * 256, 256) for u in range(2)]
        aggs = carve(work_at + 512, 256)
        axT = carve(work_at + 768, 512)
        x1T = carve(work_at + 1280, 256)
        row1 = carve(work_at + 1536, 512)
        kvr1 = carve(work_at + 2048, 512)
        key = [carve(work_at + 2560 + 256 * k, 256) for k in range(2)]
        xr = [carve(work_at + 3072 + 1024 * k, 1024) for k in range(2)]
        xs = [adj8[:, T // 4 + n, :, :].rearrange("p c i -> p (c i)").bitcast(F32) for n in range(T // 4)]

        weights = sb("weights", [P, 3 * KD * D], F32)
        wqkv = weights[:, :].rearrange("p (k n) -> p k n", k=KD)
        comb = sb("comb", [P, 2 * KD * D], F32)
        wnc = comb[:, 0:KD * D].rearrange("p (k n) -> p k n", k=KD)
        wsc = comb[:, KD * D:].rearrange("p (k n) -> p k n", k=KD)
        biasb = sb("biasb", [P, D], F32)
        raw = carve(work_at + 5120, 2048)
        wsT = raw[:, 0:512].rearrange("p (k n) -> p k n", k=KD)
        wnT = raw[:, 512:1024].rearrange("p (k n) -> p k n", k=KD)
        wc = raw[:, 1024:2048].rearrange("p (k n) -> p k n", k=2 * KD)
        bcol = sb("bcol", [P, 2 * KD], F32)
        web = sb("web", [P, D], F32)
        beb = sb("beb", [P, 1], F32)

        BANK_A = [ps[:, 0, :], ps[:, 1, :]]
        BANK_W, BANK_T, BANK_X, BANK_O = ps[:, 2, :], ps[:, 3, :], ps[:, 4, :], ps[:, 5, :]
        BANK_K, BANK_QV = ps[:, 6, :], ps[:, 7, :]

        class Sems(dict):

            def __init__(self, stage):
                self.stage = stage

            def __missing__(self, name):
                self[name] = sem(self.stage + "_" + name)
                return self[name]

        s = Sems("a")
        paced = sem("paced")
        adj_in = [s["adj_in0"], s["adj_in1"]]
        xt_in = [s["xt_in0"], s["xt_in1"]]
        XC = 4

        XSCALE, XBACK = (sb(n, [P, 1], F32) for n in ("xscale", "xback"))
        RDLOW = sb("rdlow", [P, 1], F32)
        amax = sb("amax", [P, 16], F32)
        RDEG, BN, MV, RSTD, NEWT, DEG = (stat[:, 0:1], stat[:, 2:8], stat[:, 8:10], stat[:, 10:11], stat[:, 11:12], stat[:, 12:13])
        k16 = stat[:, 16:32]
        n16 = stat[:, 32:48]
        smalli = sb("smalli", [P, 2 * SLOTS], I32)
        kint, kgrp = smalli[:, 0:SLOTS], smalli[:, SLOTS:]
        kgrpf = sb("kgrpf", [P, SLOTS], F32)

        def tiles_of_a(eng, body):
            body(0, 0, 0)
            body(1, 0, 1)
            body(2, 1, 0)
            with eng.Fori(1, T // 2 - 1) as i:
                body(i * 2 + 1, i, 1)
                body(i * 2 + 2, i + 1, 0)
            body(T - 1, T // 2 - 1, 1)

        tabw = carve(14400, (T + 1) * TAB).bitcast(I32).rearrange("p (t n) -> p t n", n=TAB)
        cls = carve(0, 256).bitcast(BF16)
        cls3 = cls.rearrange("p (c t) -> p c t", t=T)
        upperb = carve(256, P // 2).bitcast(BF16)
        onesb = carve(320, P // 2).bitcast(BF16)
        tot, incl, posw, zero = (carve(512 * k + 512, 512) for k in range(4))
        lst = listf[:, :, :].rearrange("p t k -> p (t k)")
        over = carve(2560, SLOTS + 1)
        mid = carve(2600, T * SLOTS)
        rank = sb("rank", [P, T], I32)
        flag = sb("flag", [P, 1], I32)
        s_cls, s_rank, s_rstep = sem("classes_ready"), sem("ranks_counted"), sem("rank_step")
        kvbuf = carve(0, 2 * KV_SLOTS * 2 * D).rearrange("p (s n) -> p s n", n=2 * D)
        more = adj8[:, KEPT:T, :, :].rearrange("p t c i -> p (t c i)").bitcast(F32).rearrange("p (s n) -> p s n", n=2 * D)

        def load_tail(pool, done):
            for t in range(KEPT, T):
                pool.dma_start(adj8[:, t, :, :].rearrange("p c i -> p (c i)"), dram["adj_tiles"][t]).then_inc(done, 16)

        def rows(ap, t):
            return ap[bass.ds(t * P, P), :]

        with nc.Block() as block:
            @block.gpsimd
            def _(pool):
                def load(t, q, u, kept=True):
                    if not (isinstance(t, int) and t < 2):
                        pool.wait_ge(s["agg_done"], t - 1)
                        if kept:
                            pool.wait_ge(s["kept"], t * 2 - 2)
                    src = dram["adj_tiles"][bass.ds(t, 1)].rearrange("a p n -> (a p) n")
                    pool.dma_start(stage[u].rearrange("p c i -> p (c i)"), src).then_inc(adj_in[u], 16)
                load(0, 0, 0)
                pool.wait_ge(s["xs_in3"], 16)
                load(1, 0, 1)
                with pool.Fori(1, KEPT // 2 + 1) as i:
                    load(i * 2, i, 0)
                    load(i * 2 + 1, i, 1)
                load(T - 2, T // 2 - 1, 0, False)
                load(T - 1, T // 2 - 1, 1, False)
                pool.wait_ge(s["ranked"], 1)
                overflow = pool.value_load(flag[0:1, 0:1], min_val=0, max_val=1)
                with pool.If(overflow == 0):
                    for t in range(T):
                        pool.indirect_dma_start(
                            out=table, out_offset=bass.IndirectOffsetOnAxis(ap=rank[:, t:t + 1], axis=0),
                            in_=tabw[:, t, :], in_offset=None).then_inc(s["table_out"], 16)
                    pool.wait_ge(s["table_out"], 16 * T)

            @block.sync
            def _(sp):
                sp.dma_start(cf[:, :], dram["const_f32"]).then_inc(s["const_in"], 16)
                sp.dma_start(ci[:, :], dram["const_i32"]).then_inc(s["const_in"], 16)
                sp.dma_start(wsT, dram["w_selfT0"].rearrange("(k p) n -> p k n", p=P)).then_inc(s["raw_in"], 16)
                sp.dma_start(wnT, dram["w_nbT0"].rearrange("(k p) n -> p k n", p=P)).then_inc(s["raw_in"], 16)
                sp.dma_start(wc, dram["W_comb"].rearrange("(k p) n -> p k n", p=P)).then_inc(s["raw_in"], 16)
                sp.dma_start(bcol[:, 0:KD], dram["b_self"]).then_inc(s["raw_in"], 16)
                sp.dma_start(bcol[:, KD:], dram["b_nb"]).then_inc(s["raw_in"], 16)
                for n in range(0, T // XC, 2):
                    src = dram["x"][n * XC * P:(n + 2) * XC * P, :].rearrange("(c p) d -> p c d", p=P)
                    two = adj8[:, T // 4 + n:T // 4 + n + 2, :, :].rearrange("p t c i -> p (t c i)").bitcast(F32)
                    sp.dma_start(two.rearrange("p (c d) -> p c d", d=D), src).then_inc(s["xs_in%d" % (n // 2)], 16)
                sp.dma_start(biasb[:, :], dram["b_comb"].to_broadcast([P, D])).then_inc(s["bias_in"], 16)
                sp.dma_start(web[:, 0:HD], dram["we"].to_broadcast([P, HD])).then_inc(s["w1_in"], 16)
                sp.dma_start(beb[:, :], dram["be"].to_broadcast([P, 1])).then_inc(s["w1_in"], 16)
                for j, name in enumerate(("WK1T", "WQ1T", "WV1T")):
                    sp.dma_start(wqkv[:, :, j * D:(j + 1) * D],
                                 dram[name].rearrange("(k p) n -> p k n", p=P)).then_inc(s["w1_in"], 16)

                def body(t, q, u):
                    if not (isinstance(t, int) and t == 0):
                        sp.wait_ge(s["x1_ready"], t)
                    sp.dma_start(xt[u], rows(dram["x"], t)).then_inc(xt_in[u], 16)
                    if not (isinstance(t, int) and t == 0):
                        store(t - 1)

                def store(t):
                    sp.wait_ge(s["qv_ready"], t + 1)
                    sp.wait_ge(s["x1_ready"], t + 1)
                    sp.dma_start(rows(r1, t), row1).then_inc(s["row1_out"], 16)
                    sp.wait_ge(s["k_ready"], t + 1)
                    sp.dma_start(rows(kv1, t), kvr1).then_inc(s["kv1_out"], 16)

                tiles_of_a(sp, body)
                store(T - 1)
                sp.wait_ge(s["row1_out"], 16 * T)
                sp.wait_ge(s["kv1_out"], 16 * T)
                sp.wait_ge(s["ranked"], 1)
                overflow = sp.value_load(flag[0:1, 0:1], min_val=0, max_val=1)
                with sp.If(overflow == 0):
                    sp.wait_ge(s["table_out"], 16 * T)
                    sp.dma_start(tabw[:, 0:T, :], table.rearrange("(t p) n -> p t n", p=P)).then_inc(s["tab_in"], 16)
                    sp.wait_ge(s["tab_in"], 16)

            @block.tensor
            def _(pe):
                pe.wait_ge(s["raw_in"], 80)
                pe.wait_ge(s["comb_ready"], 1)
                for half, (w, o) in enumerate(((wnT, 1), (wsT, 0))):
                    for k in range(KD):
                        for m in range(KD):
                            mm = pe.matmul(ps[:, half, k * D:(k + 1) * D], w[:, m, k * P:(k + 1) * P],
                                           wc[:, o * KD + m, :], start=(m == 0), stop=(m == KD - 1))
                mm.then_inc(s["comb_done"], 1)
                for m in range(2 * KD):
                    mm = pe.matmul(BANK_W[:, 0:D], xr[0][:, m * P:(m + 1) * P], wc[:, m, :],
                                   start=(m == 0), stop=(m == 2 * KD - 1))
                mm.then_inc(s["comb_done"], 1)
                pe.wait_ge(s["scale_ready"], 1)
                pe.matmul(BANK_T[:, 0:P], xr[1][:, 0:P], ident, start=True, stop=True).then_inc(s["comb_done"], 1)
                pe.wait_ge(s["pack_ready"], 1)
                pe.wait_ge(s["comb_ready"], 2)

                def aggregate(t, q, u):
                    two, one_before = (t - 2, q - 1, u), (t - 1, q if u else q - 1, 1 - u)
                    at = {}
                    if not (isinstance(t, int) and t < 1):
                        at.update({14: (turn_ax, one_before), 18: (layer0, one_before)})
                    if not (isinstance(t, int) and t < 2):
                        at.update({2: (turn_x1, two), 5: (project, two)})
                    pe.wait_ge(adj_in[u], 16 * q + 16)
                    for c in range(T):
                        if isinstance(t, int) and t == 0 and c % XC == 0:
                            pe.wait_ge(s["xp_ready"], c // XC + 1)
                        if c in at:
                            step, tile = at[c]
                            step(*tile)
                        mask = stage[u][:, c, :]
                        pe.matmul(BANK_A[u], mask, xp[:, c, :], start=(c == 0), stop=(c == T - 1))
                    if isinstance(t, int) and t == 0:
                        pe.wait_ge(s["comb_ready"], 4)
                    else:
                        pe.wait_ge(s["words_taken"], t)
                    for c in range(T):
                        mask = stage[u][:, c, :]
                        mm = pe.matmul(BANK_W[:, c * WC:(c + 1) * WC], mask, packb[:, :], start=True, stop=True)
                    mm.then_inc(s["agg_done"], 1)

                def turn_ax(t, q, u):
                    pe.wait_ge(s["aggs_ready"], t + 1)
                    pe.wait_ge(xt_in[u], 16 * q + 16)
                    for k in range(KD):
                        pe.transpose(BANK_T[:, k * P:(k + 1) * P], aggs[:, k * P:(k + 1) * P], ident)
                    for k in range(KD):
                        mm = pe.transpose(BANK_T[:, (KD + k) * P:(KD + k + 1) * P], xt[u][:, k * P:(k + 1) * P], ident)
                    mm.then_inc(s["ax_turned"], 1)

                def layer0(t, q, u):
                    pe.wait_ge(s["axT_ready"], t + 1)
                    for k in range(2 * KD):
                        w = wnc[:, k, :] if k < KD else wsc[:, k - KD, :]
                        mm = pe.matmul(BANK_O[:, 0:D], axT[:, k * P:(k + 1) * P], w, start=(k == 0), stop=(k == 2 * KD - 1))
                    mm.then_inc(s["o_done"], 1)

                def turn_x1(t, q, u):
                    pe.wait_ge(s["x1_ready"], t + 1)
                    for k in range(KD):
                        mm = pe.transpose(BANK_X[:, k * P:(k + 1) * P], row1[:, k * P:(k + 1) * P], ident)
                    mm.then_inc(s["x1_turned"], 1)

                def project(t, q, u):
                    if isinstance(t, int) and t == 0:
                        pe.wait_ge(s["w1_in"], 80)
                    pe.wait_ge(s["x1T_ready"], t + 1)
                    if not (isinstance(t, int) and t == 0):
                        pe.wait_ge(s["k_ready"], t)
                        pe.wait_ge(s["qv_ready"], t)
                    for k in range(KD):
                        pe.matmul(BANK_K[:, 0:D], x1T[:, k * P:(k + 1) * P], wqkv[:, k, 0:D], start=(k == 0), stop=(k == KD - 1))
                    for k in range(KD):
                        mm = pe.matmul(BANK_QV, x1T[:, k * P:(k + 1) * P], wqkv[:, k, D:3 * D], start=(k == 0), stop=(k == KD - 1))
                    mm.then_inc(s["qkv_done"], 1)

                aggregate(0, 0, 0)
                aggregate(1, 0, 1)
                aggregate(2, 1, 0)
                with pe.Fori(1, T // 2 - 1) as i:
                    aggregate(i * 2 + 1, i, 1)
                    aggregate(i * 2 + 2, i + 1, 0)
                last = (T - 1, T // 2 - 1, 1)
                aggregate(*last)
                turn_x1(T - 2, T // 2 - 1, 0)
                project(T - 2, T // 2 - 1, 0)
                turn_ax(*last)
                layer0(*last)
                pe.wait_ge(s_cls, 1)
                pe.matmul(ps[:, 0, :], upperb, cls, start=True, stop=True)
                pe.matmul(ps[:, 1, :], onesb, cls, start=True, stop=True).then_inc(s_rank, 1)
                turn_x1(*last)
                project(*last)

            @block.scalar
            def _(act):
                act.wait_ge(s["comb_done"], 1)
                act.activation(comb[:, :], ps[:, 0:2, :].rearrange("p a n -> p (a n)"), ACT.Copy).then_inc(s["comb_ready"], 1)
                act.wait_ge(s["scale_ready"], 2)

                def low(n):
                    act.wait_ge(s["x_rest"], n + 1)
                    act.activation(xp[:, n * XC:(n + 1) * XC, D:2 * D], xr[n % 2].rearrange("p (c d) -> p c d", d=D),
                                   ACT.Copy, scale=LOW).then_inc(s["xp_ready"], 1)

                for n in range(T // XC):
                    act.activation(xp[:, n * XC:(n + 1) * XC, 0:D], xs[n].rearrange("p (c d) -> p c d", d=D), ACT.Copy,
                                   scale=XSCALE[:, 0:1]).then_inc(s["x_high"], 1)
                    if n:
                        low(n - 1)
                low(T // XC - 1)

                def keep(t, q, u, half):
                    w = T * P // 2
                    act.wait_ge(adj_in[u], 16 * q + 16)
                    act.activation(adjbytes[:, bass.ds(t, 1), half * w:half * w + w].rearrange("p a n -> p (a n)"),
                                   stage[u].rearrange("p c i -> p (c i)")[:, half * w:half * w + w], ACT.Copy,
                                   scale=ONE8).then_inc(s["kept"], 1)

                def x1_turned(t):
                    act.wait_ge(s["x1_turned"], t + 1)
                    act.activation(x1T, BANK_X[:, 0:D], ACT.Copy).then_inc(s["x1T_ready"], 1)

                def projections(t):
                    act.wait_ge(s["qkv_done"], t + 1)
                    if not (isinstance(t, int) and t == 0):
                        act.wait_ge(s["row1_out"], 16 * t)
                        act.wait_ge(s["kv1_out"], 16 * t)
                    act.activation(row1[:, D:2 * D], BANK_QV[:, 0:D], ACT.Copy)
                    act.activation(kvr1[:, D:2 * D], BANK_QV[:, D:2 * D], ACT.Copy).then_inc(s["qv_ready"], 1)

                def body(t, q, u, kept):
                    first = isinstance(t, int) and t == 0
                    if not first:
                        x1_turned(t - 1)
                    act.wait_ge(s["rdeg_ready"], t + 1)
                    act.activation(aggs, BANK_A[u][:, 0:D], ACT.Copy, scale=RDEG).then_inc(s["agg_high"], 1)
                    if not first:
                        projections(t - 1)
                    act.wait_ge(s["ax_turned"], t + 1)
                    act.activation(axT, BANK_T, ACT.Copy).then_inc(s["axT_ready"], 1)
                    if kept:
                        keep(t + 1, q + u, 1 - u, 0)
                    act.wait_ge(s["var_ready"], t + 1)
                    act.activation(RSTD, RSTD, ACT.Sqrt).then_inc(s["rstd_ready"], 1)
                    if kept:
                        keep(t + 1, q + u, 1 - u, 1)

                keep(0, 0, 0, 0)
                keep(0, 0, 0, 1)
                body(0, 0, 0, True)
                body(1, 0, 1, True)
                body(2, 1, 0, True)
                with act.Fori(1, KEPT // 2 - 1) as i:
                    body(i * 2 + 1, i, 1, True)
                    body(i * 2 + 2, i + 1, 0, True)
                with act.Fori(KEPT // 2 - 1, T // 2 - 1) as i:
                    body(i * 2 + 1, i, 1, False)
                    body(i * 2 + 2, i + 1, 0, False)
                body(T - 1, T // 2 - 1, 1, False)
                x1_turned(T - 1)
                projections(T - 1)

            @block.vector
            def _(dve):
                st = Steps(dve, s["dve_step"], 0, paced)
                dve.wait_ge(s["const_in"], 32)
                st(dve.tensor_copy(packb[:, :], cf[:, C_PACK:C_PACK + WC]))
                st(dve.tensor_copy(gword, cf[:, C_GROUP:C_GROUP + WORDS]))
                dve.wait_ge(s["raw_in"], 80)
                for m in range(2 * KD):
                    ins = dve.tensor_copy(xr[0][:, m * P:(m + 1) * P], bcol[:, m:m + 1].to_broadcast([P, P]))
                    st(ins)
                st.wait()
                dve.sem_inc(s["pack_ready"], 1)
                dve.sem_inc(s["comb_ready"], 1)
                for n in range(T // XC):
                    dve.wait_ge(s["xs_in%d" % (n // 2)], 16)
                    st(dve.tensor_reduce(amax[:, n:n + 1], xs[n], AX.X, ALU.max, apply_absolute_value=True))
                st.wait()
                st(dve.tensor_reduce(amax[:, 8:9], amax[:, 0:8], AX.X, ALU.max))
                st.wait()
                st(dve.tensor_copy(xr[1][:, 0:P], amax[:, 8:9].to_broadcast([P, P])))
                st.wait()
                dve.sem_inc(s["scale_ready"], 1)
                dve.wait_ge(s["comb_done"], 3)
                st(dve.tensor_reduce(amax[:, 9:10], BANK_T[:, 0:P], AX.X, ALU.max))
                st.wait()
                bits = amax[:, :].bitcast(I32)
                one = 1 << 23
                st(dve.tensor_scalar(bits[:, 10:11], bits[:, 9:10], EXPONENT, None, ALU.bitwise_and))
                st.wait()
                st(dve.tensor_scalar(bits[:, 11:12], bits[:, 10:11], float((TOP + 1) * one), None, ALU.max))
                st.wait()
                st(dve.tensor_scalar(XBACK[:, :].bitcast(I32), bits[:, 11:12], float(-TOP * one), None, ALU.add))
                st(dve.tensor_scalar(XSCALE[:, :].bitcast(I32), bits[:, 11:12], -1.0, float((254 + TOP) * one), ALU.mult, ALU.add))
                st.wait()
                dve.sem_inc(s["scale_ready"], 1)
                for n in range(T // XC):
                    dve.wait_ge(s["x_high"], n + 1)
                    if n == 0:
                        dve.wait_ge(s["comb_done"], 2)
                    if n >= 2:
                        dve.wait_ge(s["xp_ready"], n - 1)
                    view = xp[:, n * XC:(n + 1) * XC, 0:D]
                    dve.scalar_tensor_tensor(out=xr[n % 2].rearrange("p (c d) -> p c d", d=D), in0=xs[n].rearrange("p (c d) -> p c d", d=D),
                                             scalar=XSCALE[:, 0:1], in1=view, op0=ALU.mult, op1=ALU.subtract).then_inc(s["x_rest"], 1)
                dve.wait_ge(s["w1_in"], 80)
                for h in range(1, H):
                    st(dve.tensor_copy(web[:, h * HD:(h + 1) * HD], web[:, 0:HD]))
                dve.wait_ge(s["bias_in"], 16)
                st(dve.tensor_tensor(biasb[:, :], BANK_W[:, 0:D], biasb[:, :], ALU.add))
                st.wait()
                dve.sem_inc(s["comb_ready"], 2)
                base = st.count

                def lists(t, q, u):
                    first = isinstance(t, int) and t == 0
                    st = Steps(dve, s["dve_step"], base + t * STEPS_A, paced)
                    dve.wait_ge(s["agg_done"], t + 1)
                    words = BANK_W[:, 0:T * WC].rearrange("p (c w) -> p c w", w=WC)
                    st(dve.tensor_reduce(DEG, words[:, :, WPC:WC].rearrange("p c w -> p (c w)"), AX.X, ALU.add))
                    st.wait()
                    st(dve.tensor_copy(degree[:, bass.ds(t, 1)], DEG))
                    st(dve.tensor_scalar(RDEG, DEG, 1.0, None, ALU.max))
                    st.wait()
                    st(dve.reciprocal(RDEG, RDEG))
                    st.wait()
                    st(dve.tensor_scalar(RDLOW[:, :], RDEG, XBACK[:, 0:1], 1.0 / LOW, ALU.mult, ALU.mult))
                    dve.tensor_scalar(RDEG, RDEG, XBACK[:, 0:1], None, ALU.mult).then_inc(s["rdeg_ready"], 1)
                    words, groups, key3 = words[:, :, 0:WPC], gword.rearrange("p (c w) -> p c w", w=WPC), key[0].rearrange("p (c w) -> p c w", w=WPC)
                    st(dve.scalar_tensor_tensor(out=key3, in0=words, scalar=0.0, in1=groups, op0=ALU.is_gt, op1=ALU.mult))
                    st.wait()
                    st(dve.tensor_tensor(key3, words, key3, ALU.add))
                    st.wait()
                    dve.sem_inc(s["words_taken"], 1)
                    dve.wait_ge(s["agg_high"], t + 1)
                    dve.scalar_tensor_tensor(out=aggs, in0=BANK_A[u][:, D:2 * D], scalar=RDLOW[:, 0:1], in1=aggs,
                                             op0=ALU.mult, op1=ALU.add).then_inc(s["aggs_ready"], 1)
                    if not first:
                        energy(t - 1)
                    top16(st, k16, key[0], key[1])
                    st(dve.tensor_copy(kint, k16))
                    st.wait()
                    st(dve.tensor_scalar(kgrp, kint, WORD, 4, ALU.logical_shift_right, ALU.logical_shift_left))
                    cand = key[0].bitcast(I32).rearrange("p (s b) -> p s b", b=WORD)
                    node = key[1].rearrange("p (s b) -> p s b", b=WORD)
                    st(dve.tensor_tensor(cand, kint.rearrange("p (s o) -> p s o", o=1).to_broadcast([P, SLOTS, WORD]),
                                         ci[:, C_POW:C_POW + WORD].rearrange("p (o b) -> p o b", o=1).to_broadcast([P, SLOTS, WORD]),
                                         ALU.bitwise_and))
                    st.wait()
                    st(dve.tensor_copy(kgrpf[:, :], kgrp))
                    st.wait()
                    st(dve.tensor_tensor(node, kgrpf[:, :].rearrange("p (s o) -> p s o", o=1).to_broadcast([P, SLOTS, WORD]),
                                         cf[:, C_BIT:C_BIT + WORD].rearrange("p (o b) -> p o b", o=1).to_broadcast([P, SLOTS, WORD]), ALU.add))
                    st.wait()
                    st(dve.scalar_tensor_tensor(out=key[1], in0=key[0].bitcast(I32), scalar=0.0, in1=key[1],
                                                op0=ALU.is_gt, op1=ALU.mult))
                    st.wait()
                    top16(st, n16, key[1], key[0])
                    st(dve.tensor_copy(listf[:, bass.ds(t, 1), :].rearrange("p a k -> p (a k)"), n16))
                    assert st.count == STEPS_LISTS, st.count

                def norm(t, q, u):
                    first = isinstance(t, int) and t == 0
                    st = Steps(dve, s["dve_step"], base + t * STEPS_A + STEPS_LISTS, paced)
                    dve.wait_ge(s["o_done"], t + 1)
                    if not first:
                        dve.wait_ge(s["row1_out"], 16 * t)
                    y = row1[:, 0:D]
                    st(dve.tensor_tensor(y, BANK_O[:, 0:D], biasb[:, :], ALU.add))
                    st.wait()
                    dve.wait_ge(xt_in[u], 16 * q + 16)
                    st(dve.scalar_tensor_tensor(out=y, in0=y, scalar=0.0, in1=xt[u], op0=ALU.max, op1=ALU.add))
                    st.wait()
                    layernorm(st, y, s["var_ready"], s["rstd_ready"], t)
                    dve.tensor_scalar(y, y, MV[:, 0:1], RSTD, ALU.subtract, ALU.mult).then_inc(s["x1_ready"], 1)
                    assert st.count == STEPS_A - STEPS_LISTS, st.count

                def energy(t):
                    dve.wait_ge(s["qkv_done"], t + 1)
                    if not (isinstance(t, int) and t == 0):
                        dve.wait_ge(s["kv1_out"], 16 * t)
                    dve.scalar_tensor_tensor(out=kvr1[:, 0:D], in0=BANK_K[:, 0:D], scalar=SCALE1, in1=web[:, :],
                                             op0=ALU.mult, op1=ALU.add).then_inc(s["k_ready"], 1)

                def top16(st, out16, values, spare):
                    st.wait(alone=True)
                    st(dve.max(out16[:, 0:8], values))
                    st.wait(alone=True)
                    st(dve.match_replace(spare, out16[:, 0:8], values, 0.0))
                    st.wait(alone=True)
                    st(dve.max(out16[:, 8:16], spare))
                    st.wait()

                def layernorm(st, y, var_ready, rstd_ready, t):
                    st(dve.bn_stats(BN, y))
                    st.wait(alone=True)
                    st(dve.bn_aggr(MV, BN))
                    st.wait()
                    st(dve.tensor_scalar(NEWT, MV[:, 1:2], EPS, None, ALU.add))
                    st.wait()
                    dve.reciprocal(RSTD, NEWT).then_inc(var_ready, 1)
                    dve.wait_ge(rstd_ready, t + 1)
                    st(dve.tensor_scalar(NEWT, NEWT, RSTD, RSTD, ALU.mult, ALU.mult))
                    st.wait()
                    st(dve.tensor_scalar(NEWT, NEWT, -0.5, 1.5, ALU.mult, ALU.add))
                    st.wait()
                    st(dve.tensor_tensor(RSTD, RSTD, NEWT, ALU.mult))
                    st.wait()

                def ranks():
                    st = Steps(dve, s_rstep, 0, paced)
                    st(dve.tensor_tensor(cls3, degree[:, :].rearrange("p (o t) -> p o t", o=1).to_broadcast([P, SLOTS, T]),
                                         cf[:, C_CLASS:C_CLASS + SLOTS].rearrange("p (c o) -> p c o", o=1).to_broadcast([P, SLOTS, T]),
                                         ALU.is_equal))
                    st(dve.tensor_copy(upperb, cf[:, C_UPPER:C_UPPER + P]))
                    st(dve.memset(onesb, 1.0))
                    st.wait()
                    dve.sem_inc(s_cls, 1)
                    st(dve.memset(zero, 0.0))
                    st(dve.memset(tabw.rearrange("p t n -> p (t n)"), 0))
                    st(dve.tensor_scalar(mid, lst, 0.0, 2.0 ** 20, ALU.is_equal, ALU.mult))
                    st.wait()
                    list3, mid3 = listf[:, :, :], mid.rearrange("p (t k) -> p t k", k=SLOTS)
                    st(dve.scalar_tensor_tensor(out=tabw[:, 0:T, 0:SLOTS], in0=list3, scalar=-1.0, in1=mid3, op0=ALU.add, op1=ALU.add))
                    st(dve.tensor_scalar(tabw[:, 0:T, SLOTS:2 * SLOTS].bitcast(F32), list3, 0.0, MASKED, ALU.is_equal, ALU.mult))
                    st(dve.tensor_copy(tabw[:, 0:T, 2 * SLOTS:2 * SLOTS + 1], ci[:, C_OWN:C_OWN + T].rearrange("p (t o) -> p t o", o=1)))
                    dve.wait_ge(s_rank, 1)
                    st(dve.tensor_copy(tot, ps[:, 1, :]))
                    st.wait()
                    st(dve.tensor_tensor_scan(incl, tot, zero, 0.0, ALU.add, ALU.add))
                    st.wait()
                    st(dve.tensor_tensor(posw, incl, tot, ALU.subtract))
                    st(dve.tensor_tensor(over[:, 0:SLOTS], incl.rearrange("p (c t) -> p c t", t=T)[:, :, T - 1],
                                         cf[:, C_LIMIT:C_LIMIT + SLOTS], ALU.subtract))
                    st(dve.tensor_scalar(over[:, SLOTS:SLOTS + 1], incl[:, 511:512], -1.0, float(N), ALU.mult, ALU.add))
                    st.wait()
                    st(dve.tensor_tensor(posw, posw, ps[:, 0, :], ALU.add))
                    st(dve.tensor_reduce(stat[:, 0:1], over, AX.X, ALU.max))
                    st.wait()
                    st(dve.tensor_scalar(flag[:, :], stat[:, 0:1], 0.0, None, ALU.is_gt))
                    st(dve.tensor_tensor(posw, posw, cls, ALU.mult))
                    st.wait()
                    st(dve.tensor_reduce(mid[:, 0:T], posw.rearrange("p (c t) -> p t c", t=T), AX.X, ALU.add))
                    st.wait()
                    st(dve.tensor_copy(rank[:, :], mid[:, 0:T]))
                    st.wait()
                    dve.sem_inc(s["ranked"], 1)

                def body(t, q, u):
                    lists(t, q, u)
                    norm(t, q, u)

                body(0, 0, 0)
                body(1, 0, 1)
                body(2, 1, 0)
                with dve.Fori(1, T // 2 - 1) as i:
                    body(i * 2 + 1, i, 1)
                    body(i * 2 + 2, i + 1, 0)
                last = (T - 1, T // 2 - 1, 1)
                lists(*last)
                ranks()
                norm(*last)
                energy(T - 1)
                dve.memset(kvbuf.rearrange("p s n -> p (s n)"), 0.0).then_inc(s["cleared"], 1)
                dve.memset(more.rearrange("p s n -> p (s n)"), 0.0).then_inc(s["cleared"], 1)
                dve.wait_ge(s["cleared"], 2)


        rowo = [carve(11520 + 512 * k, 512) for k in range(2)]
        kvo = [carve(12544 + 512 * k, 512) for k in range(2)]
        turnT = carve(13568, 256)
        biaso = biasb[:, :]
        stat2 = sb("stat2", [P, 64], F32)
        l_BN, l_MV = stat2[:, 0:6], stat2[:, 6:8]
        l_R, l_N = stat2[:, 8:9], stat2[:, 9:10]
        l_max, l_cmax = stat2[:, 16:24], stat2[:, 24:32]
        l_sum, l_csum, l_nmax = stat2[:, 32:33], stat2[:, 33:34], stat2[:, 34:35]

        d_own = carve(0, 512)
        d_kv = carve(512, 512)
        d_qT, d_kT = carve(1024, 256), carve(1280, 256)
        d_neg = carve(1536, P)
        d_score = carve(1664, H * P)
        d_prob = carve(2688, H * P)
        d_probT = carve(3712, H * P)
        d_acc = carve(4736, D)
        identb = carve(4992, P // 2).bitcast(BF16)
        d_mask = carve(5056, P // 2).bitcast(BF16)

        layer_sems = {1: Sems("l1"), 2: Sems("l2")}

        def dense_layer(block_no, heads, src_row, src_kv, w_names):
            L = layer_sems[block_no]
            hardmax = heads > 1
            width = heads * P
            wide = [ps[:, 2 + k, :] for k in range(4)] if hardmax else [ps[:, 2, 0:P]]
            widep = [ps[:, 2, :], ps[:, 3, :]] if hardmax else [ps[:, 2, 0:P]]
            score, prob, probT = d_score[:, 0:width], d_prob[:, 0:width], d_probT[:, 0:width]

            def sync(sp):
                for j, name in enumerate(w_names):
                    sp.dma_start(wqkv[:, :, j * D:(j + 1) * D], dram[name].rearrange("(k p) n -> p k n", p=P)).then_inc(L["w_in"], 16)
                if not hardmax:
                    sp.dma_start(biaso, dram["bo2"].to_broadcast([P, D])).then_inc(L["w_in"], 16)
                with sp.Fori(0, T) as t:
                    sp.wait_ge(L["free"], t * (2 * T + 1) + 1)
                    sp.dma_start(d_own, rows(src_row, t)).then_inc(L["own_in"], 16)
                    with sp.Fori(0, 2 * T) as c:
                        sp.wait_ge(L["free"], t * (2 * T + 1) + c + 1)
                        chunk = c % T
                        sp.dma_start(d_kv, src_kv[bass.ds(chunk * P, P), :]).then_inc(L["kv_in"], 16)
                    sp.wait_ge(L["x_ready"], t + 1)
                    if hardmax:
                        sp.wait_ge(L["rowq"], t + 1)
                        sp.dma_start(rows(r2, t), rowo[0]).then_inc(L["row_out"], 16)
                        sp.dma_start(rows(kv2, t), kvo[0]).then_inc(L["row_out"], 16)
                        sp.wait_ge(L["row_out"], t * 32 + 32)
                        sp.sem_inc(paced, 1)
                    else:
                        sp.dma_start(rows(yst, t), rowo[0][:, 0:D + 2]).then_inc(L["row_out"], 16)
                        sp.wait_ge(L["row_out"], t * 16 + 16)
                        sp.sem_inc(paced, 1)

            def tensor(pe):
                pe.wait_ge(L["w_in"], 48 if hardmax else 32)
                pe.wait_ge(L["identb"], 1)
                with pe.Fori(0, T) as t:
                    pe.wait_ge(L["own_in"], t * 16 + 16)
                    for k in range(KD):
                        mm = pe.transpose(ps[:, 0, k * P:(k + 1) * P], d_own[:, D + k * P:D + (k + 1) * P], ident)
                    mm.then_inc(L["turned_q"], 1)
                    pe.wait_ge(L["qT"], t + 1)
                    pe.sem_inc(paced, 1)

                    def scores(t, c, n):
                        pe.wait_ge(L["kv_in"], n * 16 + 16)
                        for k in range(KD):
                            pe.transpose(ps[:, 0, k * P:(k + 1) * P], d_kv[:, k * P:(k + 1) * P], ident)
                        pe.wait_ge(L["mask"], n + 1)
                        pe.matmul(ps[:, 1, 0:P], d_mask, identb, start=True, stop=True).then_inc(L["turned"], 1)
                        pe.wait_ge(L["kT"], n + 1)
                        for h in range(heads):
                            if hardmax:
                                at = HD * (h % 4)
                                k = h // 4
                                mm = pe.matmul(wide[h % 4][:, k * P:(k + 1) * P], d_qT[at:at + HD, k * P:(k + 1) * P],
                                               d_kT[at:at + HD, k * P:(k + 1) * P], start=True, stop=True)
                            else:
                                for k in range(KD):
                                    mm = pe.matmul(wide[0], d_qT[:, k * P:(k + 1) * P], d_kT[:, k * P:(k + 1) * P],
                                                   start=(k == 0), stop=(k == KD - 1))
                        mm.then_inc(L["y_done"], 1)

                    with pe.Fori(0, T) as c:
                        scores(t, c, t * (2 * T) + c)
                    with pe.Fori(0, T) as c:
                        scores(t, c, t * (2 * T) + c + T)
                        pe.wait_ge(L["prob"], t * T + c + 1)
                        for h in range(heads):
                            mm = pe.transpose(widep[h // 4][:, (h % 4) * P:(h % 4 + 1) * P], prob[:, h * P:(h + 1) * P], ident)
                        mm.then_inc(L["turned_p"], 1)
                        pe.wait_ge(L["probT"], t * T + c + 1)
                        w = D // heads
                        for h in range(heads):
                            mm = pe.matmul(ps[:, 6, h * w:(h + 1) * w], probT[:, h * P:(h + 1) * P], d_kv[:, D + h * w:D + (h + 1) * w],
                                           start=True, stop=True)
                        mm.then_inc(L["summed"], 1)
                    pe.wait_ge(L["back"], t + 1)
                    src = rowo[0][:, 0:D] if hardmax else d_acc
                    for k in range(KD):
                        mm = pe.transpose(ps[:, 0, k * P:(k + 1) * P], src[:, k * P:(k + 1) * P], ident)
                    mm.then_inc(L["y_turned"], 1)
                    pe.wait_ge(L["turn_out"], t + 1)
                    for k in range(KD):
                        if hardmax:
                            pe.matmul(ps[:, 2, :], turnT[:, k * P:(k + 1) * P], wqkv[:, k, 0:2 * D], start=(k == 0), stop=(k == KD - 1))
                        else:
                            mm = pe.matmul(ps[:, 2, 0:D], turnT[:, k * P:(k + 1) * P], wqkv[:, k, 0:D], start=(k == 0), stop=(k == KD - 1))
                    if hardmax:
                        for k in range(KD):
                            mm = pe.matmul(ps[:, 3, 0:D], turnT[:, k * P:(k + 1) * P], wqkv[:, k, 2 * D:3 * D], start=(k == 0), stop=(k == KD - 1))
                    mm.then_inc(L["proj"], 1)

            def scalar(act):
                def mask(t, c, step):
                    act.wait_ge(L["free"], t * (2 * T + 1) + step + 1)
                    src = adjbytes[:, bass.ds(t, 1), bass.ds(c * P, P)].rearrange("p a i -> p (a i)")
                    act.activation(d_mask, src, ACT.Copy, scale=1.0 / ONE8).then_inc(L["mask"], 1)

                if hardmax:
                    act.wait_ge(L["tail_in"], 64)
                with act.Fori(0, T) as t:
                    act.wait_ge(L["turned_q"], t + 1)
                    act.activation(d_qT, ps[:, 0, 0:D], ACT.Copy).then_inc(L["qT"], 1)
                    with act.Fori(0, T) as c:
                        mask(t, c, c)
                        act.wait_ge(L["turned"], t * (2 * T) + c + 1)
                        act.activation(d_kT, ps[:, 0, 0:D], ACT.Copy).then_inc(L["kT"], 1)
                    with act.Fori(0, T) as c:
                        mask(t, c, c + T)
                        act.wait_ge(L["turned"], t * (2 * T) + c + T + 1)
                        act.activation(d_kT, ps[:, 0, 0:D], ACT.Copy).then_inc(L["kT"], 1)
                        if not hardmax:
                            act.wait_ge(L["nmax"], t * T + c + 1)
                            act.activation(prob, score, ACT.Exp, bias=l_nmax, scale=SCALE2, accum_out=l_csum).then_inc(L["prob"], 1)
                        act.wait_ge(L["turned_p"], t * T + c + 1)
                        src = ps[:, 2:4, :].rearrange("p a n -> p (a n)") if hardmax else widep[0]
                        act.activation(probT, src, ACT.Copy).then_inc(L["probT"], 1)
                    if hardmax:
                        act.wait_ge(L["var"], t + 1)
                        act.activation(l_R, l_R, ACT.Sqrt).then_inc(L["rstd"], 1)
                    act.wait_ge(L["y_turned"], t + 1)
                    act.activation(turnT, ps[:, 0, 0:D], ACT.Copy).then_inc(L["turn_out"], 1)
                    if hardmax:
                        act.wait_ge(L["proj"], t + 1)
                        act.activation(kvo[0], ps[:, 2, :], ACT.Copy).then_inc(L["kvrow"], 1)
                        act.wait_ge(L["kvrow"], t + 1)
                        act.activation(rowo[0][:, D:2 * D], ps[:, 3, 0:D], ACT.Copy).then_inc(L["rowq"], 1)

            def vector(dve):
                FRONT, ONE, TWO, END = 2, 5 if hardmax else 4, 5 if hardmax else 6, 8 if hardmax else 6
                per = FRONT + T * (ONE + TWO) + END
                st = Steps(dve, L["front"], 0, paced)
                st(dve.tensor_copy(identb, ident))
                st.wait()
                dve.sem_inc(L["identb"], 1)
                dve.sem_inc(L["free"], 1)
                base = 1

                def masked(st, n):
                    dve.wait_ge(L["turned"], n + 1)
                    st(dve.tensor_scalar(d_neg, ps[:, 1, 0:P], -MASKED, MASKED, ALU.mult, ALU.add))
                    st.wait()
                    if hardmax:
                        st(dve.tensor_scalar(d_neg, d_neg, beb[:, 0:1], None, ALU.add))
                        st.wait()
                    dve.wait_ge(L["y_done"], n + 1)
                    if hardmax:
                        st(dve.tensor_tensor(score.rearrange("p (k a n) -> p a k n", k=KD, n=P),
                                             ps[:, 2:6, 0:KD * P].rearrange("p a (k n) -> p a k n", n=P),
                                             d_neg.rearrange("p (b o n) -> p b o n", o=1, b=1).to_broadcast([P, 4, KD, P]), ALU.add))
                    else:
                        st(dve.tensor_tensor(score, wide[0], d_neg, ALU.add))
                    st.wait()

                with dve.Fori(0, T) as t:
                    tb = base + t * per
                    st = Steps(dve, L["front"], tb, paced)
                    st(dve.memset(l_max[:, 0:heads], -3.0e38))
                    st(dve.memset(d_acc, 0.0))
                    st.wait(alone=True)
                    with dve.Fori(0, T) as c:
                        st = Steps(dve, L["front"], tb + c * ONE + FRONT, paced)
                        masked(st, t * (2 * T) + c)
                        st(dve.tensor_reduce(l_cmax[:, 0:heads], score.rearrange("p (h n) -> p h n", n=P), AX.X, ALU.max))
                        st.wait()
                        st(dve.tensor_tensor(l_max[:, 0:heads], l_max[:, 0:heads], l_cmax[:, 0:heads], ALU.max))
                        st.wait()
                        dve.sem_inc(L["free"], 1)
                        assert st.count == ONE, st.count
                    if not hardmax:
                        dve.memset(l_sum, 0.0).then_inc(L["var"], 1)
                        dve.wait_ge(L["var"], t + 1)
                        dve.sem_inc(paced, 1)
                    with dve.Fori(0, T) as c:
                        st = Steps(dve, L["front"], tb + c * TWO + (FRONT + T * ONE), paced)
                        masked(st, t * (2 * T) + c + T)
                        if hardmax:
                            st(dve.tensor_tensor(prob.rearrange("p (h n) -> p h n", n=P), score.rearrange("p (h n) -> p h n", n=P),
                                                 l_max.rearrange("p (h o) -> p h o", o=1).to_broadcast([P, heads, P]), ALU.is_equal))
                            st.wait()
                            dve.sem_inc(L["prob"], 1)
                        else:
                            st(dve.tensor_scalar(l_nmax, l_max[:, 0:1], -SCALE2, None, ALU.mult))
                            st.wait()
                            dve.sem_inc(L["nmax"], 1)
                            dve.wait_ge(L["prob"], t * T + c + 1)
                            st(dve.tensor_tensor(l_sum, l_sum, l_csum, ALU.add))
                            st.wait()
                        dve.wait_ge(L["summed"], t * T + c + 1)
                        st(dve.tensor_tensor(d_acc, d_acc, ps[:, 6, 0:D], ALU.add))
                        st.wait()
                        if not hardmax:
                            st(dve.memset(l_cmax[:, 0:1], 0.0))
                            st.wait()
                        dve.sem_inc(L["free"], 1)
                        assert st.count == TWO, st.count
                    st = Steps(dve, L["front"], tb + (FRONT + T * (ONE + TWO)), paced)
                    if hardmax:
                        y = rowo[0][:, 0:D]
                        st(dve.scalar_tensor_tensor(out=y, in0=d_acc, scalar=1.0 / H, in1=d_own[:, 0:D], op0=ALU.mult, op1=ALU.add))
                        st.wait()
                        statistics(dve, st, y, L["var"])
                        newton(dve, st, L["rstd"], t)
                        st(dve.tensor_scalar(y, y, l_MV[:, 0:1], l_R, ALU.subtract, ALU.mult))
                        st.wait()
                        dve.sem_inc(L["back"], 1)
                        dve.wait_ge(L["rowq"], t + 1)
                        dve.sem_inc(L["x_ready"], 1)
                    else:
                        st(dve.reciprocal(l_sum, l_sum))
                        st.wait()
                        st(dve.tensor_scalar(d_acc, d_acc, l_sum, None, ALU.mult))
                        st.wait()
                        dve.sem_inc(L["back"], 1)
                        dve.wait_ge(L["w_in"], 32)
                        y = rowo[0][:, 0:D]
                        st(dve.tensor_tensor(y, d_own[:, 0:D], biaso, ALU.add))
                        st.wait()
                        dve.wait_ge(L["proj"], t + 1)
                        st(dve.tensor_tensor(y, y, ps[:, 2, 0:D], ALU.add))
                        st.wait()
                        st(dve.bn_stats(l_BN, y))
                        st.wait(alone=True)
                        st(dve.bn_aggr(rowo[0][:, D:D + 2], l_BN))
                        st.wait()
                        dve.sem_inc(L["x_ready"], 1)
                    dve.wait_ge(L["row_out"], t * (32 if hardmax else 16) + (32 if hardmax else 16))
                    dve.sem_inc(L["free"], 1)
                    assert st.count == END, st.count

            return sync, tensor, scalar, vector

        def statistics(dve, st, y, var_ready):
            st(dve.bn_stats(l_BN, y))
            st.wait(alone=True)
            st(dve.bn_aggr(l_MV, l_BN))
            st.wait()
            st(dve.tensor_scalar(l_N, l_MV[:, 1:2], EPS, None, ALU.add))
            st.wait()
            dve.reciprocal(l_R, l_N).then_inc(var_ready, 1)

        def newton(dve, st, rstd_ready, t):
            dve.wait_ge(rstd_ready, t + 1)
            st(dve.tensor_scalar(l_N, l_N, l_R, l_R, ALU.mult, ALU.mult))
            st.wait()
            st(dve.tensor_scalar(l_N, l_N, -0.5, 1.5, ALU.mult, ALU.add))
            st.wait()
            st(dve.tensor_tensor(l_R, l_R, l_N, ALU.mult))
            st.wait()

        dense = [dense_layer(1, H, r1, kv1, ("WK2T", "WV2T", "WQ2T")), dense_layer(2, 1, r2, kv2, ("WO2T",))]
        prod = carve(9216, KV_SLOTS * D)
        g_own = [comb[:, 512 * k:512 * k + 512] for k in range(2)]
        xb = [carve(12544 + 256 * k, 256) for k in range(2)]
        attn = carve(13056, 256)
        logit = carve(13824, SLOTS * H)
        picked = carve(13952, SLOTS * H)
        negb = carve(14080, SLOTS)
        prob2 = [carve(14096 + SLOTS * k, SLOTS) for k in range(2)]
        s_idx = [carve(14128 + 20 * k, SLOTS + 1).bitcast(I32) for k in range(2)]
        sid = sb("sid", [P, 2], I32)
        s_sum = stat2[:, 36:38]
        s_inv = stat2[:, 38:39]
        RUNS = []
        for t in range(1, T - 1, 2):
            c = CAPS[t]
            assert CAPS[t + 1] <= c <= KV_SLOTS
            if RUNS and RUNS[-1][2] == c:
                RUNS[-1][1] += 2
            else:
                RUNS.append([t, 2, c])

        def ranked_tiles(eng, body):
            body(0, 0, 0, CAPS[0], 0, 0)
            before = [CAPS[0], 0]
            for first, count, slots in RUNS:
                q = (first - 1) // 2
                if count == 2:
                    body(first, q, 1, slots, before[1], before[1] - q)
                    body(first + 1, q + 1, 0, slots, before[0], before[0] - (q + 1))
                else:
                    with eng.Fori(0, count // 2) as i:
                        body(i * 2 + first, i + q, 1, slots, i * slots + before[1], i * (slots - 1) + (before[1] - q))
                        body(i * 2 + (first + 1), i + (q + 1), 0, slots, i * slots + before[0],
                             i * (slots - 1) + (before[0] - (q + 1)))
                before = [b + count // 2 * slots for b in before]
            body(T - 1, T // 2 - 1, 1, CAPS[T - 1], before[1], before[1] - (T // 2 - 1))

        def pieces(u, slots):
            near = min(slots, KV_SLOTS)
            out = [(0, kvbuf[:, KV_SLOTS * u:KV_SLOTS * u + near, :])]
            if slots > near:
                out.append((near, more[:, 0:slots - near, :]))
            return out

        def slot(u, k):
            return kvbuf[:, KV_SLOTS * u + k, :] if k < KV_SLOTS else more[:, k - KV_SLOTS, :]

        def products(rows_, slots):
            return prod.rearrange("p (s n) -> p s n", n=D)[:, 0:slots, :] if slots <= KV_SLOTS else rows_[:, :, 0:D]

        def below(t, k):
            return isinstance(t, int) and t < k

        def back(t, q, u, k):
            if k % 2 == 0:
                return t - k, q - k // 2, u
            return t - k, (q - (k - 1) // 2 if u else q - (k + 1) // 2), 1 - u

        def sparse_layer(layer):
            S = layer_sems[layer]
            one = layer == 1
            src_kv = kv1 if one else kv2

            def sync(sp):
                names = ("WK2T", "WV2T", "WQ2T") if one else ("WO2T",)
                for j, name in enumerate(names):
                    sp.dma_start(wqkv[:, :, j * D:(j + 1) * D], dram[name].rearrange("(k p) n -> p k n", p=P)).then_inc(S["w_in"], 16)
                if one:
                    def store(t, q, u):
                        sp.wait_ge(S["x_ready"], t + 1)
                        sp.wait_ge(S["rowq"], t + 1)
                        sp.dma_start(rows(r2, t), rowo[u]).then_inc(S["row_out%d" % u], 16)

                    with sp.Fori(0, T // 2) as i:
                        store(i * 2, i, 0)
                        store(i * 2 + 1, i, 1)
                    sp.wait_ge(S["row_out0"], 16 * T // 2)
                    sp.wait_ge(S["row_out1"], 16 * T // 2)
                else:
                    sp.dma_start(biaso, dram["bo2"].to_broadcast([P, D])).then_inc(S["w_in"], 16)

                    def load(t, q, u):
                        if not below(t, 2):
                            sp.wait_ge(S["own_free"], t - 1)
                        sp.dma_start(g_own[u], rows(r2, t)).then_inc(S["own_in%d" % u], 16)

                    load(0, 0, 0)
                    load(1, 0, 1)
                    with sp.Fori(1, T // 2) as i:
                        load(i * 2, i, 0)
                        load(i * 2 + 1, i, 1)

            def gpsimd(pool):
                def gather(out_ap, src, idx, s_in, skip):
                    pool.indirect_dma_start(out=out_ap, out_offset=None, in_=src,
                                            in_offset=bass.IndirectOffsetOnAxis(ap=idx, axis=0),
                                            bounds_check=N - 1, oob_is_err=not skip).then_inc(s_in, 16)

                def scatter(t, q, u):
                    pool.wait_ge(S["kvrow"] if one else S["x_ready"], t + 1)
                    pool.wait_ge(S["sid_ready"], t + 1)
                    pool.sem_inc(paced, 1)
                    src, dst = (kvo[u], kv2) if one else (rowo[u][:, 0:D + 2], yst)
                    pool.indirect_dma_start(out=dst, out_offset=bass.IndirectOffsetOnAxis(ap=sid[:, u:u + 1], axis=0),
                                            in_=src, in_offset=None).then_inc(S["kv_out%d" % u], 16)

                late = 3

                def body(t, q, u, slots, g, others):
                    pool.wait_ge(S["idx_ready"], t + 1)
                    pool.sem_inc(paced, 1)
                    for k in range(slots):
                        if not below(t, 2):
                            if k + 1 < slots:
                                pool.wait_ge(S["slots_summed%d" % u], others + (k + 2 - slots))
                            else:
                                pool.wait_ge(S["summed"], t - 1)
                            pool.sem_inc(paced, 1)
                        gather(slot(u, k), src_kv, s_idx[u][:, k:k + 1], S["kv_in%d" % u], True)
                    if one:
                        if not below(t, 2):
                            pool.wait_ge(S["y_done"], t - 1)
                            pool.sem_inc(paced, 1)
                        gather(g_own[u], r1, s_idx[u][:, SLOTS:SLOTS + 1], S["own_in%d" % u], False)
                    if not below(t, late):
                        scatter(*back(t, q, u, late))

                ranked_tiles(pool, body)
                for k in range(late - 1, -1, -1):
                    scatter(*back(T - 1, T // 2 - 1, 1, k))
                pool.wait_ge(S["kv_out0"], 16 * T // 2)
                pool.wait_ge(S["kv_out1"], 16 * T // 2)

            def tensor(pe):
                pe.wait_ge(S["w_in"], 48 if one else 32)

                def total(t, q, u, slots, g):
                    if one:
                        pe.wait_ge(S["v_ready"], t + 1)
                    if not below(t, 2):
                        pe.wait_ge(S["y_done"], t - 1)
                    for k in range(slots):
                        if not one:
                            pe.wait_ge(S["weighed%d" % u], g + k + 1)
                        done = S["summed"] if k == slots - 1 else S["slots_summed%d" % u]
                        pe.matmul(ps[:, 6 + u, 0:D], ident, slot(u, k)[:, D:2 * D], start=(k == 0), stop=(k == slots - 1)).then_inc(done, 1)

                def project(t, q, u):
                    pe.wait_ge(S["x_ready"] if one else S["attn"], t + 1)
                    src = rowo[u][:, 0:D] if one else attn
                    for k in range(KD):
                        mm = pe.transpose(ps[:, 0, k * P:(k + 1) * P], src[:, k * P:(k + 1) * P], ident)
                    mm.then_inc(S["turned"], 1)
                    pe.wait_ge(S["turn_out"], t + 1)
                    if one:
                        if not below(t, 1):
                            pe.wait_ge(S["kvrow"], t)
                            pe.wait_ge(S["rowq"], t)
                        for k in range(KD):
                            pe.matmul(ps[:, 2, :], turnT[:, k * P:(k + 1) * P], wqkv[:, k, 0:2 * D], start=(k == 0), stop=(k == KD - 1))
                        for k in range(KD):
                            mm = pe.matmul(ps[:, 3, 0:D], turnT[:, k * P:(k + 1) * P], wqkv[:, k, 2 * D:3 * D], start=(k == 0), stop=(k == KD - 1))
                    else:
                        if not below(t, 1):
                            pe.wait_ge(S["x_ready"], t)
                        for k in range(KD):
                            mm = pe.matmul(ps[:, 2, 0:D], turnT[:, k * P:(k + 1) * P], wqkv[:, k, 0:D], start=(k == 0), stop=(k == KD - 1))
                    mm.then_inc(S["proj"], 1)

                def body(t, q, u, slots, g, others):
                    total(t, q, u, slots, g)
                    if not below(t, 1):
                        project(*back(t, q, u, 1))

                ranked_tiles(pe, body)
                project(T - 1, T // 2 - 1, 1)

            def scalar(act):
                def project(t, q, u):
                    if one:
                        act.wait_ge(S["var"], t + 1)
                        act.activation(l_R, l_R, ACT.Sqrt).then_inc(S["rstd"], 1)
                    act.wait_ge(S["turned"], t + 1)
                    act.activation(turnT, ps[:, 0, 0:D], ACT.Copy).then_inc(S["turn_out"], 1)
                    if one:
                        act.wait_ge(S["proj"], t + 1)
                        if not below(t, 2):
                            act.wait_ge(S["kv_out%d" % u], 16 * q)
                            act.wait_ge(S["row_out%d" % u], 16 * q)
                        act.activation(kvo[u], ps[:, 2, :], ACT.Copy).then_inc(S["kvrow"], 1)
                        act.activation(rowo[u][:, D:2 * D], ps[:, 3, 0:D], ACT.Copy).then_inc(S["rowq"], 1)

                def body(t, q, u, slots, g, others):
                    if not one:
                        act.wait_ge(S["nmax"], t + 1)
                        act.activation(prob2[u][:, 0:slots], logit[:, 0:slots], ACT.Exp, bias=l_nmax, scale=SCALE2,
                                       accum_out=s_sum[:, u:u + 1]).then_inc(S["prob"], 1)
                        act.wait_ge(S["prob"], t + 1)
                        for k in range(slots):
                            v = slot(u, k)[:, D:2 * D]
                            act.activation(v, v, ACT.Copy, scale=prob2[u][:, k:k + 1]).then_inc(S["weighed%d" % u], 1)
                    if not below(t, 1):
                        project(*back(t, q, u, 1))

                ranked_tiles(act, body)
                project(T - 1, T // 2 - 1, 1)

            def vector(dve):
                FRONT = 7 if one else 5
                BACK = 6 if one else 7
                heads = H if one else 1

                def index(t, u):
                    src = tabw[:, bass.ds(t, 1), :].rearrange("p a n -> p (a n)")
                    dve.tensor_copy(s_idx[u][:, 0:SLOTS], src[:, 0:SLOTS]).then_inc(S["front"], 1)
                    dve.tensor_copy(s_idx[u][:, SLOTS:SLOTS + 1], src[:, 2 * SLOTS:2 * SLOTS + 1]).then_inc(S["front"], 1)

                index(0, 0)
                index(1, 1)
                dve.wait_ge(S["front"], 4)
                dve.sem_inc(S["idx_ready"], 2)
                base = 4
                if not one:
                    dve.wait_ge(S["w_in"], 32)

                def product(t, q, u, slots, g):
                    st = Steps(dve, S["front"], t * FRONT + base, paced)
                    dve.wait_ge(S["kv_in%d" % u], g * 16 + 16 * slots)
                    dve.wait_ge(S["own_in%d" % u], 16 * q + 16)
                    if not one and not below(t, 1):
                        dve.wait_ge(S["prob"], t)
                    q_row = g_own[u][:, D:2 * D]
                    for at, kv in pieces(u, slots):
                        out, n = products(kv, slots), min(slots - at, KV_SLOTS)
                        if one:
                            qv = q_row.rearrange("p (o n) -> p o n", o=1).to_broadcast([P, n, D])
                            ins = dve.tensor_tensor(out, kv[:, :, 0:D], qv, ALU.mult)
                        else:
                            for k in range(n):
                                ins = dve.tensor_tensor_reduce(out[:, k, :], kv[:, k, 0:D], q_row, 1.0, 0.0,
                                                               ALU.mult, ALU.add, logit[:, at + k:at + k + 1])
                    st(ins)
                    index(min(t + 2, T) if isinstance(t, int) else t + 2, u)
                    st.count += 2
                    st.wait()
                    dve.sem_inc(S["idx_ready"], 1)
                    if one:
                        st(dve.tensor_scalar(negb[:, 0:slots], neg_of(t, slots), beb[:, 0:1], None, ALU.add))
                        return st.count
                    st(dve.tensor_tensor(logit[:, 0:slots], logit[:, 0:slots], neg_of(t, slots), ALU.add))
                    st.wait()
                    st(dve.tensor_reduce(l_max[:, 0:1], logit[:, 0:slots], AX.X, ALU.max))
                    st.wait()
                    dve.tensor_scalar(l_nmax, l_max[:, 0:1], -SCALE2, None, ALU.mult).then_inc(S["nmax"], 1)
                    return st.count

                def neg_of(t, slots):
                    return tabw[:, bass.ds(t, 1), SLOTS:SLOTS + slots].bitcast(F32).rearrange("p a n -> p (a n)")

                def weigh(t, q, u, slots, done):
                    if one:
                        st = Steps(dve, S["front"], t * FRONT + (base + done), paced)
                        lg = logit[:, 0:slots * H].rearrange("p (s h) -> p s h", h=H)
                        pk = picked[:, 0:slots * H].rearrange("p (s h) -> p s h", h=H)
                        for at, kv in pieces(u, slots):
                            out, n = products(kv, slots), min(slots - at, KV_SLOTS)
                            ins = dve.tensor_reduce(lg[:, at:at + n, :], out.rearrange("p s (h n) -> p s h n", n=HD), AX.X, ALU.add)
                        st(ins)
                        st.wait()
                        st(dve.tensor_tensor(lg, lg, negb[:, 0:slots].rearrange("p (s o) -> p s o", o=1).to_broadcast([P, slots, H]), ALU.add))
                        st.wait()
                        st(dve.tensor_reduce(l_max, lg.rearrange("p s h -> p h s"), AX.X, ALU.max))
                        st.wait()
                        dve.tensor_tensor(pk, lg, l_max.rearrange("p (o h) -> p o h", o=1).to_broadcast([P, slots, H]),
                                          ALU.is_equal).then_inc(S["prob"], 1)
                        dve.wait_ge(S["prob"], t + 1)
                        for at, kv in pieces(u, slots):
                            n = min(slots - at, KV_SLOTS)
                            v = kv[:, :, D:2 * D].rearrange("p s (h n) -> p s h n", n=HD)
                            w = pk[:, at:at + n, :].rearrange("p s (h o) -> p s h o", o=1).to_broadcast([P, n, H, HD])
                            ins = dve.tensor_tensor(v, v, w, ALU.mult)
                        ins.then_inc(S["v_ready"], 1)
                        assert done + st.count == FRONT, (done, st.count)
                    else:
                        dve.tensor_tensor(xb[u], g_own[u][:, 0:D], biaso, ALU.add).then_inc(S["own_free"], 1)

                def name(t, q, u):
                    if not below(t, 2):
                        dve.wait_ge(S["kv_out%d" % u], 16 * q)
                    dve.tensor_copy(sid[:, u:u + 1], tabw[:, bass.ds(t, 1), 2 * SLOTS:2 * SLOTS + 1].rearrange("p a n -> p (a n)")).then_inc(S["sid_ready"], 1)

                def residual(t, q, u):
                    st = Steps(dve, S["back"], t * BACK, paced)
                    y = rowo[u][:, 0:D]
                    name(t, q, u)
                    dve.wait_ge(S["summed"], t + 1)
                    if not below(t, 2):
                        dve.wait_ge(S["row_out%d" % u], 16 * q)
                    dve.scalar_tensor_tensor(out=y, in0=ps[:, 6 + u, 0:D], scalar=1.0 / H, in1=g_own[u][:, 0:D],
                                             op0=ALU.mult, op1=ALU.add).then_inc(S["y_done"], 1)
                    dve.wait_ge(S["y_done"], t + 1)
                    statistics(dve, st, y, S["var"])
                    assert st.count == 3

                def normalize(t, q, u):
                    st = Steps(dve, S["back"], t * BACK + 3, paced)
                    y = rowo[u][:, 0:D]
                    newton(dve, st, S["rstd"], t)
                    dve.tensor_scalar(y, y, l_MV[:, 0:1], l_R, ALU.subtract, ALU.mult).then_inc(S["x_ready"], 1)
                    assert st.count == BACK - 3

                def finish(t, q, u):
                    st = Steps(dve, S["back"], t * 2, paced)
                    name(t, q, u)
                    y = rowo[u][:, 0:D]
                    dve.wait_ge(S["proj"], t + 1)
                    dve.wait_ge(S["own_free"], t + 1)
                    st(dve.tensor_tensor(y, ps[:, 2, 0:D], xb[u], ALU.add))
                    st.wait()
                    st(dve.bn_stats(l_BN, y))
                    st.wait(alone=True)
                    dve.bn_aggr(rowo[u][:, D:D + 2], l_BN).then_inc(S["x_ready"], 1)

                def divide(t, q, u):
                    dve.reciprocal(s_inv, s_sum[:, u:u + 1]).then_inc(S["mem"], 1)
                    dve.wait_ge(S["mem"], t + 1)
                    dve.wait_ge(S["summed"], t + 1)
                    dve.tensor_scalar(attn, ps[:, 6 + u, 0:D], s_inv, None, ALU.mult).then_inc(S["attn"], 1)
                    dve.wait_ge(S["attn"], t + 1)
                    dve.sem_inc(S["y_done"], 1)

                def body(t, q, u, slots, g, others):
                    done = product(t, q, u, slots, g)
                    if one:
                        if not below(t, 1):
                            residual(*back(t, q, u, 1))
                        weigh(t, q, u, slots, done)
                        if not below(t, 1):
                            normalize(*back(t, q, u, 1))
                    else:
                        assert done == FRONT
                        if not below(t, 2):
                            finish(*back(t, q, u, 2))
                        if not below(t, 1):
                            divide(*back(t, q, u, 1))
                        weigh(t, q, u, slots, done)

                ranked_tiles(dve, body)
                last = (T - 1, T // 2 - 1, 1)
                if one:
                    residual(*last)
                    normalize(*last)
                else:
                    finish(*back(*last, 1))
                    divide(*last)
                    finish(*last)

            return sync, tensor, scalar, vector, gpsimd

        sparse = [sparse_layer(1), sparse_layer(2)]
        for n in range(2):
            ways = (sparse[n], dense[n])

            def either(eng, k):
                overflow = eng.value_load(flag[0:1, 0:1], min_val=0, max_val=1)
                with eng.If(overflow == 0):
                    ways[0][k](eng)
                with eng.Else():
                    ways[1][k](eng)

            with nc.Block() as block:
                @block.gpsimd
                def _(pool):
                    overflow = pool.value_load(flag[0:1, 0:1], min_val=0, max_val=1)
                    with pool.If(overflow == 0):
                        ways[0][4](pool)
                    with pool.Else():
                        if n == 0:
                            load_tail(pool, layer_sems[1]["tail_in"])
                            pool.wait_ge(layer_sems[1]["tail_in"], 64)

                @block.sync
                def _(sp):
                    either(sp, 0)

                @block.tensor
                def _(pe):
                    either(pe, 1)

                @block.scalar
                def _(act):
                    either(act, 2)

                @block.vector
                def _(dve):
                    either(dve, 3)
        PARTS = 3
        GROUP = 4
        BATCH = 8
        ys = carve(0, T * (D + 2)).rearrange("p (t n) -> p t n", n=D + 2)
        b3 = T * (D + 2)
        rstd = carve(b3, T)
        newt = carve(b3 + T, T)
        vr = carve(b3 + 2 * T, T)
        vp = carve(b3 + 3 * T, T * 4 // 2).bitcast(BF16).rearrange("p (t n) -> p t n", n=4)
        b3 += 3 * T + T * 2
        x3T = [carve(b3 + 256 * k, 256) for k in range(2)]
        X3B = 4
        x3b = [carve(b3 + 512 + 256 * k, 256) for k in range(X3B)]
        term = [carve(b3 + 512 + 256 * (X3B + k), 256) for k in range(2)]
        b3 += 1024 + 256 * X3B
        srow = carve(b3, N)
        b3 += N
        wsumb = carve(b3, 256)
        s_col = carve(b3 + 256, T)
        nmean = carve(b3 + 256 + T, T)
        mv3, w3, r3 = carve(b3 + 512, 2 * BATCH), carve(b3 + 544, BATCH), carve(b3 + 560, BATCH)
        rt3, nm3 = carve(b3 + 576, T), carve(b3 + 576 + T, T)
        onesf = carve(b3 + 576 + 2 * T, P)
        w3s = weights[:, 0:KD * D].rearrange("p (k n) -> p k n", k=KD)
        w3n = weights[:, KD * D:2 * KD * D].rearrange("p (k n) -> p k n", k=KD)
        BN3 = [stat[:, 0:6], stat[:, 6:12]]
        u3 = Sems("l3")

        def of_batch(ap, b):
            return ap[:, bass.ds(b * BATCH, BATCH)]

        with nc.Block() as block:
            @block.gpsimd
            def _(pool):
                pool.wait_ge(u3["y_in"], 64)
                load_tail(pool, u3["tail_in"])

            @block.sync
            def _(sp):
                src = yst.rearrange("(t p) n -> p t n", p=P)
                for k in range(4):
                    sp.dma_start(ys[:, 8 * k:8 * k + 8, :], src[:, 8 * k:8 * k + 8, :]).then_inc(u3["y_in"], 16)
                sp.dma_start(w3n, dram["WN3T"].rearrange("(k p) n -> p k n", p=P)).then_inc(u3["w_in"], 16)
                sp.dma_start(w3s, dram["WS3T"].rearrange("(k p) n -> p k n", p=P)).then_inc(u3["w_in"], 16)
                with sp.Fori(0, T // 2) as i:
                    sp.wait_ge(u3["out_ready"], i * 2 + 2)
                    dst = out[bass.ds(i * (2 * P), 2 * P), :].rearrange("(a p) n -> p a n", p=P)
                    sp.dma_start(dst, ys[:, bass.ds(i * 2, 2), 0:D]).then_inc(u3["out"], 16)
                sp.wait_ge(u3["out"], 16 * T // 2)

            @block.tensor
            def _(pe):
                pe.wait_ge(u3["w_in"], 32)
                pe.wait_ge(u3["wsum"], 1)
                for k in range(KD):
                    mm = pe.matmul(ps[:, 0, 0:D], onesf, w3n[:, k, :], start=(k == 0), stop=(k == KD - 1))
                mm.then_inc(u3["wsum_out"], 1)
                pe.wait_ge(u3["parts"], 1)
                pe.wait_ge(u3["wsum"], 2)

                def column(t):
                    if t % GROUP == 0:
                        pe.wait_ge(u3["s_out"], t // GROUP + 1)
                    return pe.matmul(ps[:, 0, t:t + 1], srow[0:PARTS, t * P:(t + 1) * P], onesf[0:PARTS, 0:1], start=True, stop=True)

                for g in range(T // GROUP):
                    if g == KEPT // GROUP:
                        pe.wait_ge(u3["tail_in"], 64)
                    for c in range(T):
                        if g >= 2 and c % (T // GROUP) == 0:
                            column((g - 2) * GROUP + c // (T // GROUP))
                        mask = adj8[:, g * GROUP:(g + 1) * GROUP, c, :]
                        mm = pe.matmul(ps[0:PARTS, g, :], vp[:, c, 0:PARTS], mask, start=(c == 0), stop=(c == T - 1))
                    mm.then_inc(u3["s_done"], 1)
                for t in range(T - 2 * GROUP, T):
                    mm = column(t)
                mm.then_inc(u3["s_col"], 1)

                def turn(t, v, b):
                    pe.wait_ge(u3["norm"], t + 1)
                    for k in range(KD):
                        mm = pe.transpose(ps[:, 2 + v, k * P:(k + 1) * P], x3b[b][:, k * P:(k + 1) * P], ident)
                    mm.then_inc(u3["turned"], 1)

                def project(t, v):
                    pe.wait_ge(u3["x3T"], t + 1)
                    if not (isinstance(t, int) and t < 2):
                        pe.wait_ge(u3["combined"], t - 1)
                    bank = ps[:, 4 + v, 0:D]
                    for k in range(KD):
                        mm = pe.matmul(bank, x3T[v][:, k * P:(k + 1) * P], w3s[:, k, :], start=(k == 0), stop=(k == KD - 1))
                    mm.then_inc(u3["proj"], 1)

                turn(0, 0, 0)
                for j in range(X3B):
                    turn(j + 1, (j + 1) % 2, (j + 1) % X3B)
                    project(j, j % 2)
                with pe.Fori(1, T // X3B - 1) as i:
                    for j in range(X3B):
                        turn(i * X3B + (j + 1), (j + 1) % 2, (j + 1) % X3B)
                        project(i * X3B + j, j % 2)
                for j in range(X3B):
                    if j < X3B - 1:
                        turn(T - X3B + j + 1, (j + 1) % 2, (j + 1) % X3B)
                    project(T - X3B + j, j % 2)

            @block.scalar
            def _(act):
                act.wait_ge(u3["step"], 2)
                act.activation(rstd, rstd, ACT.Sqrt).then_inc(u3["sq"], 1)
                act.wait_ge(u3["wsum_out"], 1)
                act.activation(wsumb, ps[:, 0, 0:D], ACT.Copy).then_inc(u3["wsum"], 1)
                act.wait_ge(u3["parts"], 2)

                def normalize(t, b):
                    y = ys[:, bass.ds(t, 1), 0:D].rearrange("p a n -> p (a n)")
                    if not (isinstance(t, int) and t < X3B):
                        act.wait_ge(u3["combined"], t - (X3B - 1))
                    act.activation(x3b[b], y, ACT.Identity, bias=nmean[:, bass.ds(t, 1)], scale=rstd[:, bass.ds(t, 1)]).then_inc(u3["norm"], 1)

                for t in range(X3B):
                    normalize(t, t)
                for g in range(T // GROUP):
                    act.wait_ge(u3["s_done"], g + 1)
                    act.activation(srow[0:PARTS, g * GROUP * P:(g + 1) * GROUP * P], ps[0:PARTS, g, :], ACT.Copy).then_inc(u3["s_out"], 1)
                act.wait_ge(u3["s_col"], 1)
                act.activation(s_col, ps[:, 0, 0:T], ACT.Copy).then_inc(u3["s_col"], 1)

                def scale(t):
                    y = ys[:, bass.ds(t, 1), 0:D].rearrange("p a n -> p (a n)")
                    act.activation(y, y, ACT.Identity, bias=nm3[:, bass.ds(t, 1)], scale=rt3[:, bass.ds(t, 1)]).then_inc(u3["out_ready"], 1)

                def body(t, j, v):
                    act.wait_ge(u3["turned"], t + 1)
                    act.activation(x3T[v], ps[:, 2 + v, 0:D], ACT.Copy).then_inc(u3["x3T"], 1)

                def root(b):
                    act.wait_ge(u3["var"], b + 1)
                    act.activation(r3, r3, ACT.Sqrt).then_inc(u3["root"], 1)

                def batch(b):
                    for j in range(BATCH):
                        t = b * BATCH + j
                        body(t, j, j % 2)
                        if not (isinstance(t, int) and (t < 2 or t - 2 + X3B >= T)):
                            normalize(t + (X3B - 2), (j - 2) % X3B)
                        if j == 1 and not (isinstance(b, int) and b == 0):
                            act.wait_ge(u3["scaled"], b)
                        if j >= 1 and not (isinstance(b, int) and b == 0):
                            scale((b - 1) * BATCH + j - 1)
                    if not (isinstance(b, int) and b == 0):
                        scale((b - 1) * BATCH + BATCH - 1)
                    root(b)

                batch(0)
                with act.Fori(1, T // BATCH - 1) as b:
                    batch(b)
                batch(T // BATCH - 1)
                act.wait_ge(u3["scaled"], T // BATCH)
                for j in range(BATCH):
                    scale(T - BATCH + j)

            @block.vector
            def _(dve):
                st = Steps(dve, u3["step"], 0, paced)
                dve.memset(onesf, 1.0).then_inc(u3["wsum"], 1)
                dve.wait_ge(u3["y_in"], 64)
                mean, var = ys[:, :, D:D + 1].rearrange("p t o -> p (t o)"), ys[:, :, D + 1:D + 2].rearrange("p t o -> p (t o)")
                st(dve.tensor_scalar(newt, var, EPS, None, ALU.add))
                st.wait()
                st(dve.reciprocal(rstd, newt))
                dve.wait_ge(u3["sq"], 1)
                st(dve.tensor_tensor(newt, newt, rstd, ALU.mult))
                st.wait()
                st(dve.tensor_tensor(newt, newt, rstd, ALU.mult))
                st.wait()
                st(dve.tensor_scalar(newt, newt, -0.5, 1.5, ALU.mult, ALU.add))
                st.wait()
                st(dve.tensor_tensor(rstd, rstd, newt, ALU.mult))
                st.wait()
                first = ys[:, :, 0:1].rearrange("p t o -> p (t o)")
                st(dve.tensor_tensor(vr, first, mean, ALU.subtract))
                st.wait()
                st(dve.tensor_tensor(vr, vr, rstd, ALU.mult))
                st.wait()
                for part in range(PARTS):
                    st(dve.tensor_copy(vp[:, :, part:part + 1].rearrange("p t o -> p (t o)"), vr))
                    st.wait()
                    if part < PARTS - 1:
                        st(dve.tensor_tensor(vr, vr, vp[:, :, part:part + 1].rearrange("p t o -> p (t o)"), ALU.subtract))
                        st.wait()
                dve.sem_inc(u3["parts"], 1)
                st(dve.scalar_tensor_tensor(out=nmean, in0=mean, scalar=-1.0, in1=rstd, op0=ALU.mult, op1=ALU.mult))
                st.wait()
                dve.sem_inc(u3["parts"], 1)
                dve.wait_ge(u3["wsum"], 2)
                dve.wait_ge(u3["s_col"], 2)

                def y_of(t):
                    return ys[:, bass.ds(t, 1), 0:D].rearrange("p a n -> p (a n)")

                def add_term(t, v):
                    dve.wait_ge(u3["proj"], t + 1)
                    dve.scalar_tensor_tensor(out=term[v], in0=wsumb, scalar=s_col[:, bass.ds(t, 1)], in1=ps[:, 4 + v, 0:D],
                                             op0=ALU.mult, op1=ALU.add).then_inc(u3["termed"], 1)

                def combine(t, b):
                    dve.wait_ge(u3["termed"], t + 1)
                    dve.wait_ge(u3["norm"], t + 1)
                    dve.scalar_tensor_tensor(out=y_of(t), in0=term[b % 2], scalar=0.0, in1=x3b[b], op0=ALU.max, op1=ALU.add).then_inc(u3["combined"], 1)

                def stats(t, v):
                    dve.wait_ge(u3["combined"], t + 1)
                    dve.sem_inc(paced, 1)
                    dve.bn_stats(BN3[v], y_of(t)).then_inc(u3["stats"], 1)

                def aggregate(t, j, v):
                    dve.wait_ge(u3["stats"], t + 1)
                    dve.sem_inc(paced, 1)
                    dve.bn_aggr(mv3[:, 2 * j:2 * j + 2], BN3[v]).then_inc(u3["norm_out"], 1)

                def batch(b):
                    for j in range(BATCH + 1):
                        t = b * BATCH + j
                        if j < BATCH:
                            add_term(t, j % 2)
                        if j:
                            stats(t - 1, (j - 1) % 2)
                        if j < BATCH:
                            combine(t, j % X3B)
                        if j:
                            aggregate(t - 1, j - 1, (j - 1) % 2)
                    st = Steps(dve, u3["batch"], b * 8, paced)
                    mv = mv3.rearrange("p (t n) -> p t n", n=2)
                    m, va = (mv[:, :, n:n + 1].rearrange("p t o -> p (t o)") for n in range(2))
                    r, w, rt, nm = r3, w3, of_batch(rt3, b), of_batch(nm3, b)
                    dve.wait_ge(u3["norm_out"], b * BATCH + BATCH)
                    st(dve.tensor_scalar(w, va, EPS, None, ALU.add))
                    st.wait()
                    dve.reciprocal(r, w).then_inc(u3["var"], 1)
                    dve.wait_ge(u3["root"], b + 1)
                    st(dve.tensor_tensor(w, w, r, ALU.mult))
                    st.wait()
                    st(dve.tensor_tensor(w, w, r, ALU.mult))
                    st.wait()
                    st(dve.tensor_scalar(w, w, -0.5, 1.5, ALU.mult, ALU.add))
                    st.wait()
                    st(dve.tensor_scalar(w, w, -1.0, None, ALU.mult))
                    st.wait()
                    st(dve.scalar_tensor_tensor(out=rt, in0=w, scalar=-1.0, in1=r, op0=ALU.mult, op1=ALU.mult))
                    st(dve.tensor_tensor(w, w, r, ALU.mult))
                    st.wait()
                    st(dve.tensor_tensor(nm, m, w, ALU.mult))
                    st.wait()
                    dve.sem_inc(u3["scaled"], 1)
                    assert st.count == 8, st.count

                with dve.Fori(0, T // BATCH) as b:
                    batch(b)


def constants():
    import numpy as np
    f = np.zeros((P, C_F32), np.float32)
    f[:, C_IDENT:C_IDENT + P] = np.eye(P)
    f[:, C_UPPER:C_UPPER + P] = np.triu(np.ones((P, P)), 1)
    j = np.arange(P)
    f[j, C_PACK + j // WORD] = 2.0 ** (j % WORD)
    f[:, C_PACK + WPC] = 1.0
    f[:, C_GROUP:C_GROUP + WORDS] = np.arange(WORDS) * 2.0 ** WORD
    f[:, C_CLASS:C_CLASS + SLOTS] = np.arange(SLOTS, 0, -1)
    f[:, C_LIMIT:C_LIMIT + SLOTS] = [P * sum(c >= k for c in CAPS) for k in range(SLOTS, 0, -1)]
    f[:, C_BIT:C_BIT + WORD] = np.arange(WORD) + 1
    i = np.zeros((P, C_I32), np.int32)
    i[:, C_POW:C_POW + WORD] = 1 << np.arange(WORD)
    i[:, C_OWN:C_OWN + T] = np.arange(T)[None, :] * P + j[:, None]
    return f, i


def layout(x, adj, L0_gnn_W_self, L0_gnn_b_self, L0_gnn_W_nb, L0_gnn_b_nb, L0_gnn_W_comb, L0_gnn_b_comb,
           L1_gnn_WQ, L1_gnn_WK, L1_gnn_WV, L1_gnn_we, L1_gnn_be,
           L2_gnn_Wq, L2_gnn_Wk, L2_gnn_Wv, L2_gnn_Wo, L2_gnn_bo, L3_gnn_w_self, L3_gnn_w_neigh):
    import numpy as np
    c = np.ascontiguousarray
    a = np.asarray
    f, i = constants()
    return {
        "x": c(a(x)),
        "adj_tiles": c(a(adj).reshape(T, P, T, P).transpose(0, 3, 2, 1)).reshape(T, P, T * P),
        "w_selfT0": c(a(L0_gnn_W_self).T), "w_nbT0": c(a(L0_gnn_W_nb).T), "W_comb": c(a(L0_gnn_W_comb)),
        "b_self": c(a(L0_gnn_b_self).reshape(KD, P).T), "b_nb": c(a(L0_gnn_b_nb).reshape(KD, P).T),
        "b_comb": c(a(L0_gnn_b_comb).reshape(1, D)),
        "WQ1T": c(a(L1_gnn_WQ).T), "WK1T": c(a(L1_gnn_WK).T), "WV1T": c(a(L1_gnn_WV).T),
        "we": c(a(L1_gnn_we)), "be": c(a(L1_gnn_be).reshape(1, 1)),
        "WQ2T": c(a(L2_gnn_Wq).T), "WK2T": c(a(L2_gnn_Wk).T), "WV2T": c(a(L2_gnn_Wv).T),
        "WO2T": c(a(L2_gnn_Wo).T), "bo2": c(a(L2_gnn_bo).reshape(1, D)),
        "WS3T": c(a(L3_gnn_w_self).T), "WN3T": c(a(L3_gnn_w_neigh).T),
        "const_f32": f, "const_i32": i,
    }


def kernel(**inputs):
    import concourse.bacc as bacc
    from concourse.bass_utils import run_bass_kernel_spmd

    arrays = {f"in_{k}": v for k, v in layout(**inputs).items()}
    nc = bacc.Bacc("TRN2", target_bir_lowering=False, num_devices=1)
    dram = {k[3:]: nc.dram_tensor(k, v.shape, mybir.dt.from_np(v.dtype), kind="ExternalInput").ap()
            for k, v in arrays.items()}
    out = nc.dram_tensor("out_x", (N, D), F32, kind="ExternalOutput").ap()
    build_program(nc, dram, out)
    return run_bass_kernel_spmd(nc, [arrays], core_ids=[0]).results[0]["out_x"]
```
